# Optimizing a Trainium2 kernel written in Bass

```python
import numpy as np
import jax
import jax.numpy as jnp

def _softmax(x, axis=-1):
    return jax.nn.softmax(x, axis=axis)

def _gelu(x):
    return jax.nn.gelu(x, approximate=True)

def _silu(x):
    return jax.nn.silu(x)

def _sigmoid(x):
    return jax.nn.sigmoid(x)

def _layernorm(x, axis=-1, eps=1e-05):
    m = jnp.mean(x, axis=axis, keepdims=True)
    v = jnp.var(x, axis=axis, keepdims=True)
    return (x - m) / jnp.sqrt(v + eps)

def _scatter_add(tgt, idx, src, axis=0):
    return tgt.at[idx].add(src)

def _segment_sum(src, seg, n):
    return jax.ops.segment_sum(src, seg, n)
kernel_name = 'mk_adaln_d1_jaxref_r8_20db4c'

def setup_inputs(seed: int=0):
    np.random.seed(seed)
    _w = jnp.asarray

    def _L0_attn_setup():
        import jax, jax.numpy as jnp
        import numpy as np
        LN_EPS = 1e-05
        ATTN_EPS = 1e-05

        def _ln(x, w, b):
            mu = x.mean(-1, keepdims=True)
            var = ((x - mu) ** 2).mean(-1, keepdims=True)
            return (x - mu) * jax.lax.rsqrt(var + LN_EPS) * w + b

        def _build_mask(heads, l):
            h2 = heads // 2
            slopes = 2.0 ** jnp.linspace(0.0, -8.0, h2)
            idx = jnp.arange(l)
            decay = -jnp.maximum(idx[:, None] - idx[None, :], 0).astype(jnp.float32)
            alibi = jnp.exp(slopes[:, None, None] * decay)
            return jnp.concatenate([alibi, jnp.ones((heads - h2, l, l), dtype=jnp.float32)], axis=0)
        key = jax.random.key(seed)
        ks = jax.random.split(key, 8)
        b, l, d_model = (2, 256, 128)
        heads, exp = (16, 2)
        d_exp = d_model * exp
        d_head = d_exp // heads
        depth = 12
        f32 = jnp.float32
        inp = {'x': jax.random.normal(ks[0], (b, l, d_model), dtype=f32), 'in_ln_w': jnp.ones((d_model,), f32), 'in_ln_b': jnp.zeros((d_model,), f32), 'q_ln_w': jnp.ones((d_model,), f32), 'q_ln_b': jnp.zeros((d_model,), f32), 'k_ln_w': jnp.ones((d_model,), f32), 'k_ln_b': jnp.zeros((d_model,), f32), 'out_ln_w': jnp.ones((d_model,), f32), 'out_ln_b': jnp.zeros((d_model,), f32), 'W_in': jax.random.normal(ks[1], (d_model, 2 * d_exp), f32) * 0.02, 'W_out': jax.random.normal(ks[2], (d_exp, d_model), f32) * (0.02 / np.sqrt(2 * depth)), 'Wq': jax.random.normal(ks[3], (d_model, d_exp), f32) * 0.02, 'bq': jax.random.normal(ks[4], (d_exp,), f32) * 0.02, 'Wk': jax.random.normal(ks[5], (d_model, d_exp), f32) * 0.02, 'bk': jax.random.normal(ks[6], (d_exp,), f32) * 0.02, 'smear_factor': jnp.linspace(-6.0, 6.0, heads).astype(f32), 'log_scale': jnp.full((heads,), 0.25 * np.log(d_head), f32)}
        return inp
    _L0_attn_in = _L0_attn_setup()

    def _L0_ffn_setup():
        import jax, jax.numpy as jnp
        import numpy as np
        TOP_K = 2
        key = jax.random.key(seed)
        ks = jax.random.split(key, 6)
        B, T, D, H, E = (4, 256, 128, 512, 8)
        s = 0.02
        return {'x': jax.random.normal(ks[0], (B, T, D), dtype=jnp.float32), 'Wg': jax.random.normal(ks[1], (E, D), dtype=jnp.float32) * s, 'W1': jax.random.normal(ks[2], (E, H, D), dtype=jnp.float32) * s, 'b1': jax.random.normal(ks[3], (E, H), dtype=jnp.float32) * s, 'W2': jax.random.normal(ks[4], (E, D, H), dtype=jnp.float32) * s, 'b2': jax.random.normal(ks[5], (E, D), dtype=jnp.float32) * s}
    _L0_ffn_in = _L0_ffn_setup()
    _L0_c = _w((lambda *s: np.random.randn(*s).astype(np.float32) * 0.05)(4, 128))
    _L0_wmod = _w((lambda *s: np.random.randn(*s).astype(np.float32) * 0.05)(128, 6 * 128) * 128 ** (-0.5))
    _d = {'L0_attn_x': _L0_attn_in['x'], 'L0_attn_in_ln_w': _L0_attn_in['in_ln_w'], 'L0_attn_in_ln_b': _L0_attn_in['in_ln_b'], 'L0_attn_q_ln_w': _L0_attn_in['q_ln_w'], 'L0_attn_q_ln_b': _L0_attn_in['q_ln_b'], 'L0_attn_k_ln_w': _L0_attn_in['k_ln_w'], 'L0_attn_k_ln_b': _L0_attn_in['k_ln_b'], 'L0_attn_out_ln_w': _L0_attn_in['out_ln_w'], 'L0_attn_out_ln_b': _L0_attn_in['out_ln_b'], 'L0_attn_W_in': _L0_attn_in['W_in'], 'L0_attn_W_out': _L0_attn_in['W_out'], 'L0_attn_Wq': _L0_attn_in['Wq'], 'L0_attn_bq': _L0_attn_in['bq'], 'L0_attn_Wk': _L0_attn_in['Wk'], 'L0_attn_bk': _L0_attn_in['bk'], 'L0_attn_smear_factor': _L0_attn_in['smear_factor'], 'L0_attn_log_scale': _L0_attn_in['log_scale'], 'L0_ffn_Wg': _L0_ffn_in['Wg'], 'L0_ffn_W1': _L0_ffn_in['W1'], 'L0_ffn_b1': _L0_ffn_in['b1'], 'L0_ffn_W2': _L0_ffn_in['W2'], 'L0_ffn_b2': _L0_ffn_in['b2'], 'L0_c': _L0_c, 'L0_wmod': _L0_wmod}
    _x0 = _d['L0_attn_x']
    _d['L0_attn_x'] = jax.random.normal(jax.random.fold_in(jax.random.key(seed), 1), (4, 1024, 128), dtype=_x0.dtype)
    del _x0
    return _d

def reference(L0_attn_x, L0_attn_in_ln_w, L0_attn_in_ln_b, L0_attn_q_ln_w, L0_attn_q_ln_b, L0_attn_k_ln_w, L0_attn_k_ln_b, L0_attn_out_ln_w, L0_attn_out_ln_b, L0_attn_W_in, L0_attn_W_out, L0_attn_Wq, L0_attn_bq, L0_attn_Wk, L0_attn_bk, L0_attn_smear_factor, L0_attn_log_scale, L0_ffn_Wg, L0_ffn_W1, L0_ffn_b1, L0_ffn_W2, L0_ffn_b2, L0_c, L0_wmod):

    def _L0_attn_ref(x, in_ln_w, in_ln_b, q_ln_w, q_ln_b, k_ln_w, k_ln_b, out_ln_w, out_ln_b, W_in, W_out, Wq, bq, Wk, bk, smear_factor, log_scale):
        import jax, jax.numpy as jnp
        import numpy as np
        LN_EPS = 1e-05
        ATTN_EPS = 1e-05

        def _ln(x, w, b):
            mu = x.mean(-1, keepdims=True)
            var = ((x - mu) ** 2).mean(-1, keepdims=True)
            return (x - mu) * jax.lax.rsqrt(var + LN_EPS) * w + b

        def _build_mask(heads, l):
            h2 = heads // 2
            slopes = 2.0 ** jnp.linspace(0.0, -8.0, h2)
            idx = jnp.arange(l)
            decay = -jnp.maximum(idx[:, None] - idx[None, :], 0).astype(jnp.float32)
            alibi = jnp.exp(slopes[:, None, None] * decay)
            return jnp.concatenate([alibi, jnp.ones((heads - h2, l, l), dtype=jnp.float32)], axis=0)
        b, l, d_model = x.shape
        heads = smear_factor.shape[0]
        d_exp = W_in.shape[1] // 2
        d_head = d_exp // heads
        vp = _ln(x, in_ln_w, in_ln_b) @ W_in
        v, p = jnp.split(vp, 2, axis=-1)
        q = _ln(x, q_ln_w, q_ln_b) @ Wq + bq
        k = _ln(x, k_ln_w, k_ln_b) @ Wk + bk

        def to_heads(t):
            return t.reshape(b, l, heads, d_head).transpose(0, 2, 1, 3)
        q, k, v = (to_heads(q), to_heads(k), to_heads(v))
        q = jax.nn.softmax(q, axis=-1)
        k = jax.nn.softmax(k, axis=-1)
        smear = jax.nn.sigmoid(smear_factor)[None, :, None, None]
        k_prev = jnp.pad(k, ((0, 0), (0, 0), (1, 0), (0, 0)))[:, :, :l, :]
        k = (1.0 - smear) * k + smear * k_prev
        s = jnp.exp(log_scale)[None, :, None, None]
        q = q / s
        k = k / s
        mask = _build_mask(heads, l)
        attn = jnp.tril(jnp.einsum('bhid,bhjd->bhij', q, k) * mask)
        norm = 1.0 / (attn.sum(axis=-1) + ATTN_EPS)
        o = jnp.einsum('bhij,bhjd->bhid', attn * norm[..., None], v)
        o = o.transpose(0, 2, 1, 3).reshape(b, l, d_exp)
        out = _ln(jax.nn.silu(p) * o @ W_out, out_ln_w, out_ln_b)
        return out

    def _L0_ffn_ref(x, Wg, W1, b1, W2, b2):
        import jax, jax.numpy as jnp
        import numpy as np
        TOP_K = 2
        B, T, D = x.shape
        N = B * T
        xf = x.reshape(N, D)
        logits = jnp.einsum('nd,ed->ne', xf, Wg)
        top_logits, top_idx = jax.lax.top_k(logits, TOP_K)
        top_w = jax.nn.softmax(top_logits, axis=-1)
        h = jax.nn.gelu(jnp.einsum('nd,ehd->neh', xf, W1) + b1[None], approximate=False)
        all_out = jnp.einsum('neh,edh->ned', h, W2) + b2[None]
        selected = jnp.take_along_axis(all_out, top_idx[:, :, None], axis=1)
        out = jnp.sum(selected * top_w[:, :, None], axis=1)
        return out.reshape(B, T, D)
    x = L0_attn_x
    mod = (_silu(L0_c) @ L0_wmod).reshape(L0_c.shape[0], 6, 1, -1)
    sa, ca, ga, sb, cb, gb = (mod[:, 0], mod[:, 1], mod[:, 2], mod[:, 3], mod[:, 4], mod[:, 5])
    ga = (2 * (ga >= 0) - 1) * jnp.maximum(jnp.abs(ga), 0.25)
    gb = (2 * (gb >= 0) - 1) * jnp.maximum(jnp.abs(gb), 0.25)
    h = _layernorm(x, axis=-1) * (1 + ca) + sa
    x = x + ga * _L0_attn_ref(h, L0_attn_in_ln_w, L0_attn_in_ln_b, L0_attn_q_ln_w, L0_attn_q_ln_b, L0_attn_k_ln_w, L0_attn_k_ln_b, L0_attn_out_ln_w, L0_attn_out_ln_b, L0_attn_W_in, L0_attn_W_out, L0_attn_Wq, L0_attn_bq, L0_attn_Wk, L0_attn_bk, L0_attn_smear_factor, L0_attn_log_scale)
    h = _layernorm(x, axis=-1) * (1 + cb) + sb
    x = x + gb * _L0_ffn_ref(h, L0_ffn_Wg, L0_ffn_W1, L0_ffn_b1, L0_ffn_W2, L0_ffn_b2)
    return x

_drawn_inputs = setup_inputs


def setup_inputs(seed=0):
    import zlib

    import numpy as np

    out = dict(_drawn_inputs(seed))
    spreads = {'L0_attn_in_ln_w': (1.0, 0.6),
     'L0_attn_in_ln_b': (0.0, 0.516),
     'L0_attn_q_ln_w': (1.0, 0.6),
     'L0_attn_q_ln_b': (0.0, 0.8),
     'L0_attn_k_ln_w': (1.0, 0.6),
     'L0_attn_k_ln_b': (0.0, 0.8),
     'L0_attn_out_ln_w': (1.0, 0.6),
     'L0_attn_out_ln_b': (0.0, 0.305),
     'L0_attn_log_scale': (0.6931471824645996, 0.6)}
    factors = {'L0_attn_Wq': 8.0,
     'L0_attn_bq': 23.879,
     'L0_attn_Wk': 8.0,
     'L0_attn_bk': 8.0,
     'L0_attn_smear_factor': 8.0,
     'L0_ffn_Wg': 6.365,
     'L0_ffn_W1': 6.057,
     'L0_ffn_b1': 8.0,
     'L0_ffn_W2': 5.955,
     'L0_ffn_b2': 8.0}
    for name, (base, spread) in spreads.items():
        noise = np.random.default_rng([zlib.crc32(name.encode()), seed]).standard_normal(out[name].shape)
        drawn = base * np.exp(spread * noise) if base else spread * noise
        out[name] = jnp.asarray(drawn.astype(out[name].dtype))
    for name, factor in factors.items():
        out[name] = (out[name] * factor).astype(out[name].dtype)
    return out
```

```python
from contextlib import ExitStack

import numpy as np

import concourse.bass as bass
from concourse import mybir

F32 = mybir.dt.float32
BF16 = mybir.dt.bfloat16
I32 = mybir.dt.int32
U32 = mybir.dt.uint32
ALU = mybir.AluOpType
ACT = mybir.ActivationFunctionType
AX = mybir.AxisListType

B, L, D = 4, 1024, 128
P = 128
NC = L // P
NT = B * NC
DE = 256
H = 16
DH = DE // H
HD = H // 2
E, HID = 8, 512
VW = DH + 1
HV = 8 * VW
EPS = 1e-5

REGION = B * L + P
XROWS = E * REGION + P
XW = D + 2
FT = 2 * B * L // P + E
RING = 4

C_ID = 0
C_MASK = C_ID + P
C_PM = C_MASK + H * P
C_WQ = C_PM + 2
C_BM = C_WQ + 2 * P
C_LAM = C_BM + 2 * HV
C_WK = C_LAM + 2
C_TRI = C_WK + H
C_ONE = C_TRI + P
C_IOTA = C_ONE + P
C_REG = C_IOTA + E
C_TAU = C_REG + E
C_ROW = C_TAU + FT
C_PAD = C_ROW + 2 * B
C_N = C_PAD + 1


def slot(h):
    return 4 * (h % 8 // 2) + 2 * (h // 8) + h % 2


def shape_constants():
    slope = (2.0 ** np.linspace(0.0, -8.0, HD)).astype(np.float32).astype(np.float64)
    rate = np.concatenate([slope, np.zeros(H - HD)])
    t = np.arange(P)
    k = np.zeros((P, C_N), np.float64)
    k[:, C_ID:C_ID + P] = np.eye(P)
    ahead = t[None, :] - t[:, None]
    for h in range(H):
        s, at = rate[h], C_MASK + slot(h) * P
        k[:, at:at + P] = np.where(ahead >= 0, np.exp(-s * np.maximum(ahead, 0)), 0.0)
    for par in range(2):
        k[:, C_PM + par] = (t // DH) % 2 == par
    for half in range(2):
        r = rate[8 * half + t // DH]
        k[:, C_WQ + half * P:C_WQ + (half + 1) * P] = np.exp(-r[:, None] * (t[None, :] + 1))
        own = (t // DH)[:, None] == np.arange(8)[None, :].repeat(VW, 1)
        k[:, C_BM + half * HV:C_BM + (half + 1) * HV] = own
        k[:, C_LAM + half] = np.exp(-r * P)
    k[:, C_TRI:C_TRI + P] = t[:, None] < t[None, :]
    k[:, C_ONE:C_ONE + P] = 1.0
    k[:, C_IOTA:C_IOTA + E] = np.arange(E)
    k[:, C_REG:C_REG + E] = np.arange(E) * REGION
    k[:, C_TAU:C_TAU + FT] = np.arange(FT)
    for b in range(B):
        for choice in range(2):
            k[:, C_ROW + 2 * b + choice] = choice * B * L + b * P + t
    k[:, C_PAD] = 2 * B * L + t
    k[:, C_WK:C_WK + H] = np.exp(-rate[None, :] * (P - 1 - t)[:, None])
    return k.astype(np.float32)


def until(eng, sem, value):
    if isinstance(value, int) and value <= 0:
        return
    eng.wait_ge(sem, value)


def build(nc, x, in_w, in_b, q_w, q_b, k_w, k_b, out_w, out_b, W_in, W_out, Wq, bq, Wk, bk,
          smear, log_scale, Wg, W1, b1, W2, b2, cond, wmod, consts, out):
    ctx = ExitStack()
    with ctx:
        def sb(name, shape, dt=F32):
            return ctx.enter_context(nc.sbuf_tensor(name, shape, dt))

        def psum(name):
            return ctx.enter_context(nc.psum_tensor(name, [P, 512], F32))

        def sem(name):
            return ctx.enter_context(nc.semaphore(name))

        x_all = sb("x_all", [P, NT, D])
        zT_all = sb("zT_all", [P, NT * P])
        y_all = sb("y_all", [P, NT, D])
        cst = sb("cst", [P, C_N])
        ident = cst[:, C_ID:C_ID + P]
        mod = sb("mod", [P, B, 6 * D])
        gaw = sb("gaw", [P, B, D])
        gab = sb("gab", [P, B, D])
        wcat = sb("wcat", [P, 4 * DE])
        wraw = sb("wraw", [P, 4 * DE])
        bias = sb("bias", [P, 4 * DE])
        wo_sb = sb("wo_sb", [P, 2, D])
        cols = sb("cols", [P, 6])
        bcol = sb("bcol", [P, 3, P])
        bqk = sb("bqk", [P, 2 * DE])
        ow_bc = sb("ow_bc", [P, 2, D])
        hv = sb("hv", [P, 2, H])
        sig = sb("sig", [P, 2, H])
        hexp = sb("hexp", [P, H])
        deps = sb("deps", [P, H])
        cT = sb("cT", [P, B])
        cE = sb("cE", [P, B])
        cR = sb("cR", [P, B])
        cS = sb("cS", [P, B])
        cB = sb("cB", [P, B, P])
        wmod_sb = sb("wmod_sb", [P, 6 * D])
        half = sb("half", [P, B])

        st = sb("st", [P, B, 6])
        mv = sb("mv", [P, B, 2])
        seen = sb("seen", [P, 1])
        seen_p = sb("seen_p", [P, 2])
        ve = sb("ve", [P, B])
        rstd = sb("rstd", [P, B])
        ya = sb("ya", [P, B, D])
        yb = sb("yb", [P, B, D])
        sq = sb("sq", [P, B, D])
        zt = sb("zt", [P, B, D])

        zs = sb("zs", [P, B * P])
        qk = sb("qk", [P, 2 * DE])
        mx = sb("mx", [P, 2 * H])
        ex = sb("ex", [P, 2 * DE])
        sm = sb("sm", [P, 2 * H])
        rs = sb("rs", [P, 2 * H])
        rk = sb("rk", [P, 2, H])
        qh = sb("qh", [P, DE])
        k2 = sb("k2", [P, DE])
        kf = sb("kf", [P, DE])
        kp = sb("kp", [P, B, DE])
        kw = sb("kw", [P, DE])
        vs = sb("vs", [P, 2, H, VW])
        ps_ = sb("ps_", [P, B, DE])
        ep = sb("ep", [P, B, DE])
        qeo = sb("qeo", [P, 2, 2, P])
        qw = sb("qw", [P, 2, P])
        kT = sb("kT", [P, 2, P])
        Pm = sb("Pm", [P, H, P])
        state = sb("state", [P, B, H, 32])
        own_kv = sb("own_kv", [P, H, VW])
        oT = sb("oT", [P, 4, P])
        den = sb("den", [P, H])
        tt = sb("tt", [P, DE])
        tr = sb("tr", [P, DE])
        av = sb("av", [P, DE])
        gg = sb("gg", [P, DE])
        gT = sb("gT", [P, 2, P])

        w1n = sb("w1n", [P, E, 4, D])
        w2n = sb("w2n", [P, E, HID])
        w1T = w1n[:, :, :, :].rearrange("p e h d -> p (e h d)")
        w2T = w2n[:, :, :].rearrange("p e h -> p (e h)")
        b1_bc = zT_all
        b2_bc = sb("b2_bc", [P, E * D])
        wgn = sb("wgn", [E, D])
        wgT = sb("wgT", [P, E])
        tri = sb("tri", [P, P], BF16)
        one = sb("one", [P, P], BF16)
        lg = sb("lg", [P, B, E])
        m8 = sb("m8", [P, B, 8])
        i8 = sb("i8", [P, B, 8], U32)
        i8f = sb("i8f", [P, B, 2])
        pick = sb("pick", [P, 2, B, E])
        used = sb("used", [P, B * E], BF16)
        gap = sb("gap", [P, B])
        e2 = sb("e2", [P, B])
        e3 = sb("e3", [P, B])
        count = sb("count", [P, E])
        posb = sb("posb", [P, B, E])
        posr = sb("posr", [P, B, E])
        prod = sb("prod", [P, 2, B, E])
        dest = sb("dest", [P, 2, B])
        desti = sb("desti", [P, 2, B], I32)
        ids = sb("ids", [P, B, 2])
        rows = sb("rows", [P, B, 2, XW])
        pad = sb("pad", [P, XW])
        cnt1 = sb("cnt1", [P, E])
        cnti = sb("cnti", [P, E], I32)
        nts = sb("nts", [P, E])
        cum = sb("cum", [P, 3, E])
        room = Pm[:, :, :].rearrange("p h i -> p (h i)")
        ge = room[0:1, 0:FT * E].rearrange("p (t e) -> p t e", e=E)
        gn = room[0:1, FT * E:2 * FT * E].rearrange("p (t e) -> p t e", e=E)
        hh = room[:, 0:2 * HID].rearrange("p (u h) -> p u h", u=2)
        hT = room[:, 2 * HID:4 * HID].rearrange("p (u h t) -> p u h t", u=2, h=4)
        meta = sb("meta", [1, 5, FT])
        meta_i = sb("meta_i", [1, 2, FT], I32)
        pad_f = sb("pad_f", [1, E])
        pad_i = sb("pad_i", [1, E + 1], I32)
        xt = sb("xt", [P, RING, XW])
        xT, yt, ys = (wmod_sb[:, i * 2 * P:(i + 1) * 2 * P].rearrange("p (u d) -> p u d", u=2) for i in range(3))
        X = nc.dram_tensor("expert_in", (XROWS, XW), F32).ap()
        Y = nc.dram_tensor("expert_out", (2 * NT * P, D), F32).ap()

        PA, PV, TD, TA, S0, S1, O, M = (psum(n) for n in ("PA", "PV", "TD", "TA", "S0", "S1", "O", "M"))
        S = (S0, S1)

        names = ("w x_in cs sigE sigA sigR sigB ce cr cb mp mc kpz fold bp bc1 half_ok g1 "
                 "a_st a_mv a_ve a_rs a_y a_y1 a_y2 a_st2 a_mv2 a_ve2 a_rs2 a_z a_zT a_za "
                 "zs pqk pvp qk mx vv vp d e ee sum r rk qh k2 ka kb k1 kf kw tq tk qt qw kt sc pm o u s1 st "
                 "oc g dn tt tr av gg tg gt y yc "
                 "b_st b_mv b_ve b_rs b_t b_t1 b_t2 b_x2 b_out "
                 "ww wb wt we wg wgt init c_st c_mv c_ve c_rs c_n c_m c_h c_r c_hT c_hs c_lg c_l c_m8 c_i8 c_if c_pk "
                 "c_us c_gap c_e2 c_w1 c_w2 c_w3 c_ps c_pb c_cnt c_pr c_pd c_d c_di c_id c_idn c_sc "
                 "tile meta padf padd x_ld "
                 "c_seen f_seen f_xt0 f_xt1 f_xt2 f_xt3 f_sc0 f_sc1 f_sc2 f_sc3 f_xp f_xT f_m1 f_hb f_h f_th f_hT f_m2 f_yb f_y o_ld0 o_ld1 o_s o_g o_x")
        s = {n: sem("s_" + n) for n in names.split()}

        block = ctx.enter_context(nc.Block())

        def bcast(ap, n):
            return ap.unsqueeze(2).to_broadcast([ap.shape[0], ap.shape[1], n])

        def expert_of(eng, t):
            at = meta_i[0:1, 1, t:t + 1] if isinstance(t, int) else meta_i[0:1, 1, bass.ds(t, 1)]
            return eng.value_load(at, min_val=0, max_val=E - 1)

        heads = lambda ap: ap.rearrange("p (h f) -> p h f", f=DH)

        @block.sync
        def _(sp):
            for c in range(NC):
                sp.dma_start(x_all[:, 4 * c:4 * c + 4, :],
                             x[:, c * P:(c + 1) * P, :].rearrange("b p d -> p b d")).then_inc(s["x_in"], 16)
            for e in range(E):
                sp.dma_start(w1n[:, e, :, :], W1[e].rearrange("(h p) d -> p h d", p=P)).then_inc(s["ww"], 16)
                sp.dma_start(w2n[:, e, :], W2[e]).then_inc(s["ww"], 16)
            sp.dma_start(wgn[:, :], Wg).then_inc(s["wg"], 16)
            sp.dma_start(b2_bc[:, :], b2.rearrange("e d -> (e d)").partition_broadcast(P)).then_inc(s["wb"], 16)
            def shift(c, b):
                n = c * 4 + b
                done = n + 1
                until(sp, s["k2"], done)
                sp.dma_start(kp[1:113, b, :], k2[0:112, :]).then_inc(s["ka"], 16)
                sp.dma_start(kp[113:128, b, :], k2[112:127, :]).then_inc(s["ka"], 16)
                until(sp, s["kf"], done)
                sp.dma_start(kp[0:1, b, :], k2[127:128, :]).then_inc(s["kb"], 16)

            for b in range(B):
                shift(0, b)
            with sp.Fori(1, NC) as c:
                for b in range(B):
                    shift(c, b)
            sp.wait_ge(s["meta"], 2)
            sp.wait_ge(s["init"], 3)
            for e in range(E + 1):
                r = sp.value_load(pad_i[0:1, e:e + 1], min_val=0, max_val=XROWS - P)
                sp.dma_start(X[bass.ds(r, P), :], pad[:, :]).then_inc(s["padd"], 16)
            sp.wait_ge(s["padd"], 16 * (E + 1))
            sp.wait_ge(s["c_sc"], 16 * 2 * NT)

            def fetch(t, u, turn):
                r = sp.value_load(meta_i[0:1, 0, bass.ds(t, 1)] if not isinstance(t, int) else meta_i[0:1, 0, t:t + 1],
                                  min_val=0, max_val=XROWS - P)
                until(sp, s[f"f_sc{u}"], 16 * turn)
                sp.dma_start(xt[:, u, :], X[bass.ds(r, P), :]).then_inc(s[f"f_xt{u}"], 16)

            for u in range(RING):
                fetch(u, u, 0)
            with sp.Fori(1, FT // RING) as k:
                for u in range(RING):
                    fetch(k * RING + u, u, k)

            for u in range(RING):
                sp.wait_ge(s[f"f_sc{u}"], 16 * FT // RING)
            for c in range(NC):
                if c >= 2:
                    sp.wait_ge(s["o_s"], c - 1)
                for choice in range(2):
                    r0 = choice * NT * P + c * B * P
                    sp.dma_start(y_all[:, 8 * (c % 2) + 4 * choice:8 * (c % 2) + 4 * choice + 4, :],
                                 Y[r0:r0 + B * P, :].rearrange("(b p) d -> p b d", p=P)).then_inc(s[f"o_ld{c % 2}"], 16)
            for c in range(NC):
                sp.wait_ge(s["o_x"], c + 1)
                sp.dma_start(out[:, c * P:(c + 1) * P, :].rearrange("b p d -> p b d"),
                             x_all[:, 4 * c:4 * c + 4, :]).then_inc(s["b_out"], 16)
            sp.wait_ge(s["b_out"], 16 * NC)

        @block.scalar
        def _(act):
            act.dma_start(cst[:, :], consts).then_inc(s["w"], 16)
            act.dma_start(wmod_sb[:, :], wmod).then_inc(s["w"], 16)
            act.dma_start(cT[:, :], cond.rearrange("b k -> k b"), allow_slow_non_contiguous=True).then_inc(s["w"], 16)
            for i, v in enumerate((q_w, q_b, k_w, k_b, in_w, in_b)):
                act.dma_start(cols[:, i:i + 1], v.unsqueeze(1), allow_slow_non_contiguous=True).then_inc(s["w"], 16)
            act.dma_start(wraw[:, 0:DE], Wq).then_inc(s["w"], 16)
            act.dma_start(wraw[:, DE:2 * DE], Wk).then_inc(s["w"], 16)
            act.dma_start(wraw[:, 2 * DE:], W_in).then_inc(s["w"], 16)
            act.dma_start(wo_sb[:, :, :], W_out.rearrange("(h k) d -> k h d", h=2)).then_inc(s["w"], 16)
            for i, v in enumerate((bq, bk)):
                act.dma_start(bqk[:, i * DE:(i + 1) * DE], v.partition_broadcast(P)).then_inc(s["w"], 16)
            for i, v in enumerate((out_w, out_b)):
                act.dma_start(ow_bc[:, i, :], v.partition_broadcast(P)).then_inc(s["w"], 16)
            for i, v in enumerate((smear, log_scale)):
                act.dma_start(hv[:, i, :], v.partition_broadcast(P)).then_inc(s["w"], 16)
            act.wait_ge(s["w"], 16 * NW)
            act.activation(cE[:, :], cT[:, :], ACT.Exp, scale=-1.0).then_inc(s["ce"], 1)
            act.activation(hexp[:, :], hv[:, 0, :], ACT.Exp, scale=-1.0).then_inc(s["sigE"], 1)
            act.activation(deps[:, :], hv[:, 1, :], ACT.Exp, scale=2.0).then_inc(s["sigA"], 1)
            with act.Fori(0, NC) as c:
                act.wait_ge(s["a_zT"], c + 1)
                act.copy(zT_all[:, bass.ds(c * 512, 512)], TA[:, :]).then_inc(s["a_za"], 1)

            def stage_z(c):
                until(act, s["pvp"], c * 4)
                act.copy(zs[:, :], zT_all[:, bass.ds(c * 512, 512)]).then_inc(s["zs"], 1)

            def front(n, b):
                until(act, s["d"], n + 1)
                until(act, s["kf"], n)
                until(act, s["k2"], n)
                act.activation(ex[:, :], qk[:, :], ACT.Exp).then_inc(s["e"], 1)
                until(act, s["vp"], n + 1)
                until(act, s["tt"], n - 3)
                act.activation(ep[:, b, :], ps_[:, b, :], ACT.Exp, scale=-1.0).then_inc(s["ee"], 1)

            def step(c, b, first=False, last=False):
                n = c * 4 + b
                nxt = (b + 1) % B
                until(act, s["tk"], n + 1)
                until(act, s["o"], n)
                act.copy(kT[:, :, :], TA[:, 0:2 * P]).then_inc(s["kt"], 1)
                if b == 3 and not last:
                    stage_z(c + 1)
                if not last:
                    front(n + 1, nxt)
                if not first:
                    until(act, s["tg"], n)
                    until(act, s["y"], n - 1)
                    act.copy(gT[:, :, :], TA[:, 0:2 * P]).then_inc(s["gt"], 1)
                    until(act, s["y"], n)
                    act.copy(y_all[:, bass.ds(n - 1, 1), :], TA[:, 256:256 + D]).then_inc(s["yc"], 1)
                until(act, s["o"], n + 1)
                until(act, s["g"], n)
                act.copy(oT[:, :, :], O[:, :]).then_inc(s["oc"], 1)
                if isinstance(c, int):
                    e = b if c == 0 else 4 + b
                    for i, dst in enumerate((w1T, w2T)):
                        act.wait_ge(s["wt"], 2 * e + i + 1)
                        act.copy(dst[:, e * HID:(e + 1) * HID], O[:, :]).then_inc(s["we"], 1)

            act.wait_ge(s["a_za"], NC)
            stage_z(0)
            front(0, 0)
            for b in range(B):
                step(0, b, first=b == 0)
            with act.Fori(1, NC - 1) as c:
                for b in range(B):
                    step(c, b)
            for b in range(B):
                step(NC - 1, b, last=b == 3)
            n = NT
            act.wait_ge(s["tg"], n)
            act.wait_ge(s["y"], n - 1)
            act.copy(gT[:, :, :], TA[:, 0:2 * P]).then_inc(s["gt"], 1)
            act.wait_ge(s["y"], n)
            act.copy(y_all[:, n - 1, :], TA[:, 256:256 + D]).then_inc(s["yc"], 1)
            act.wait_ge(s["zs"], NC)
            act.dma_start(b1_bc[:, :], b1.rearrange("e h -> (e h)").partition_broadcast(P)).then_inc(s["wb"], 16)
            act.wait_ge(s["wgt"], 1)
            act.copy(wgT[:, :], TD[:, 0:E]).then_inc(s["wgt"], 1)
            act.wait_ge(s["pvp"], NT)
            with act.Fori(0, NC) as c:
                until(act, s["c_hT"], c + 1)
                act.copy(zs[:, :], TA[:, :]).then_inc(s["c_hs"], 1)
                until(act, s["c_gap"], c + 1)
                act.activation(e2[:, :], gap[:, :], ACT.Exp).then_inc(s["c_e2"], 1)
                until(act, s["c_h"], c + 1)
                until(act, s["c_sc"], c * 8 * 16)
                for choice in range(2):
                    act.copy(rows[:, :, choice, 0:D], zt[:, :, :]).then_inc(s["c_r"], 1)

            def xT_copy(t, u):
                until(act, s["f_xp"], t + 1)
                until(act, s["f_m1"], t - 1)
                act.copy(xT[:, u % 2, :], (TA, TD)[u % 2][:, 0:P]).then_inc(s["f_xT"], 1)

            def gelu(t, u):
                until(act, s["f_hb"], t + 1)
                act.activation(hh[:, u % 2, :], hh[:, u % 2, :], ACT.Gelu).then_inc(s["f_h"], 1)

            def expert(t, u, ahead):
                if ahead > 3:
                    xT_copy(t + 3, (u + 3) % RING)
                if ahead > 1:
                    gelu(t + 1, (u + 1) % RING)

            for t in range(3):
                xT_copy(t, t)
            gelu(0, 0)
            with act.Fori(0, FT // RING - 1) as k:
                for u in range(RING):
                    expert(k * RING + u, u, RING)
            for u in range(RING):
                expert(FT - RING + u, u, RING - u)

        @block.gpsimd
        def _(pool):
            pool.memset(half[:, :], -0.5).then_inc(s["half_ok"], 1)
            pool.memset(kp[0:1, :, :], 0.0).then_inc(s["kpz"], 1)
            pool.wait_ge(s["half_ok"], 1)
            with pool.Fori(0, NC) as c:
                for v_ready, r_ready in (("a_ve", "a_rs"), ("a_ve2", "a_rs2")):
                    pool.wait_ge(s[v_ready], c + 1)
                    pool.tensor_tensor(rstd[:, :], ve[:, :], half[:, :], ALU.pow).then_inc(s[r_ready], 1)

            def front1(n):
                until(pool, s["mx"], n + 1)
                pool.tensor_tensor(heads(qk[:, :]), heads(qk[:, :]), bcast(mx[:, :], DH),
                                   ALU.subtract).then_inc(s["d"], 1)

            def front2(n):
                until(pool, s["rk"], n + 1)
                until(pool, s["tq"], n)
                pool.tensor_tensor(heads(qh[:, :]), heads(ex[:, 0:DE]), bcast(rs[:, 0:H], DH),
                                   ALU.mult).then_inc(s["qh"], 1)
                until(pool, s["kb"], n * 16)
                pool.tensor_tensor(heads(k2[:, :]), heads(ex[:, DE:]), bcast(rk[:, 1, :], DH),
                                   ALU.mult).then_inc(s["k2"], 1)

            def step(c, b, first=False, last=False):
                n = c * 4 + b
                until(pool, s["kf"], n + 1)
                until(pool, s["u"], n)
                pool.tensor_tensor(heads(kw[:, :]), heads(kf[:, :]), bcast(cst[:, C_WK:C_WK + H], DH),
                                   ALU.mult).then_inc(s["kw"], 1)
                if not first:
                    until(pool, s["av"], n)
                    until(pool, s["tr"], n)
                    until(pool, s["tg"], n - 1)
                    pool.tensor_tensor(gg[:, :], av[:, :], tr[:, :], ALU.mult).then_inc(s["gg"], 1)
                if not last:
                    front1(n + 1)
                    front2(n + 1)

            front1(0)
            front2(0)
            for b in range(B):
                step(0, b, first=b == 0)
            with pool.Fori(1, NC - 1) as c:
                for b in range(B):
                    step(c, b)
            for b in range(B):
                step(NC - 1, b, last=b == 3)
            pool.wait_ge(s["av"], NT)
            pool.wait_ge(s["tr"], NT)
            pool.wait_ge(s["tg"], NT - 1)
            pool.tensor_tensor(gg[:, :], av[:, :], tr[:, :], ALU.mult).then_inc(s["gg"], 1)
            with pool.Fori(0, NC) as c:
                for v_ready, r_ready in (("b_ve", "b_rs"), ("c_ve", "c_rs")):
                    pool.wait_ge(s[v_ready], c + 1)
                    pool.tensor_tensor(rstd[:, :], ve[:, :], half[:, :], ALU.pow).then_inc(s[r_ready], 1)
                pool.wait_ge(s["c_di"], c + 1)
                pool.tensor_tensor(seen_p[:, 0:1], half[:, 0:1], half[:, 0:1], ALU.mult).then_inc(s["c_seen"], 1)
                for b in range(B):
                    for choice in range(2):
                        pool.indirect_dma_start(
                            X, bass.IndirectOffsetOnAxis(ap=desti[:, choice, b:b + 1], axis=0),
                            rows[:, b, choice, :], None).then_inc(s["c_sc"], 16)

            def scatter(t, u):
                until(pool, s["f_y"], t + 1)
                pool.tensor_tensor(seen_p[:, 1:2], half[:, 0:1], half[:, 0:1], ALU.mult).then_inc(s["f_seen"], 1)
                pool.indirect_dma_start(
                    Y, bass.IndirectOffsetOnAxis(ap=xt[:, u, D + 1:D + 2].bitcast(I32), axis=0),
                    ys[:, u % 2, :], None, bounds_check=2 * NT * P - 1, oob_is_err=False).then_inc(s[f"f_sc{u}"], 16)

            with pool.Fori(0, FT // RING) as k:
                for u in range(RING):
                    scatter(k * RING + u, u)

        @block.vector
        def _(dve):
            dve.memset(vs[:, :, :, :], 1.0).then_inc(s["g1"], 1)
            dve.memset(state[:, :, :, :], 0.0).then_inc(s["g1"], 1)
            dve.wait_ge(s["w"], 16 * NW)
            dve.wait_ge(s["ce"], 1)
            dve.tensor_scalar_add(cR[:, :], cE[:, :], 1.0).then_inc(s["cr"], 1)
            dve.wait_ge(s["cr"], 1)
            dve.reciprocal(cE[:, :], cR[:, :]).then_inc(s["cr"], 1)
            dve.wait_ge(s["cr"], 2)
            dve.tensor_tensor(cS[:, :], cE[:, :], cT[:, :], ALU.mult).then_inc(s["cr"], 1)
            dve.wait_ge(s["cr"], 3)
            dve.tensor_copy(cB[:, :, :], bcast(cS[:, :], P)).then_inc(s["cb"], 1)
            dve.wait_ge(s["sigE"], 1)
            dve.tensor_scalar_add(sig[:, 0, :], hexp[:, :], 1.0).then_inc(s["sigR"], 1)
            dve.wait_ge(s["sigR"], 1)
            dve.reciprocal(sig[:, 1, :], sig[:, 0, :]).then_inc(s["sigR"], 1)
            dve.wait_ge(s["sigR"], 2)
            dve.tensor_scalar(sig[:, 0, :], sig[:, 1, :], -1.0, 1.0, ALU.mult, ALU.add).then_inc(s["sigR"], 1)
            dve.wait_ge(s["sigA"], 1)
            dve.tensor_scalar_mul(deps[:, :], deps[:, :], EPS).then_inc(s["sigR"], 1)
            for i, (lo, hi) in enumerate(((0, DE), (DE, 2 * DE), (2 * DE, 4 * DE))):
                dve.tensor_scalar_mul(wcat[:, lo:hi], wraw[:, lo:hi], cols[:, 2 * i:2 * i + 1]).then_inc(s["fold"], 1)
                dve.tensor_copy(bcol[:, i, :], cols[:, 2 * i + 1:2 * i + 2].to_broadcast([P, P])).then_inc(s["fold"], 1)
            dve.wait_ge(s["bp"], 1)
            dve.tensor_tensor(bias[:, 0:512], PA[:, :], bqk[:, :], ALU.add).then_inc(s["bc1"], 1)
            dve.tensor_copy(bias[:, 512:], PV[:, :]).then_inc(s["bc1"], 1)
            for b in range(B):
                dve.wait_ge(s["mp"], b + 1)
                dve.tensor_copy(mod[:, b, 0:512], S0[:, :])
                dve.tensor_copy(mod[:, b, 512:], S1[:, 0:256]).then_inc(s["mc"], 1)
            dve.wait_ge(s["mc"], B)
            for i in (1, 4):
                m = mod[:, :, i * D:(i + 1) * D]
                dve.tensor_scalar_add(m, m, 1.0).then_inc(s["mc"], 1)
            for i, tmp in ((2, ya), (5, yb)):
                m = mod[:, :, i * D:(i + 1) * D]
                dve.tensor_scalar(tmp[:, :, :], m, 0.0, 2.0, ALU.is_ge, ALU.mult).then_inc(s["mc"], 1)
            dve.wait_ge(s["mc"], B + 4)
            for i, tmp in ((2, zt), (5, sq)):
                m = mod[:, :, i * D:(i + 1) * D]
                dve.scalar_tensor_tensor(tmp[:, :, :], m, -1.0, m, ALU.mult, ALU.max).then_inc(s["mc"], 1)
            dve.wait_ge(s["mc"], B + 6)
            for i, tmp in ((2, zt), (5, sq)):
                dve.tensor_scalar_max(tmp[:, :, :], tmp[:, :, :], 0.25).then_inc(s["mc"], 1)
            dve.wait_ge(s["mc"], B + 8)
            for i, sign, size in ((2, ya, zt), (5, yb, sq)):
                dve.scalar_tensor_tensor(mod[:, :, i * D:(i + 1) * D], sign[:, :, :], -1.0, size[:, :, :],
                                         ALU.add, ALU.mult).then_inc(s["mc"], 1)
            dve.wait_ge(s["mc"], B + 10)
            for i, dst in enumerate((gaw, gab)):
                dve.tensor_tensor(dst[:, :, :], mod[:, :, 2 * D:3 * D],
                                  ow_bc[:, i, :].unsqueeze(1).to_broadcast([P, B, D]), ALU.mult).then_inc(s["mc"], 1)
            dve.wait_ge(s["mc"], B + 12)

            with dve.Fori(0, NC) as c:
                dve.wait_ge(s["x_in"], 16 * NC)
                for b in range(B):
                    dve.bn_stats(st[:, b, :], x_all[:, bass.ds(c * 4 + b, 1), :]).then_inc(s["a_st"], 1)
                dve.wait_ge(s["a_st"], c * 4 + 4)
                dve.tensor_copy(seen[:, :], st[:, 3, 0:1])
                for b in range(B):
                    dve.bn_aggr(mv[:, b, :], st[:, b, :]).then_inc(s["a_mv"], 1)
                dve.wait_ge(s["a_mv"], c * 4 + 4)
                dve.tensor_scalar_add(ve[:, :], mv[:, :, 1], EPS).then_inc(s["a_ve"], 1)
                dve.wait_ge(s["a_rs"], c + 1)
                for b in range(B):
                    dve.tensor_scalar(ya[:, b, :], x_all[:, bass.ds(c * 4 + b, 1), :].rearrange("p o d -> p (o d)"),
                                      mv[:, b, 0:1], rstd[:, b:b + 1], ALU.subtract, ALU.mult).then_inc(s["a_y"], 1)
                dve.wait_ge(s["a_y"], c * 4 + 4)
                dve.tensor_tensor(yb[:, :, :], ya[:, :, :], mod[:, :, D:2 * D], ALU.mult).then_inc(s["a_y1"], 1)
                dve.wait_ge(s["a_y1"], c + 1)
                dve.tensor_tensor(ya[:, :, :], yb[:, :, :], mod[:, :, 0:D], ALU.add).then_inc(s["a_y2"], 1)
                dve.wait_ge(s["a_y2"], c + 1)
                for b in range(B):
                    dve.bn_stats(st[:, b, :], ya[:, b, :]).then_inc(s["a_st2"], 1)
                dve.wait_ge(s["a_st2"], c * 4 + 4)
                dve.tensor_copy(seen[:, :], st[:, 3, 0:1])
                for b in range(B):
                    dve.bn_aggr(mv[:, b, :], st[:, b, :]).then_inc(s["a_mv2"], 1)
                dve.wait_ge(s["a_mv2"], c * 4 + 4)
                dve.tensor_scalar_add(ve[:, :], mv[:, :, 1], EPS).then_inc(s["a_ve2"], 1)
                dve.wait_ge(s["a_rs2"], c + 1)
                until(dve, s["a_zT"], c)
                for b in range(B):
                    dve.tensor_scalar(zt[:, b, :], ya[:, b, :], mv[:, b, 0:1], rstd[:, b:b + 1],
                                      ALU.subtract, ALU.mult).then_inc(s["a_z"], 1)

            def front1(n, b):
                until(dve, s["pqk"], n + 1)
                until(dve, s["e"], n)
                dve.tensor_tensor(qk[:, :], PA[:, :], bias[:, 0:512], ALU.add).then_inc(s["qk"], 1)
                until(dve, s["pvp"], n + 1)
                until(dve, s["u"], n - 1)
                dve.tensor_tensor(vs[:, b % 2, :, 0:DH], heads(PV[:, 0:DE]), heads(bias[:, 512:768]),
                                  ALU.add).then_inc(s["vv"], 1)
                dve.tensor_tensor(ps_[:, b, :], PV[:, DE:], bias[:, 768:], ALU.add).then_inc(s["vp"], 1)
                until(dve, s["qk"], n + 1)
                dve.tensor_reduce(mx[:, :], heads(qk[:, :]), AX.X, ALU.max).then_inc(s["mx"], 1)

            def front2(n):
                until(dve, s["e"], n + 1)
                dve.tensor_reduce(sm[:, :], heads(ex[:, :]), AX.X, ALU.add).then_inc(s["sum"], 1)
                until(dve, s["sum"], n + 1)
                until(dve, s["k2"], n)
                dve.reciprocal(rs[:, :], sm[:, :]).then_inc(s["r"], 1)
                until(dve, s["r"], n + 1)
                dve.tensor_tensor(rk[:, :, :], sig[:, :, :], rs[:, H:].unsqueeze(1).to_broadcast([P, 2, H]),
                                  ALU.mult).then_inc(s["rk"], 1)
                until(dve, s["rk"], n + 1)
                until(dve, s["tk"], n)
                until(dve, s["kw"], n)
                dve.tensor_tensor(heads(kf[:, :]), heads(ex[:, DE:]), bcast(rk[:, 0, :], DH),
                                  ALU.mult).then_inc(s["k1"], 1)

            def front3(n, b):
                until(dve, s["k1"], n + 1)
                until(dve, s["ka"], n * 32 + 32)
                until(dve, s["kb"], n * 16 - 48)
                if isinstance(n, int) and n == 0:
                    dve.wait_ge(s["kpz"], 1)
                dve.tensor_tensor(kf[:, :], kf[:, :], kp[:, b, :], ALU.add).then_inc(s["kf"], 1)

            def back(n, b):
                until(dve, s["g"], n + 1)
                G = M[:, :].rearrange("p (h w) -> p h w", w=32)
                dve.tensor_tensor(den[:, :], G[:, :, DH], deps[:, :], ALU.add).then_inc(s["dn"], 1)
                until(dve, s["gg"], n)
                dve.tensor_tensor(heads(av[:, :]), G[:, :, 0:DH], heads(ps_[:, b, :]), ALU.mult).then_inc(s["av"], 1)
                until(dve, s["dn"], n + 1)
                until(dve, s["ee"], n + 1)
                dve.scalar_tensor_tensor(heads(tt[:, :]), heads(ep[:, b, :]), 1.0, bcast(den[:, :], DH),
                                         ALU.add, ALU.mult).then_inc(s["tt"], 1)
                until(dve, s["tt"], n + 1)
                dve.reciprocal(tr[:, :], tt[:, :]).then_inc(s["tr"], 1)

            def masked(n, j):
                until(dve, s["sc"], n * 4 + j + 1)
                until(dve, s["o"], n)
                mask = cst[:, C_MASK + 4 * j * P:C_MASK + 4 * (j + 1) * P].rearrange("p (h i) -> p h i", i=P)
                dve.tensor_tensor(Pm[:, 4 * j:4 * j + 4, :], S[j % 2][:, :].rearrange("p (h i) -> p h i", i=P), mask,
                                  ALU.mult).then_inc(s["pm"], 1)

            def step(c, b, first=False, last=False):
                n = c * 4 + b
                nxt = (b + 1) % B
                until(dve, s["tq"], n + 1)
                until(dve, s["o"], n)
                for half_ in range(2):
                    dve.tensor_tensor(qeo[:, half_, :, :],
                                      TD[:, half_ * P:(half_ + 1) * P].unsqueeze(1).to_broadcast([P, 2, P]),
                                      bcast(cst[:, C_PM:C_PM + 2], P), ALU.mult).then_inc(s["qt"], 1)
                dve.tensor_tensor(qw[:, :, :].rearrange("p a i -> p (a i)"), TD[:, 0:2 * P], cst[:, C_WQ:C_WQ + 2 * P],
                                  ALU.mult).then_inc(s["qw"], 1)
                if not first:
                    back(n - 1, (b - 1) % B)
                if not last:
                    front1(n + 1, nxt)
                masked(n, 0)
                masked(n, 1)
                masked(n, 2)
                if not last:
                    front2(n + 1)
                masked(n, 3)
                if not last:
                    front3(n + 1, nxt)
                until(dve, s["u"], n + 1)
                dve.tensor_tensor(own_kv[:, :, :], M[:, 0:2 * HV].rearrange("p (h w) -> p h w", w=VW),
                                  cst[:, C_BM:C_BM + 2 * HV].rearrange("p (h w) -> p h w", w=VW),
                                  ALU.mult).then_inc(s["s1"], 1)
                until(dve, s["s1"], n + 1)
                until(dve, s["o"], n + 1)
                for half_ in range(2):
                    own = state[:, b, 8 * half_:8 * half_ + 8, 0:VW]
                    dve.scalar_tensor_tensor(own, own, cst[:, C_LAM + half_:C_LAM + half_ + 1],
                                             own_kv[:, 8 * half_:8 * half_ + 8, :], ALU.mult, ALU.add).then_inc(s["st"], 1)

            dve.memset(pad[:, 0:D + 1], 0.0).then_inc(s["init"], 1)
            dve.tensor_copy(pad[:, D + 1:].bitcast(I32), cst[:, C_PAD:C_PAD + 1]).then_inc(s["init"], 1)
            dve.memset(pad_i[:, :], E * REGION).then_inc(s["init"], 1)
            dve.memset(count[:, :], 0.0).then_inc(s["init"], 1)
            dve.tensor_copy(ids[:, :, :].rearrange("p b c -> p (b c)"), cst[:, C_ROW:C_ROW + 2 * B]).then_inc(s["init"], 1)
            dve.tensor_copy(tri[:, :], cst[:, C_TRI:C_TRI + P]).then_inc(s["init"], 1)
            dve.tensor_copy(one[:, :], cst[:, C_ONE:C_ONE + P]).then_inc(s["init"], 1)
            dve.wait_ge(s["init"], 7)
            dve.wait_ge(s["g1"], 2)
            front1(0, 0)
            front2(0)
            front3(0, 0)
            for b in range(B):
                step(0, b, first=b == 0)
            with dve.Fori(1, NC - 1) as c:
                for b in range(B):
                    step(c, b)
            for b in range(B):
                step(NC - 1, b, last=b == 3)
            back(NT - 1, 3)

            dve.wait_ge(s["yc"], NT)
            with dve.Fori(0, NC) as c:
                for b in range(B):
                    dve.bn_stats(st[:, b, :], y_all[:, bass.ds(c * 4 + b, 1), :]).then_inc(s["b_st"], 1)
                dve.wait_ge(s["b_st"], c * 4 + 4)
                dve.tensor_copy(seen[:, :], st[:, 3, 0:1])
                for b in range(B):
                    dve.bn_aggr(mv[:, b, :], st[:, b, :]).then_inc(s["b_mv"], 1)
                dve.wait_ge(s["b_mv"], c * 4 + 4)
                dve.tensor_scalar_add(ve[:, :], mv[:, :, 1], EPS).then_inc(s["b_ve"], 1)
                dve.wait_ge(s["b_rs"], c + 1)
                for b in range(B):
                    dve.tensor_scalar(ya[:, b, :], y_all[:, bass.ds(c * 4 + b, 1), :].rearrange("p o d -> p (o d)"),
                                      mv[:, b, 0:1], rstd[:, b:b + 1], ALU.subtract, ALU.mult).then_inc(s["b_t"], 1)
                dve.wait_ge(s["b_t"], c * 4 + 4)
                dve.tensor_tensor(yb[:, :, :], ya[:, :, :], gaw[:, :, :], ALU.mult).then_inc(s["b_t1"], 1)
                dve.wait_ge(s["b_t1"], c + 1)
                dve.tensor_tensor(ya[:, :, :], yb[:, :, :], gab[:, :, :], ALU.add).then_inc(s["b_t2"], 1)
                dve.wait_ge(s["b_t2"], c + 1)
                xc = x_all[:, bass.ds(c * 4, 4), :]
                dve.tensor_tensor(xc, xc, ya[:, :, :], ALU.add).then_inc(s["b_x2"], 1)
                dve.wait_ge(s["b_x2"], c + 1)
                dve.tensor_copy(seen[:, :], ya[:, 0, 0:1])
                for b in range(B):
                    dve.bn_stats(st[:, b, :], x_all[:, bass.ds(c * 4 + b, 1), :]).then_inc(s["c_st"], 1)
                dve.wait_ge(s["c_st"], c * 4 + 4)
                dve.tensor_copy(seen[:, :], st[:, 3, 0:1])
                for b in range(B):
                    dve.bn_aggr(mv[:, b, :], st[:, b, :]).then_inc(s["c_mv"], 1)
                dve.wait_ge(s["c_mv"], c * 4 + 4)
                dve.tensor_scalar_add(ve[:, :], mv[:, :, 1], EPS).then_inc(s["c_ve"], 1)
                dve.wait_ge(s["c_rs"], c + 1)
                for b in range(B):
                    dve.tensor_scalar(ya[:, b, :], x_all[:, bass.ds(c * 4 + b, 1), :].rearrange("p o d -> p (o d)"),
                                      mv[:, b, 0:1], rstd[:, b:b + 1], ALU.subtract, ALU.mult).then_inc(s["c_n"], 1)
                dve.wait_ge(s["c_n"], c * 4 + 4)
                dve.tensor_tensor(yb[:, :, :], ya[:, :, :], mod[:, :, 4 * D:5 * D], ALU.mult).then_inc(s["c_m"], 1)
                dve.wait_ge(s["c_m"], c + 1)
                until(dve, s["c_r"], 2 * c)
                until(dve, s["c_hT"], c)
                dve.tensor_tensor(zt[:, :, :], yb[:, :, :], mod[:, :, 3 * D:4 * D], ALU.add).then_inc(s["c_h"], 1)
                dve.wait_ge(s["c_lg"], c + 1)
                dve.tensor_copy(lg[:, :, :].rearrange("p b e -> p (b e)"), PA[:, 0:B * E]).then_inc(s["c_l"], 1)
                dve.wait_ge(s["c_l"], c + 1)
                dve.tensor_copy(seen[:, :], lg[:, 0, 0:1])
                for b in range(B):
                    dve.max(m8[:, b, :], lg[:, b, :]).then_inc(s["c_m8"], 1)
                dve.wait_ge(s["c_m8"], c * 4 + 4)
                dve.tensor_tensor(gap[:, :], m8[:, :, 1], m8[:, :, 0], ALU.subtract).then_inc(s["c_gap"], 1)
                for b in range(B):
                    dve.max_index(i8[:, b, :], m8[:, b, :], lg[:, b, :]).then_inc(s["c_i8"], 1)
                dve.wait_ge(s["c_i8"], c * 4 + 4)
                dve.tensor_copy(i8f[:, :, :], i8[:, :, 0:2]).then_inc(s["c_if"], 1)
                dve.wait_ge(s["c_if"], c + 1)
                iota = cst[:, C_IOTA:C_IOTA + E].unsqueeze(1).to_broadcast([P, B, E])
                for choice in range(2):
                    dve.tensor_tensor(pick[:, choice, :, :], iota, bcast(i8f[:, :, choice], E),
                                      ALU.is_equal).then_inc(s["c_pk"], 1)
                dve.wait_ge(s["c_pk"], 2 * c + 2)
                dve.tensor_tensor(used[:, :].rearrange("p (b e) -> p b e", e=E), pick[:, 0, :, :], pick[:, 1, :, :],
                                  ALU.add).then_inc(s["c_us"], 1)
                dve.wait_ge(s["c_e2"], c + 1)
                dve.tensor_scalar_add(e3[:, :], e2[:, :], 1.0).then_inc(s["c_w1"], 1)
                dve.wait_ge(s["c_w1"], c + 1)
                until(dve, s["c_sc"], c * 8 * 16)
                dve.reciprocal(rows[:, :, 0, D], e3[:, :]).then_inc(s["c_w2"], 1)
                dve.wait_ge(s["c_w2"], c + 1)
                dve.tensor_tensor(rows[:, :, 1, D], rows[:, :, 0, D], e2[:, :], ALU.mult).then_inc(s["c_w3"], 1)
                dve.tensor_copy(rows[:, :, :, D + 1].bitcast(I32), ids[:, :, :]).then_inc(s["c_id"], 1)
                dve.wait_ge(s["c_id"], c + 1)
                dve.tensor_scalar_add(ids[:, :, :], ids[:, :, :], float(B * P)).then_inc(s["c_idn"], 1)
                dve.wait_ge(s["c_ps"], c + 1)
                dve.tensor_tensor(posb[:, :, :], PV[:, 0:B * E].rearrange("p (b e) -> p b e", e=E),
                                  count[:, :].unsqueeze(1).to_broadcast([P, B, E]), ALU.add).then_inc(s["c_pb"], 1)
                dve.wait_ge(s["c_pb"], c + 1)
                dve.tensor_tensor(count[:, :], count[:, :], PV[:, B * E:(B + 1) * E], ALU.add).then_inc(s["c_cnt"], 1)
                dve.tensor_tensor(posr[:, :, :], posb[:, :, :],
                                  cst[:, C_REG:C_REG + E].unsqueeze(1).to_broadcast([P, B, E]), ALU.add).then_inc(s["c_pr"], 1)
                dve.wait_ge(s["c_pr"], c + 1)
                for choice in range(2):
                    dve.tensor_tensor(prod[:, choice, :, :], pick[:, choice, :, :], posr[:, :, :],
                                      ALU.mult).then_inc(s["c_pd"], 1)
                dve.wait_ge(s["c_pd"], 2 * c + 2)
                dve.tensor_reduce(dest[:, :, :], prod[:, :, :, :], AX.X, ALU.add).then_inc(s["c_d"], 1)
                dve.wait_ge(s["c_d"], c + 1)
                dve.wait_ge(s["c_w3"], c + 1)
                until(dve, s["c_seen"], c)
                dve.wait_ge(s["c_r"], 2 * c + 2)
                dve.tensor_copy(desti[:, :, :], dest[:, :, :]).then_inc(s["c_di"], 1)

            dve.wait_ge(s["c_cnt"], NC)
            dve.tensor_scalar_add(cnt1[:, :], count[:, :], float(P - 1)).then_inc(s["tile"], 1)
            dve.tensor_tensor(pad_f[:, :], count[0:1, :], cst[0:1, C_REG:C_REG + E], ALU.add).then_inc(s["tile"], 1)
            dve.wait_ge(s["tile"], 2)
            dve.tensor_copy(pad_i[:, 0:E], pad_f[:, :]).then_inc(s["meta"], 1)
            dve.tensor_copy(cnti[:, :], cnt1[:, :]).then_inc(s["tile"], 1)
            dve.wait_ge(s["tile"], 3)
            dve.tensor_single_scalar(cnti[:, :], cnti[:, :], 7, op=ALU.logical_shift_right).then_inc(s["tile"], 1)
            dve.wait_ge(s["tile"], 4)
            dve.tensor_copy(nts[:, :], cnti[:, :]).then_inc(s["tile"], 1)
            dve.wait_ge(s["tile"], 5)
            src = nts[:, :]
            for i, d in enumerate((1, 2, 4)):
                dve.tensor_copy(cum[:, i, 0:d], src[:, 0:d]).then_inc(s["tile"], 1)
                dve.tensor_tensor(cum[:, i, d:], src[:, d:], src[:, 0:E - d], ALU.add).then_inc(s["tile"], 1)
                dve.wait_ge(s["tile"], 2 * i + 7)
                src = cum[:, i, :]
            tau = cst[0:1, C_TAU:C_TAU + FT]
            dve.tensor_tensor(ge[:, :, :], bcast(tau, E), cum[0:1, 2, :].unsqueeze(1).to_broadcast([1, FT, E]),
                              ALU.is_ge).then_inc(s["tile"], 1)
            dve.wait_ge(s["tile"], 12)
            dve.tensor_tensor(gn[:, :, :], ge[:, :, :], nts[0:1, :].unsqueeze(1).to_broadcast([1, FT, E]),
                              ALU.mult).then_inc(s["tile"], 1)
            dve.tensor_reduce(meta[:, 0, :], ge[:, :, :], AX.X, ALU.add).then_inc(s["tile"], 1)
            dve.wait_ge(s["tile"], 14)
            dve.tensor_reduce(meta[:, 1, :], gn[:, :, :], AX.X, ALU.add).then_inc(s["tile"], 1)
            dve.tensor_scalar(meta[:, 2, :], meta[:, 0, :], float(E), None, ALU.is_lt).then_inc(s["tile"], 1)
            dve.wait_ge(s["tile"], 16)
            dve.tensor_tensor(meta[:, 3, :], tau, meta[:, 1, :], ALU.subtract).then_inc(s["tile"], 1)
            dve.wait_ge(s["tile"], 17)
            dve.tensor_tensor(meta[:, 4, :], meta[:, 3, :], meta[:, 2, :], ALU.mult).then_inc(s["tile"], 1)
            dve.tensor_scalar(meta[:, 1, :], meta[:, 0, :], float(REGION), None, ALU.mult).then_inc(s["tile"], 1)
            dve.wait_ge(s["tile"], 19)
            dve.scalar_tensor_tensor(meta[:, 3, :], meta[:, 4, :], float(P), meta[:, 1, :], ALU.mult,
                                     ALU.add).then_inc(s["tile"], 1)
            dve.tensor_scalar_min(meta_i[:, 1, :], meta[:, 0, :], float(E - 1)).then_inc(s["tile"], 1)
            dve.wait_ge(s["tile"], 21)
            dve.tensor_copy(meta_i[:, 0, :], meta[:, 3, :]).then_inc(s["meta"], 1)
            dve.wait_ge(s["meta"], 2)
            dve.wait_ge(s["wb"], 32)

            def hidden(t, u):
                e = expert_of(dve, t)
                until(dve, s["f_m1"], t + 1)
                until(dve, s["f_th"], t - 1)
                dve.tensor_tensor(hh[:, u % 2, :], S[u % 2][:, :], b1_bc[:, bass.ds(e * HID, HID)],
                                  ALU.add).then_inc(s["f_hb"], 1)

            def hidden_T(t, u):
                until(dve, s["f_th"], t + 1)
                until(dve, s["f_m2"], t - 1)
                dve.tensor_copy(hT[:, u % 2, :, :].rearrange("p h t -> p (h t)"), (PA, PV)[u % 2][:, :]).then_inc(s["f_hT"], 1)

            def gated(t, u, turn):
                e = expert_of(dve, t)
                until(dve, s["f_m2"], t + 1)
                until(dve, s["f_seen"], t)
                dve.tensor_tensor(yt[:, u % 2, :], (O, M)[u % 2][:, 0:D], b2_bc[:, bass.ds(e * D, D)],
                                  ALU.add).then_inc(s["f_yb"], 1)
                until(dve, s["f_yb"], t + 1)
                until(dve, s[f"f_sc{(u - 2) % RING}"], 16 * (turn + (u >= 2)))
                dve.tensor_scalar_mul(ys[:, u % 2, :], yt[:, u % 2, :], xt[:, u, D:D + 1]).then_inc(s["f_y"], 1)

            def expert(t, u, turn, ahead):
                hidden_T(t, u)
                if ahead > 2:
                    hidden(t + 2, (u + 2) % RING)
                gated(t, u, turn)

            hidden(0, 0)
            hidden(1, 1)
            for u in range(RING):
                expert(u, u, 0, RING)
            with dve.Fori(1, FT // RING - 1) as k:
                for u in range(RING):
                    expert(k * RING + u, u, k, RING)
            for u in range(RING):
                expert(FT - RING + u, u, FT // RING - 1, RING - u)

            for c in range(NC):
                dve.wait_ge(s[f"o_ld{c % 2}"], 32 * (c // 2 + 1))
                y0 = 8 * (c % 2)
                dve.tensor_tensor(ya[:, :, :], y_all[:, y0:y0 + 4, :], y_all[:, y0 + 4:y0 + 8, :], ALU.add).then_inc(s["o_s"], 1)
                dve.wait_ge(s["o_s"], c + 1)
                dve.tensor_tensor(yb[:, :, :], ya[:, :, :], mod[:, :, 5 * D:], ALU.mult).then_inc(s["o_g"], 1)
                dve.wait_ge(s["o_g"], c + 1)
                xc = x_all[:, 4 * c:4 * c + 4, :]
                dve.tensor_tensor(xc, xc, yb[:, :, :], ALU.add).then_inc(s["o_x"], 1)

        @block.tensor
        def _(pe):
            pe.wait_ge(s["fold"], 6)
            pe.wait_ge(s["w"], 16 * NW)
            pe.matmul(PA[:, 0:DE], bcol[:, 0, :], wraw[:, 0:DE], start=True, stop=True)
            pe.matmul(PA[:, DE:], bcol[:, 1, :], wraw[:, DE:2 * DE], start=True, stop=True)
            pe.matmul(PV[:, :], bcol[:, 2, :], wraw[:, 2 * DE:], start=True, stop=True).then_inc(s["bp"], 1)
            pe.wait_ge(s["cb"], 1)
            for b in range(B):
                until(pe, s["mc"], b)
                pe.matmul(S0[:, :], cB[:, b, :], wmod_sb[:, 0:512], start=True, stop=True)
                pe.matmul(S1[:, 0:256], cB[:, b, :], wmod_sb[:, 512:], start=True, stop=True).then_inc(s["mp"], 1)
            with pe.Fori(0, NC) as c:
                pe.wait_ge(s["a_z"], c * 4 + 4)
                until(pe, s["a_za"], c)
                for b in range(B):
                    last_ = pe.transpose(TA[:, b * P:(b + 1) * P], zt[:, b, :], ident)
                last_.then_inc(s["a_zT"], 1)

            def front(n, b):
                until(pe, s["qk"], n)
                pe.matmul(PA[:, :], zs[:, b * P:(b + 1) * P], wcat[:, 0:512], start=True, stop=True).then_inc(s["pqk"], 1)
                until(pe, s["vp"], n)
                pe.matmul(PV[:, :], zs[:, b * P:(b + 1) * P], wcat[:, 512:], start=True, stop=True).then_inc(s["pvp"], 1)

            def scores(n, j):
                until(pe, s["pm"], n * 4 + j - 1)
                r = 32 * j
                for half_ in range(2):
                    ins = pe.matmul(S[j % 2][:, half_ * 256:(half_ + 1) * 256], kT[r:r + 32, half_, :],
                                    qeo[r:r + 32, half_, :, :], start=True, stop=True)
                ins.then_inc(s["sc"], 1)

            def values(n, b, j):
                until(pe, s["pm"], n * 4 + 2 * (j % 2) + 2)
                if j == 0:
                    until(pe, s["qw"], n + 1)
                    until(pe, s["oc"], n)
                    if isinstance(n, int):
                        until(pe, s["we"], 2 * n if n <= 4 else 8 + 2 * max(n - NT + 4, 0))
                    until(pe, s["st"], 2 * (n - 3))
                    until(pe, s["vv"], n + 1)
                half_ = j // 2
                lhsT = state[:, b, 4 * j:4 * j + 4, :].rearrange("p h w -> p (h w)")
                oj = O[:, j * P:(j + 1) * P]
                pe.matmul(oj, lhsT, qw[:, half_, :], start=True, stop=False, skip_group_check=True)
                for i in range(4):
                    h = 4 * j + i
                    ins = pe.matmul(oj[32 * i:32 * i + VW, :], vs[:, b % 2, h, :], Pm[:, slot(h), :],
                                    start=False, stop=True, tile_position=(0, 32 * i), skip_group_check=True)
                if j == 3:
                    ins.then_inc(s["o"], 1)

            def g_back(n):
                until(pe, s["oc"], n + 1)
                until(pe, s["s1"], n + 1)
                until(pe, s["av"], n)
                for j in range(4):
                    ins = pe.transpose(M[:, j * P:(j + 1) * P], oT[:, j, :], ident)
                ins.then_inc(s["g"], 1)

            def t_gate(n):
                until(pe, s["gg"], n + 1)
                until(pe, s["kt"], n + 2)
                until(pe, s["yc"], n)
                for i in range(2):
                    ins = pe.transpose(TA[:, i * P:(i + 1) * P], gg[:, i * P:(i + 1) * P], ident)
                ins.then_inc(s["tg"], 1)

            def out_proj(n):
                until(pe, s["gt"], n + 1)
                for i in range(2):
                    ins = pe.matmul(TA[:, 256:256 + D], gT[:, i, :], wo_sb[:, i, :], start=i == 0, stop=i == 1)
                ins.then_inc(s["y"], 1)

            def step(c, b, first=False, last=False):
                n = c * 4 + b
                nxt = (b + 1) % B
                until(pe, s["qh"], n + 1)
                until(pe, s["qw"], n)
                for i in range(2):
                    ins = pe.transpose(TD[:, i * P:(i + 1) * P], qh[:, i * P:(i + 1) * P], ident)
                ins.then_inc(s["tq"], 1)
                until(pe, s["kf"], n + 1)
                until(pe, s["yc"], n - 1)
                for i in range(2):
                    ins = pe.transpose(TA[:, i * P:(i + 1) * P], kf[:, i * P:(i + 1) * P], ident)
                ins.then_inc(s["tk"], 1)
                if not first:
                    g_back(n - 1)
                if not last:
                    if b == 3:
                        until(pe, s["zs"], c + 2)
                    front(n + 1, nxt)
                until(pe, s["qt"], n * 2 + 2)
                until(pe, s["kt"], n + 1)
                scores(n, 0)
                scores(n, 1)
                if not first:
                    t_gate(n - 1)
                scores(n, 2)
                values(n, b, 0)
                scores(n, 3)
                values(n, b, 2)
                if not first:
                    out_proj(n - 1)
                values(n, b, 1)
                values(n, b, 3)
                until(pe, s["kw"], n + 1)
                until(pe, s["av"], n)
                for i in range(2):
                    ins = pe.matmul(M[:, i * HV:(i + 1) * HV], kw[:, i * P:(i + 1) * P],
                                    vs[:, b % 2, 8 * i:8 * i + 8, :], start=True, stop=True)
                ins.then_inc(s["u"], 1)
                if isinstance(c, int):
                    e = b if c == 0 else 4 + b
                    pe.wait_ge(s["ww"], 16 * 2 * E)
                    pe.wait_ge(s["oc"], n + 1)
                    for i in range(2):
                        until(pe, s["we"], 2 * e + i)
                        for k in range(4):
                            src = w1n[:, e, k, :] if i == 0 else w2n[:, e, k * P:(k + 1) * P]
                            ins = pe.transpose(O[:, k * P:(k + 1) * P], src, ident)
                        ins.then_inc(s["wt"], 1)

            pe.wait_ge(s["bc1"], 2)
            pe.wait_ge(s["zs"], 1)
            front(0, 0)
            for b in range(B):
                step(0, b, first=b == 0)
            with pe.Fori(1, NC - 1) as c:
                for b in range(B):
                    step(c, b)
            for b in range(B):
                step(NC - 1, b, last=b == 3)
            g_back(NT - 1)
            pe.wait_ge(s["gg"], NT)
            pe.wait_ge(s["yc"], NT - 1)
            for i in range(2):
                ins = pe.transpose(TA[:, i * P:(i + 1) * P], gg[:, i * P:(i + 1) * P], ident)
            ins.then_inc(s["tg"], 1)
            out_proj(NT - 1)

            pe.wait_ge(s["wg"], 16)
            pe.wait_ge(s["qw"], NT)
            pe.transpose(TD[:, 0:E], wgn[:, :], ident[0:E, 0:E]).then_inc(s["wgt"], 1)
            pe.wait_ge(s["wgt"], 2)
            pe.wait_ge(s["yc"], NT)
            pe.wait_ge(s["init"], 7)
            with pe.Fori(0, NC) as c:
                pe.wait_ge(s["c_h"], c + 1)
                until(pe, s["c_hs"], c)
                for b in range(B):
                    ins = pe.transpose(TA[:, b * P:(b + 1) * P], zt[:, b, :], ident)
                ins.then_inc(s["c_hT"], 1)
                pe.wait_ge(s["c_hs"], c + 1)
                until(pe, s["c_l"], c)
                for b in range(B):
                    ins = pe.matmul(PA[:, b * E:(b + 1) * E], zs[:, b * P:(b + 1) * P], wgT[:, :], start=True, stop=True)
                ins.then_inc(s["c_lg"], 1)
                pe.wait_ge(s["c_us"], c + 1)
                until(pe, s["c_cnt"], c)
                for b in range(B + 1):
                    for a in range(min(b + 1, B)):
                        ins = pe.matmul(PV[:, b * E:(b + 1) * E], (tri if a == b else one)[:, :],
                                        used[:, a * E:(a + 1) * E], start=a == 0, stop=a == min(b, B - 1))
                ins.then_inc(s["c_ps"], 1)

            def x_transpose(t, u, turn):
                until(pe, s[f"f_xt{u}"], 16 * turn + 16)
                until(pe, s["f_xT"], t - 1)
                pe.transpose((TA, TD)[u % 2][:, 0:P], xt[:, u, 0:D], ident).then_inc(s["f_xp"], 1)

            def up(t, u):
                e = expert_of(pe, t)
                until(pe, s["f_xT"], t + 1)
                until(pe, s["f_hb"], t - 1)
                pe.matmul(S[u % 2][:, :], xT[:, u % 2, :], w1T[:, bass.ds(e * HID, HID)], start=True,
                          stop=True).then_inc(s["f_m1"], 1)

            def h_transpose(t, u):
                until(pe, s["f_h"], t + 1)
                until(pe, s["f_hT"], t - 1)
                for k in range(4):
                    ins = pe.transpose((PA, PV)[u % 2][:, k * P:(k + 1) * P], hh[:, u % 2, k * P:(k + 1) * P], ident)
                ins.then_inc(s["f_th"], 1)

            def down(t, u):
                e = expert_of(pe, t)
                until(pe, s["f_hT"], t + 1)
                until(pe, s["f_yb"], t - 1)
                for k in range(4):
                    ins = pe.matmul((O, M)[u % 2][:, 0:D], hT[:, u % 2, k, :], w2T[:, bass.ds(e * HID + k * P, P)],
                                    start=k == 0, stop=k == 3)
                ins.then_inc(s["f_m2"], 1)

            def expert(t, u, turn, ahead):
                h_transpose(t, u)
                if ahead > 2:
                    up(t + 2, (u + 2) % RING)
                down(t, u)
                if ahead > 3:
                    x_transpose(t + 3, (u + 3) % RING, turn + (u >= 1))

            pe.wait_ge(s["meta"], 2)
            pe.wait_ge(s["we"], 2 * E)
            x_transpose(0, 0, 0)
            x_transpose(1, 1, 0)
            up(0, 0)
            x_transpose(2, 2, 0)
            up(1, 1)
            for u in range(RING):
                expert(u, u, 0, RING)
            with pe.Fori(1, FT // RING - 1) as k:
                for u in range(RING):
                    expert(k * RING + u, u, k, RING)
            for u in range(RING):
                expert(FT - RING + u, u, FT // RING - 1, RING - u)


NW = 19
_INS = ["L0_attn_x", "L0_attn_in_ln_w", "L0_attn_in_ln_b", "L0_attn_q_ln_w", "L0_attn_q_ln_b", "L0_attn_k_ln_w",
        "L0_attn_k_ln_b", "L0_attn_out_ln_w", "L0_attn_out_ln_b", "L0_attn_W_in", "L0_attn_W_out", "L0_attn_Wq",
        "L0_attn_bq", "L0_attn_Wk", "L0_attn_bk", "L0_attn_smear_factor", "L0_attn_log_scale", "L0_ffn_Wg",
        "L0_ffn_W1", "L0_ffn_b1", "L0_ffn_W2", "L0_ffn_b2", "L0_c", "L0_wmod"]


def kernel(**inputs):
    import numpy as _np
    import concourse.bacc as _bacc
    from concourse import mybir as _mybir
    from concourse.bass_utils import run_bass_kernel_spmd as _run

    nc = _bacc.Bacc("TRN2", target_bir_lowering=False, num_devices=1)
    arrays, args = {}, []
    for name in _INS:
        a = _np.ascontiguousarray(inputs[name])
        arrays[f"in_{name}_dram"] = a
        args.append(nc.dram_tensor(f"in_{name}_dram", a.shape, _mybir.dt.from_np(a.dtype), kind="ExternalInput").ap())
    k = shape_constants()
    arrays["consts_dram"] = k
    args.append(nc.dram_tensor("consts_dram", k.shape, F32, kind="ExternalInput").ap())
    out = nc.dram_tensor("out_0_dram", (B, L, D), F32, kind="ExternalOutput").ap()
    build(nc, *args, out)
    r = _run(nc, [arrays], core_ids=[0])
    return r.results[0]["out_0_dram"]
```

```python
from contextlib import ExitStack

import numpy as np

import concourse.bass as bass
from concourse import mybir

F32 = mybir.dt.float32
BF16 = mybir.dt.bfloat16
I32 = mybir.dt.int32
U32 = mybir.dt.uint32
ALU = mybir.AluOpType
ACT = mybir.ActivationFunctionType
AX = mybir.AxisListType

B, L, D = 4, 1024, 128
P = 128
NC = L // P
NT = B * NC
DE = 256
H = 16
DH = DE // H
HD = H // 2
E, HID = 8, 512
VW = DH + 1
HV = 8 * VW
EPS = 1e-5

REGION = B * L + P
XROWS = E * REGION + P
XW = D + 2
FT = 2 * B * L // P + E
RING = 8

C_ID = 0
C_MASK = C_ID + P
C_PM = C_MASK + H * P
C_WQ = C_PM + 2
C_BM = C_WQ + 2 * P
C_LAM = C_BM + 2 * HV
C_WK = C_LAM + 2
C_TRI = C_WK + H
C_ONE = C_TRI + P
C_IOTA = C_ONE + P
C_REG = C_IOTA + E
C_TAU = C_REG + E
C_ROW = C_TAU + FT
C_PAD = C_ROW + 2 * B
C_N = C_PAD + 1


def slot(h):
    return 4 * (h % 8 // 2) + 2 * (h // 8) + h % 2


def shape_constants():
    slope = (2.0 ** np.linspace(0.0, -8.0, HD)).astype(np.float32).astype(np.float64)
    rate = np.concatenate([slope, np.zeros(H - HD)])
    t = np.arange(P)
    k = np.zeros((P, C_N), np.float64)
    k[:, C_ID:C_ID + P] = np.eye(P)
    ahead = t[None, :] - t[:, None]
    for h in range(H):
        s, at = rate[h], C_MASK + slot(h) * P
        k[:, at:at + P] = np.where(ahead >= 0, np.exp(-s * np.maximum(ahead, 0)), 0.0)
    for par in range(2):
        k[:, C_PM + par] = (t // DH) % 2 == par
    for half in range(2):
        r = rate[8 * half + t // DH]
        k[:, C_WQ + half * P:C_WQ + (half + 1) * P] = np.exp(-r[:, None] * (t[None, :] + 1))
        own = (t // DH)[:, None] == np.arange(8)[None, :].repeat(VW, 1)
        k[:, C_BM + half * HV:C_BM + (half + 1) * HV] = own
        k[:, C_LAM + half] = np.exp(-r * P)
    k[:, C_TRI:C_TRI + P] = t[:, None] < t[None, :]
    k[:, C_ONE:C_ONE + P] = 1.0
    k[:, C_IOTA:C_IOTA + E] = np.arange(E)
    k[:, C_REG:C_REG + E] = np.arange(E) * REGION
    k[:, C_TAU:C_TAU + FT] = np.arange(FT)
    for b in range(B):
        for choice in range(2):
            k[:, C_ROW + 2 * b + choice] = choice * B * L + b * P + t
    k[:, C_PAD] = 2 * B * L + t
    k[:, C_WK:C_WK + H] = np.exp(-rate[None, :] * (P - 1 - t)[:, None])
    return k.astype(np.float32)


def until(eng, sem, value):
    if isinstance(value, int) and value <= 0:
        return
    eng.wait_ge(sem, value)


def build(nc, x, in_w, in_b, q_w, q_b, k_w, k_b, out_w, out_b, W_in, W_out, Wq, bq, Wk, bk,
          smear, log_scale, Wg, W1, b1, W2, b2, cond, wmod, consts, out):
    ctx = ExitStack()
    with ctx:
        def sb(name, shape, dt=F32):
            return ctx.enter_context(nc.sbuf_tensor(name, shape, dt))

        def psum(name):
            return ctx.enter_context(nc.psum_tensor(name, [P, 512], F32))

        def sem(name):
            return ctx.enter_context(nc.semaphore(name))

        x_all = sb("x_all", [P, NT, D])
        zT_all = sb("zT_all", [P, NT * P])
        y_all = sb("y_all", [P, NT, D])
        cst = sb("cst", [P, C_N])
        ident = cst[:, C_ID:C_ID + P]
        mod = sb("mod", [P, B, 6 * D])
        gaw = sb("gaw", [P, B, D])
        gab = sb("gab", [P, B, D])
        wcat = sb("wcat", [P, 4 * DE])
        wraw = sb("wraw", [P, 4 * DE])
        wo_sb = sb("wo_sb", [P, 2, D])
        cols = sb("cols", [P, 6])
        bcol = sb("bcol", [P, 4, P])
        bqk = sb("bqk", [P, 2 * DE])
        ow_bc = sb("ow_bc", [P, 2, D])
        hv = sb("hv", [P, 2, H])
        sig = sb("sig", [P, 2, H])
        hexp = sb("hexp", [P, H])
        deps = sb("deps", [P, H])
        cT = sb("cT", [P, B])
        cE = sb("cE", [P, B])
        cR = sb("cR", [P, B])
        cS = sb("cS", [P, B])
        cB = sb("cB", [P, B, P])
        wmod_sb = sb("wmod_sb", [P, 6 * D])
        half = sb("half", [P, B])

        st = sb("st", [P, B, 6])
        mv = sb("mv", [P, B, 2])
        seen = sb("seen", [P, 4])
        seen_p = sb("seen_p", [P, 1 + RING])
        ve = sb("ve", [P, B])
        rstd = sb("rstd", [P, B])
        ya = sb("ya", [P, B, D])
        yb = sb("yb", [P, B, D])
        sq = sb("sq", [P, B, D])
        zt = sb("zt", [P, B, D])

        zs = sb("zs", [P, B * P])
        qk = sb("qk", [P, 2 * DE])
        mx = sb("mx", [P, 2 * H])
        ex = sb("ex", [P, 2 * DE])
        sm = sb("sm", [P, 2, 2 * H])
        rs = sb("rs", [P, H])
        rk = sb("rk", [P, 2, H])
        k1 = sb("k1", [P, DE])
        k2 = sb("k2", [P, DE])
        kf = sb("kf", [P, DE])
        kp = sb("kp", [P, B, DE])
        kw = sb("kw", [P, DE])
        vs = sb("vs", [P, 2, H, VW])
        ps_ = sb("ps_", [P, B, DE])
        ep = sb("ep", [P, B, DE])
        qeo = sb("qeo", [P, 2, 2, 2, P])
        qT = sb("qT", [P, 2 * P])
        qw = sb("qw", [P, 2, 2, P])
        kT = sb("kT", [P, 2, P])
        Pm = sb("Pm", [P, H, P])
        state = sb("state", [P, B, H, 32])
        own_kv = sb("own_kv", [P, H, VW])
        oT = sb("oT", [P, 4, P])
        den = sb("den", [P, 2, H])
        epsq = sb("epsq", [P, 2, H])
        av = sb("av", [P, DE])
        gg = sb("gg", [P, DE])
        gT = sb("gT", [P, 2, P])

        nst = sb("nst", [P, 2, 6])
        nmv = sb("nmv", [P, 2, 2])
        nve = sb("nve", [P, 2])
        nrs = sb("nrs", [P, 2])
        nt = sb("nt", [P, 2, D])
        np_ = sb("np", [P, 3, D])
        h_all = zT_all

        w1n = sb("w1n", [P, E, 4, D])
        w2n = sb("w2n", [P, E, HID])
        w1T = w1n[:, :, :, :].rearrange("p e h d -> p (e h d)")
        w2T = w2n[:, :, :].rearrange("p e h -> p (e h)")
        b1n = sb("b1n", [4 * E, P])
        b1T = sb("b1T", [P, 4 * E])
        b2_row = sb("b2_row", [1, E * D])
        wgn = sb("wgn", [E, D])
        wgT = sb("wgT", [P, E])
        tri = sb("tri", [P, P], BF16)
        one = sb("one", [P, P], BF16)
        hs = ep[:, :, :].rearrange("p b d -> p (b d)")[:, 0:B * P]
        hTs = wraw[:, :].rearrange("p (q t) -> p q t", q=2)
        lg = sb("lg", [P, B, E])
        m8 = sb("m8", [P, B, 8])
        i8 = sb("i8", [P, B, 8], U32)
        i8f = sb("i8f", [P, B, 2])
        pick = sb("pick", [P, 2, B, E])
        used = sb("used", [P, B * E], BF16)
        gap = sb("gap", [P, B])
        e2 = sb("e2", [P, B])
        e3 = sb("e3", [P, B])
        count = sb("count", [P, E])
        posb = sb("posb", [P, B, E])
        posr = sb("posr", [P, B, E])
        prod = sb("prod", [P, 2, B, E])
        dest = sb("dest", [P, 2, B])
        desti = sb("desti", [P, 2, 2, B], I32)
        ids = sb("ids", [P, B, 2])
        rows = y_all[:, :, :].rearrange("p n d -> p (n d)")[:, 0:4 * B * XW].rearrange(
            "p (q b c w) -> p q b c w", q=2, b=B, c=2)
        pad = sb("pad", [P, XW])
        cnt1 = sb("cnt1", [P, E])
        cnti = sb("cnti", [P, E], I32)
        nts = sb("nts", [P, E])
        cum = sb("cum", [P, 3, E])
        room = Pm[:, :, :].rearrange("p h i -> p (h i)")
        ge = room[0:1, 0:FT * E].rearrange("p (t e) -> p t e", e=E)
        gn = room[0:1, FT * E:2 * FT * E].rearrange("p (t e) -> p t e", e=E)
        hT = room[:, 0:2 * HID].rearrange("p (u h t) -> p u h t", u=2, h=4)
        w1s = zT_all[:, 0:4 * HID].rearrange("p (u h) -> p u h", u=4)
        xT = zT_all[:, 4 * HID:4 * HID + 4 * P].rearrange("p (u t) -> p u t", u=4)
        meta = sb("meta", [1, 5, FT])
        meta_i = sb("meta_i", [1, 2, FT], I32)
        pad_f = sb("pad_f", [1, E])
        pad_i = sb("pad_i", [1, E + 1], I32)
        xt = state[:, :, :, :].rearrange("p b h w -> p (b h w)")[:, 0:RING * XW].rearrange("p (u w) -> p u w", u=RING)
        ys = kp[:, :, :].rearrange("p b (u d) -> p (b u) d", d=D)
        X = nc.dram_tensor("expert_in", (XROWS, XW), F32).ap()
        Y = nc.dram_tensor("expert_out", (2 * NT * P, D), F32).ap()

        PA, PV, TD, TA, S0, S1, O, M = (psum(n) for n in ("PA", "PV", "TD", "TA", "S0", "S1", "O", "M"))
        S = (S0, S1)

        names = ("w x_in sigE sigA sigR ce cr cb mp mc kpz fold bp bc1 half_ok g1 "
                 "a_st a_mv a_ve a_rs a_y a_m a_st2 a_mv2 a_ve2 a_rs2 a_z a_zT a_za "
                 "zs pqk pvp mx vv vp d e sp sum r rk eq k2 ka kb k1 kf kw tq tk qT qt qw kt sc pm o u s1 st "
                 "oc g dn av gg tg gt y yc "
                 "b_out n_yst n_xst n_ymv n_xmv n_ve n_rs n_yt n_xt n_x n_xp n_h n_hp "
                 "ww wb wt we wg wgt init c_z c_r c_hT c_hs c_lg c_l c_m8 c_i8 c_if c_pk "
                 "c_us c_gap c_e2 c_w c_ps c_pl c_cnt c_di c_id c_idn c_sc0 c_sc1 "
                 "tile meta padf padd b1 "
                 "c_seen f_seen f_xp f_xT f_ws f_m1 f_h f_m2 f_y o_s o_g o_x "
                 + " ".join(f"f_xt{u} f_sc{u}" for u in range(RING)) + " " + " ".join(f"o_ld{i}" for i in range(4)))
        s = {n: sem("s_" + n) for n in names.split()}

        block = ctx.enter_context(nc.Block())

        def bcast(ap, n):
            return ap.unsqueeze(2).to_broadcast([ap.shape[0], ap.shape[1], n])

        def expert_of(eng, t):
            at = meta_i[0:1, 1, t:t + 1] if isinstance(t, int) else meta_i[0:1, 1, bass.ds(t, 1)]
            return eng.value_load(at, min_val=0, max_val=E - 1)

        heads = lambda ap: ap.rearrange("p (h f) -> p h f", f=DH)

        @block.sync
        def _(sp):
            for c in range(NC):
                sp.dma_start(x_all[:, 4 * c:4 * c + 4, :],
                             x[:, c * P:(c + 1) * P, :].rearrange("b p d -> p b d")).then_inc(s["x_in"], 16)
            for e in range(E):
                sp.dma_start(w1n[:, e, :, :], W1[e].rearrange("(h p) d -> p h d", p=P)).then_inc(s["ww"], 16)
                sp.dma_start(w2n[:, e, :], W2[e]).then_inc(s["ww"], 16)
            sp.dma_start(wgn[:, :], Wg).then_inc(s["wg"], 16)
            sp.dma_start(b1n[:, :], b1.rearrange("e (k p) -> (e k) p", p=P)).then_inc(s["wg"], 16)
            sp.dma_start(b2_row[:, :], b2.rearrange("e d -> (e d)").unsqueeze(0)).then_inc(s["wb"], 16)
            def shift(c, b):
                n = c * 4 + b
                done = n + 1
                until(sp, s["k2"], done)
                sp.dma_start(kp[1:113, b, :], k2[0:112, :]).then_inc(s["ka"], 16)
                sp.dma_start(kp[113:128, b, :], k2[112:127, :]).then_inc(s["ka"], 16)
                until(sp, s["kf"], done)
                sp.dma_start(kp[0:1, b, :], k2[127:128, :]).then_inc(s["kb"], 16)

            for b in range(B):
                shift(0, b)
            with sp.Fori(1, NC) as c:
                for b in range(B):
                    shift(c, b)
            sp.wait_ge(s["meta"], 2)
            sp.wait_ge(s["init"], 3)
            for e in range(E + 1):
                r = sp.value_load(pad_i[0:1, e:e + 1], min_val=0, max_val=XROWS - P)
                sp.dma_start(X[bass.ds(r, P), :], pad[:, :]).then_inc(s["padd"], 16)
            sp.wait_ge(s["padd"], 16 * (E + 1))
            for q in range(2):
                sp.wait_ge(s[f"c_sc{q}"], 16 * NT)

            def fetch(t, u, turn):
                r = sp.value_load(meta_i[0:1, 0, t:t + 1] if isinstance(t, int) else meta_i[0:1, 0, bass.ds(t, 1)],
                                  min_val=0, max_val=XROWS - P)
                until(sp, s[f"f_sc{u}"], 16 * turn)
                sp.dma_start(xt[:, u, :], X[bass.ds(r, P), :]).then_inc(s[f"f_xt{u}"], 16)

            for u in range(RING):
                fetch(u, u, 0)
            with sp.Fori(1, FT // RING) as k:
                for u in range(RING):
                    fetch(k * RING + u, u, k)

            for u in range(RING):
                sp.wait_ge(s[f"f_sc{u}"], 16 * FT // RING)
            for c in range(NC):
                if c >= 4:
                    sp.wait_ge(s["o_s"], c - 3)
                for choice in range(2):
                    r0, y0 = choice * NT * P + c * B * P, 8 * (c % 4) + 4 * choice
                    sp.dma_start(y_all[:, y0:y0 + 4, :],
                                 Y[r0:r0 + B * P, :].rearrange("(b p) d -> p b d", p=P)).then_inc(s[f"o_ld{c % 4}"], 16)
            sp.wait_ge(s["b_out"], 16 * NC)

        @block.scalar
        def _(act):
            act.dma_start(cst[:, :], consts).then_inc(s["w"], 16)
            act.dma_start(wmod_sb[:, :], wmod).then_inc(s["w"], 16)
            act.dma_start(cT[:, :], cond.rearrange("b k -> k b"), allow_slow_non_contiguous=True).then_inc(s["w"], 16)
            for i, v in enumerate((q_w, q_b, k_w, k_b, in_w, in_b)):
                act.dma_start(cols[:, i:i + 1], v.unsqueeze(1), allow_slow_non_contiguous=True).then_inc(s["w"], 16)
            act.dma_start(wraw[:, 0:DE], Wq).then_inc(s["w"], 16)
            act.dma_start(wraw[:, DE:2 * DE], Wk).then_inc(s["w"], 16)
            act.dma_start(wraw[:, 2 * DE:], W_in).then_inc(s["w"], 16)
            act.dma_start(wo_sb[:, :, :], W_out.rearrange("(h k) d -> k h d", h=2)).then_inc(s["w"], 16)
            for i, v in enumerate((bq, bk)):
                act.dma_start(bqk[:, i * DE:(i + 1) * DE], v.partition_broadcast(P)).then_inc(s["w"], 16)
            for i, v in enumerate((out_w, out_b)):
                act.dma_start(ow_bc[:, i, :], v.partition_broadcast(P)).then_inc(s["w"], 16)
            for i, v in enumerate((smear, log_scale)):
                act.dma_start(hv[:, i, :], v.partition_broadcast(P)).then_inc(s["w"], 16)
            act.wait_ge(s["w"], 16 * NW)
            act.activation(cE[:, :], cT[:, :], ACT.Exp, scale=-1.0).then_inc(s["ce"], 1)
            act.activation(hexp[:, :], hv[:, 0, :], ACT.Exp, scale=-1.0).then_inc(s["sigE"], 1)
            act.activation(deps[:, :], hv[:, 1, :], ACT.Exp, scale=2.0).then_inc(s["sigA"], 1)
            with act.Fori(0, NC) as c:
                act.wait_ge(s["a_zT"], c + 1)
                act.activation(zT_all[:, bass.ds(c * 512, 512)], TA[:, :], ACT.Identity, bias=1.0).then_inc(s["a_za"], 1)

            def stage_z(c):
                until(act, s["pvp"], c * 4)
                act.copy(zs[:, :], zT_all[:, bass.ds(c * 512, 512)]).then_inc(s["zs"], 1)

            def front(n, b):
                until(act, s["pvp"], n + 1)
                until(act, s["u"], n - 1)
                act.copy(vs[:, b % 2, :, 0:DH], heads(PV[:, 0:DE])).then_inc(s["vv"], 1)
                until(act, s["sp"], n - 3)
                act.copy(ps_[:, b, :], PV[:, DE:]).then_inc(s["vp"], 1)
                act.activation(ep[:, b, :], PV[:, DE:], ACT.Tanh, scale=0.5).then_inc(s["vp"], 1)
                until(act, s["d"], n + 1)
                until(act, s["tq"], n)
                until(act, s["k2"], n)
                until(act, s["sum"], n)
                act.activation(ex[:, :], qk[:, :], ACT.Exp).then_inc(s["e"], 1)
            def queries(n, b):
                until(act, s["tq"], n + 1)
                until(act, s["qw"], n)
                act.copy(qT[:, :], TD[:, 0:2 * P]).then_inc(s["qT"], 1)
                until(act, s["qT"], n + 1)
                until(act, s["o"], n - 1)
                for half_ in range(2):
                    for par in range(2):
                        act.activation(qeo[:, b % 2, half_, par, :], qT[:, half_ * P:(half_ + 1) * P], ACT.Copy,
                                       scale=cst[:, C_PM + par:C_PM + par + 1]).then_inc(s["qt"], 1)

            def step(c, b, first=False, last=False):
                n = c * 4 + b
                nxt = (b + 1) % B
                until(act, s["tk"], n + 1)
                until(act, s["o"], n)
                act.copy(kT[:, :, :], TA[:, 0:2 * P]).then_inc(s["kt"], 1)
                if not last:
                    front(n + 1, nxt)
                if not first:
                    until(act, s["tg"], n)
                    until(act, s["y"], n - 1)
                    act.copy(gT[:, :, :], TA[:, 0:2 * P]).then_inc(s["gt"], 1)
                if not last:
                    queries(n + 1, nxt)
                if not first:
                    until(act, s["y"], n)
                    act.copy(y_all[:, bass.ds(n - 1, 1), :], TA[:, 256:256 + D]).then_inc(s["yc"], 1)
                until(act, s["o"], n + 1)
                until(act, s["g"], n)
                act.copy(oT[:, :, :], O[:, :]).then_inc(s["oc"], 1)
                if isinstance(c, int):
                    e = b if c == 0 else 4 + b
                    for i, dst in enumerate((w1T, w2T)):
                        act.wait_ge(s["wt"], 2 * e + i + 1)
                        act.copy(dst[:, e * HID:(e + 1) * HID], O[:, :]).then_inc(s["we"], 1)
                if b == 2 and not (isinstance(c, int) and c == NC - 1):
                    stage_z(c + 1)

            act.wait_ge(s["a_za"], NC)
            stage_z(0)
            front(0, 0)
            queries(0, 0)
            for b in range(B):
                step(0, b, first=b == 0)
            with act.Fori(1, NC - 1) as c:
                for b in range(B):
                    step(c, b)
            for b in range(B):
                step(NC - 1, b, last=b == 3)
            n = NT
            act.wait_ge(s["tg"], n)
            act.wait_ge(s["y"], n - 1)
            act.copy(gT[:, :, :], TA[:, 0:2 * P]).then_inc(s["gt"], 1)
            act.wait_ge(s["y"], n)
            act.copy(y_all[:, n - 1, :], TA[:, 256:256 + D]).then_inc(s["yc"], 1)
            act.wait_ge(s["wgt"], 1)
            act.copy(b1T[:, :], TD[:, E:E + 4 * E]).then_inc(s["wgt"], 1)
            act.copy(wgT[:, :], TD[:, 0:E]).then_inc(s["wgt"], 1)
            def route(c, q, turn):
                chunk = h_all[:, bass.ds(c * 512, 512)]
                act.copy(hs[:, :], chunk).then_inc(s["c_z"], 1)
                until(act, s["c_hT"], c + 1)
                until(act, s["c_lg"], c - 1)
                until(act, s[f"c_sc{q}"], 16 * 2 * B * turn)
                act.copy(hTs[:, q, :], (TA, PA)[q][:, :]).then_inc(s["c_hs"], 1)
                act.copy(rows[:, q, :, :, 0:D],
                         chunk.rearrange("p (b d) -> p b d", b=B).unsqueeze(2).to_broadcast([P, B, 2, D])).then_inc(s["c_r"], 1)
                until(act, s["c_gap"], c + 1)
                act.activation(e2[:, :], gap[:, :], ACT.Exp).then_inc(s["c_e2"], 1)

            act.wait_ge(s["n_h"], NT)
            for q in range(2):
                route(q, q, 0)
            with act.Fori(1, NC // 2) as k:
                for q in range(2):
                    route(2 * k + q, q, k)

            def expert(t, u):
                e = expert_of(act, t)
                until(act, s["f_m1"], t + 1)
                until(act, s["f_m2"], t - 1)
                for k in range(4):
                    act.activation(hT[:, u % 2, k, :], S[u % 2][:, k * P:(k + 1) * P], ACT.Gelu,
                                   bias=b1T[:, bass.ds(e * 4 + k, 1)]).then_inc(s["f_h"], 1)

            act.wait_ge(s["meta"], 2)
            for u in range(RING):
                expert(u, u)
            with act.Fori(1, FT // RING) as k:
                for u in range(RING):
                    expert(k * RING + u, u)
            for c in range(NC):
                act.wait_ge(s["o_x"], c + 1)
                act.dma_start(out[:, c * P:(c + 1) * P, :].rearrange("b p d -> p b d"),
                              x_all[:, 4 * c:4 * c + 4, :]).then_inc(s["b_out"], 16)

        @block.gpsimd
        def _(pool):
            pool.memset(half[:, :], -0.5).then_inc(s["half_ok"], 1)
            pool.memset(kp[0:1, :, :], 0.0).then_inc(s["kpz"], 1)
            pool.wait_ge(s["half_ok"], 1)
            with pool.Fori(0, NC) as c:
                for v_ready, r_ready in (("a_ve", "a_rs"), ("a_ve2", "a_rs2")):
                    pool.wait_ge(s[v_ready], c + 1)
                    pool.tensor_tensor(rstd[:, :], ve[:, :], half[:, :], ALU.pow).then_inc(s[r_ready], 1)

            def front(n, b):
                until(pool, s["rk"], n + 1)
                until(pool, s["kb"], n * 16)
                pool.tensor_tensor(heads(k2[:, :]), heads(ex[:, DE:]), bcast(rk[:, 1, :], DH),
                                   ALU.mult).then_inc(s["k2"], 1)
                until(pool, s["kf"], n)
                pool.tensor_tensor(heads(k1[:, :]), heads(ex[:, DE:]), bcast(rk[:, 0, :], DH),
                                   ALU.mult).then_inc(s["k1"], 1)
            def norm_power(n):
                m = n - 2
                on = lambda k: not isinstance(k, int) or 0 <= k < NT
                lo, hi = 0 if on(m) else 1, 2 if on(m - 1) else 1
                until(pool, s["n_ve"], m + 1)
                pool.tensor_tensor(nrs[:, lo:hi], nve[:, lo:hi], half[:, lo:hi], ALU.pow).then_inc(s["n_rs"], 1)

            def norm_affine(n, b):
                m = n - 2
                on = lambda k: not isinstance(k, int) or 0 <= k < NT
                if on(m):
                    by = (b - 2) % B
                    xm = x_all[:, bass.ds(m, 1), :].rearrange("p o d -> p (o d)")
                    until(pool, s["n_yt"], m + 1)
                    pool.tensor_tensor(np_[:, 0, :], nt[:, 0, :], gaw[:, by, :], ALU.mult).then_inc(s["n_xp"], 1)
                    until(pool, s["n_xp"], 2 * m + 1)
                    pool.tensor_tensor(np_[:, 1, :], np_[:, 0, :], gab[:, by, :], ALU.add).then_inc(s["n_xp"], 1)
                if on(m - 1):
                    bx = (b - 3) % B
                    until(pool, s["n_xt"], m)
                    pool.tensor_tensor(np_[:, 2, :], nt[:, 1, :], mod[:, bx, 4 * D:5 * D], ALU.mult).then_inc(s["n_hp"], 1)
                if on(m):
                    until(pool, s["n_xp"], 2 * m + 2)
                    pool.tensor_tensor(xm, xm, np_[:, 1, :], ALU.add).then_inc(s["n_x"], 1)
                if on(m - 1):
                    until(pool, s["n_hp"], m)
                    pool.tensor_tensor(h_all[:, bass.ds((m - 1) * D, D)], np_[:, 2, :], mod[:, bx, 3 * D:4 * D],
                                       ALU.add).then_inc(s["n_h"], 1)

            def gate(n, b):
                until(pool, s["av"], n + 1)
                until(pool, s["tg"], n)
                pool.tensor_tensor(gg[:, :], av[:, :], ps_[:, b, :], ALU.mult).then_inc(s["gg"], 1)

            def step(c, b, first=False, last=False):
                n = c * 4 + b
                until(pool, s["kf"], n + 1)
                until(pool, s["u"], n)
                pool.tensor_tensor(heads(kw[:, :]), heads(kf[:, :]), bcast(cst[:, C_WK:C_WK + H], DH),
                                   ALU.mult).then_inc(s["kw"], 1)
                if not first:
                    gate(n - 1, (b - 1) % B)
                if not isinstance(n, int) or n >= 2:
                    norm_power(n)
                if not last:
                    front(n + 1, (b + 1) % B)
                if not isinstance(n, int) or n >= 2:
                    norm_affine(n, b)

            front(0, 0)
            for b in range(B):
                step(0, b, first=b == 0)
            with pool.Fori(1, NC - 1) as c:
                for b in range(B):
                    step(c, b)
            for b in range(B):
                step(NC - 1, b, last=b == 3)
            gate(NT - 1, 3)
            for n in range(NT, NT + 3):
                norm_power(n)
                norm_affine(n, n % B)

            def send(c, q):
                until(pool, s["c_di"], c + 1)
                pool.tensor_tensor(seen_p[:, 0:1], half[:, 0:1], half[:, 0:1], ALU.mult).then_inc(s["c_seen"], 1)
                for b in range(B):
                    for choice in range(2):
                        pool.indirect_dma_start(
                            X, bass.IndirectOffsetOnAxis(ap=desti[:, q, choice, b:b + 1], axis=0),
                            rows[:, q, b, choice, :], None).then_inc(s[f"c_sc{q}"], 16)

            for q in range(2):
                send(q, q)
            with pool.Fori(1, NC // 2) as k:
                for q in range(2):
                    send(2 * k + q, q)

            def scatter(t, u):
                until(pool, s["f_y"], t + 1)
                pool.tensor_tensor(seen_p[:, 1 + u:2 + u], half[:, 0:1], half[:, 0:1], ALU.mult).then_inc(s["f_seen"], 1)
                pool.indirect_dma_start(
                    Y, bass.IndirectOffsetOnAxis(ap=xt[:, u, D + 1:D + 2].bitcast(I32), axis=0),
                    ys[:, u, :], None, bounds_check=2 * NT * P - 1, oob_is_err=False).then_inc(s[f"f_sc{u}"], 16)

            for u in range(RING):
                scatter(u, u)
            with pool.Fori(1, FT // RING) as k:
                for u in range(RING):
                    scatter(k * RING + u, u)

        @block.vector
        def _(dve):
            dve.memset(vs[:, :, :, :], 1.0).then_inc(s["g1"], 1)
            dve.memset(state[:, :, :, :], 0.0).then_inc(s["g1"], 1)
            dve.wait_ge(s["w"], 16 * NW)
            dve.wait_ge(s["ce"], 1)
            dve.tensor_scalar_add(cR[:, :], cE[:, :], 1.0).then_inc(s["cr"], 1)
            dve.wait_ge(s["cr"], 1)
            dve.reciprocal(cE[:, :], cR[:, :]).then_inc(s["cr"], 1)
            dve.wait_ge(s["cr"], 2)
            dve.tensor_tensor(cS[:, :], cE[:, :], cT[:, :], ALU.mult).then_inc(s["cr"], 1)
            dve.wait_ge(s["cr"], 3)
            dve.tensor_copy(cB[:, :, :], bcast(cS[:, :], P)).then_inc(s["cb"], 1)
            dve.wait_ge(s["sigE"], 1)
            dve.tensor_scalar_add(sig[:, 0, :], hexp[:, :], 1.0).then_inc(s["sigR"], 1)
            dve.wait_ge(s["sigR"], 1)
            dve.reciprocal(sig[:, 1, :], sig[:, 0, :]).then_inc(s["sigR"], 1)
            dve.wait_ge(s["sigR"], 2)
            dve.tensor_scalar(sig[:, 0, :], sig[:, 1, :], -1.0, 1.0, ALU.mult, ALU.add).then_inc(s["sigR"], 1)
            dve.wait_ge(s["sigA"], 1)
            dve.tensor_scalar_mul(deps[:, :], deps[:, :], EPS).then_inc(s["sigR"], 1)
            dve.tensor_scalar_mul(wo_sb[:, :, :], wo_sb[:, :, :], 0.5).then_inc(s["sigR"], 1)
            for i, (lo, hi) in enumerate(((0, DE), (DE, 2 * DE), (2 * DE, 4 * DE))):
                dve.tensor_scalar_mul(wcat[:, lo:hi], wraw[:, lo:hi], cols[:, 2 * i:2 * i + 1]).then_inc(s["fold"], 1)
                dve.tensor_copy(bcol[:, i, :], cols[:, 2 * i + 1:2 * i + 2].to_broadcast([P, P])).then_inc(s["fold"], 1)
            dve.memset(bcol[:, 3, :], -1.0).then_inc(s["fold"], 1)
            dve.wait_ge(s["bp"], 1)
            dve.tensor_tensor(bqk[:, :], PA[:, :], bqk[:, :], ALU.add).then_inc(s["bc1"], 1)
            dve.wait_ge(s["bc1"], 1)
            for lo, src in ((0, bqk), (512, PV)):
                w = wcat[:, lo:lo + 512]
                dve.scalar_tensor_tensor(w, src[:, :], 1.0 / D, w, ALU.mult, ALU.add).then_inc(s["bc1"], 1)
            for b in range(B):
                dve.wait_ge(s["mp"], b + 1)
                dve.tensor_copy(mod[:, b, 0:512], S0[:, :])
                dve.tensor_copy(mod[:, b, 512:], S1[:, 0:256]).then_inc(s["mc"], 1)
            dve.wait_ge(s["mc"], B)
            for i in (1, 4):
                m = mod[:, :, i * D:(i + 1) * D]
                dve.tensor_scalar_add(m, m, 1.0).then_inc(s["mc"], 1)
            for i, tmp in ((2, ya), (5, yb)):
                m = mod[:, :, i * D:(i + 1) * D]
                dve.tensor_scalar(tmp[:, :, :], m, 0.0, 2.0, ALU.is_ge, ALU.mult).then_inc(s["mc"], 1)
            dve.wait_ge(s["mc"], B + 4)
            for i, tmp in ((2, zt), (5, sq)):
                m = mod[:, :, i * D:(i + 1) * D]
                dve.scalar_tensor_tensor(tmp[:, :, :], m, -1.0, m, ALU.mult, ALU.max).then_inc(s["mc"], 1)
            dve.wait_ge(s["mc"], B + 6)
            for i, tmp in ((2, zt), (5, sq)):
                dve.tensor_scalar_max(tmp[:, :, :], tmp[:, :, :], 0.25).then_inc(s["mc"], 1)
            dve.wait_ge(s["mc"], B + 8)
            for i, sign, size in ((2, ya, zt), (5, yb, sq)):
                dve.scalar_tensor_tensor(mod[:, :, i * D:(i + 1) * D], sign[:, :, :], -1.0, size[:, :, :],
                                         ALU.add, ALU.mult).then_inc(s["mc"], 1)
            dve.wait_ge(s["mc"], B + 10)
            for i, dst in enumerate((gaw, gab)):
                dve.tensor_tensor(dst[:, :, :], mod[:, :, 2 * D:3 * D],
                                  ow_bc[:, i, :].unsqueeze(1).to_broadcast([P, B, D]), ALU.mult).then_inc(s["mc"], 1)
            dve.wait_ge(s["mc"], B + 12)

            with dve.Fori(0, NC) as c:
                dve.wait_ge(s["x_in"], 16 * NC)
                for b in range(B):
                    dve.bn_stats(st[:, b, :], x_all[:, bass.ds(c * 4 + b, 1), :]).then_inc(s["a_st"], 1)
                dve.wait_ge(s["a_st"], c * 4 + 4)
                dve.tensor_copy(seen[:, 0:1], st[:, 3, 0:1])
                for b in range(B):
                    dve.bn_aggr(mv[:, b, :], st[:, b, :]).then_inc(s["a_mv"], 1)
                dve.wait_ge(s["a_mv"], c * 4 + 4)
                dve.tensor_scalar_add(ve[:, :], mv[:, :, 1], EPS).then_inc(s["a_ve"], 1)
                dve.wait_ge(s["a_rs"], c + 1)
                for b in range(B):
                    dve.tensor_scalar(ya[:, b, :], x_all[:, bass.ds(c * 4 + b, 1), :].rearrange("p o d -> p (o d)"),
                                      mv[:, b, 0:1], rstd[:, b:b + 1], ALU.subtract, ALU.mult).then_inc(s["a_y"], 1)
                dve.wait_ge(s["a_y"], c * 4 + 4)
                dve.tensor_tensor(yb[:, :, :], ya[:, :, :], mod[:, :, D:2 * D], ALU.mult).then_inc(s["a_m"], 1)
                dve.wait_ge(s["a_m"], 2 * c + 1)
                dve.tensor_tensor(ya[:, :, :], yb[:, :, :], mod[:, :, 0:D], ALU.add).then_inc(s["a_m"], 1)
                dve.wait_ge(s["a_m"], 2 * c + 2)
                for b in range(B):
                    dve.bn_stats(st[:, b, :], ya[:, b, :]).then_inc(s["a_st2"], 1)
                dve.wait_ge(s["a_st2"], c * 4 + 4)
                dve.tensor_copy(seen[:, 0:1], st[:, 3, 0:1])
                for b in range(B):
                    dve.bn_aggr(mv[:, b, :], st[:, b, :]).then_inc(s["a_mv2"], 1)
                dve.wait_ge(s["a_mv2"], c * 4 + 4)
                dve.tensor_scalar_add(ve[:, :], mv[:, :, 1], EPS).then_inc(s["a_ve2"], 1)
                dve.wait_ge(s["a_rs2"], c + 1)
                until(dve, s["a_zT"], c)
                for b in range(B):
                    dve.tensor_scalar(zt[:, b, :], ya[:, b, :], mv[:, b, 0:1], rstd[:, b:b + 1],
                                      ALU.subtract, ALU.mult).then_inc(s["a_z"], 1)

            def front1(n, b):
                until(dve, s["pqk"], n + 1)
                dve.tensor_reduce(mx[:, :], heads(PA[:, :]), AX.X, ALU.max).then_inc(s["mx"], 1)
                until(dve, s["mx"], n + 1)
                until(dve, s["e"], n)
                dve.tensor_tensor(heads(qk[:, :]), heads(PA[:, :]), bcast(mx[:, :], DH), ALU.subtract).then_inc(s["d"], 1)

            def front2(n, b):
                until(dve, s["e"], n + 1)
                dve.tensor_reduce(sm[:, b % 2, :], heads(ex[:, :]), AX.X, ALU.add).then_inc(s["sum"], 1)
                until(dve, s["sum"], n + 1)
                dve.reciprocal(rs[:, :], sm[:, b % 2, H:]).then_inc(s["r"], 1)
                until(dve, s["r"], n + 1)
                until(dve, s["k1"], n)
                dve.tensor_tensor(rk[:, :, :], sig[:, :, :], rs[:, :].unsqueeze(1).to_broadcast([P, 2, H]),
                                  ALU.mult).then_inc(s["rk"], 1)
                until(dve, s["vp"], 2 * n + 2)
                dve.scalar_tensor_tensor(ps_[:, b, :], ep[:, b, :], 1.0, ps_[:, b, :], ALU.add, ALU.mult).then_inc(s["sp"], 1)
                until(dve, s["dn"], 2 * (n - 1))
                dve.tensor_tensor(epsq[:, b % 2, :], deps[:, :], sm[:, b % 2, 0:H], ALU.mult).then_inc(s["eq"], 1)

            def front3(n, b):
                until(dve, s["k1"], n + 1)
                until(dve, s["ka"], n * 32 + 32)
                until(dve, s["kb"], n * 16 - 48)
                if isinstance(n, int) and n == 0:
                    dve.wait_ge(s["kpz"], 1)
                until(dve, s["kw"], n)
                until(dve, s["tk"], n)
                dve.tensor_tensor(kf[:, :], k1[:, :], kp[:, b, :], ALU.add).then_inc(s["kf"], 1)

            def back(n, b):
                until(dve, s["g"], n + 1)
                until(dve, s["eq"], n + 1)
                G = M[:, :].rearrange("p (h w) -> p h w", w=32)
                dve.tensor_tensor(den[:, 0, :], G[:, :, DH], epsq[:, b % 2, :], ALU.add).then_inc(s["dn"], 1)
                until(dve, s["dn"], 2 * n + 1)
                dve.reciprocal(den[:, 1, :], den[:, 0, :]).then_inc(s["dn"], 1)
                until(dve, s["dn"], 2 * n + 2)
                until(dve, s["gg"], n)
                until(dve, s["sp"], n + 1)
                dve.tensor_tensor(heads(av[:, :]), G[:, :, 0:DH], bcast(den[:, 1, :], DH), ALU.mult).then_inc(s["av"], 1)

            def queries(n, b):
                until(dve, s["qT"], n + 1)
                until(dve, s["o"], n - 1)
                dve.tensor_tensor(qw[:, b % 2, :, :].rearrange("p a i -> p (a i)"), qT[:, :], cst[:, C_WQ:C_WQ + 2 * P],
                                  ALU.mult).then_inc(s["qw"], 1)

            def masked(n, j):
                until(dve, s["sc"], n * 4 + j + 1)
                until(dve, s["o"], n)
                mask = cst[:, C_MASK + 4 * j * P:C_MASK + 4 * (j + 1) * P].rearrange("p (h i) -> p h i", i=P)
                dve.tensor_tensor(Pm[:, 4 * j:4 * j + 4, :], S[j % 2][:, :].rearrange("p (h i) -> p h i", i=P), mask,
                                  ALU.mult).then_inc(s["pm"], 1)

            def step(c, b, first=False, last=False):
                n = c * 4 + b
                nxt = (b + 1) % B
                if not last:
                    front1(n + 1, nxt)
                if not first:
                    back(n - 1, (b - 1) % B)
                masked(n, 0)
                if not isinstance(n, int) or n >= 2:
                    statistics(n, b)
                masked(n, 1)
                if not last:
                    front2(n + 1, nxt)
                if not isinstance(n, int) or n >= 2:
                    normalise(n, b)
                masked(n, 2)
                masked(n, 3)
                if not last:
                    queries(n + 1, nxt)
                    front3(n + 1, nxt)
                until(dve, s["u"], n + 1)
                dve.tensor_tensor(own_kv[:, :, :], M[:, 0:2 * HV].rearrange("p (h w) -> p h w", w=VW),
                                  cst[:, C_BM:C_BM + 2 * HV].rearrange("p (h w) -> p h w", w=VW),
                                  ALU.mult).then_inc(s["s1"], 1)
                until(dve, s["s1"], n + 1)
                until(dve, s["o"], n + 1)
                for half_ in range(2):
                    own = state[:, b, 8 * half_:8 * half_ + 8, 0:VW]
                    dve.scalar_tensor_tensor(own, own, cst[:, C_LAM + half_:C_LAM + half_ + 1],
                                             own_kv[:, 8 * half_:8 * half_ + 8, :], ALU.mult, ALU.add).then_inc(s["st"], 1)

            def statistics(n, b):
                m = n - 2
                y_on = not isinstance(n, int) or 0 <= m < NT
                x_on = not isinstance(n, int) or 0 <= m - 1 < NT
                if y_on:
                    until(dve, s["yc"], m + 1)
                    dve.tensor_copy(seen[:, 0:1], cst[:, 0:1])
                    dve.bn_stats(nst[:, 0, :], y_all[:, bass.ds(m, 1), :]).then_inc(s["n_yst"], 1)
                if x_on:
                    until(dve, s["n_x"], m)
                    dve.tensor_copy(seen[:, 1:2], cst[:, 0:1])
                    dve.bn_stats(nst[:, 1, :], x_all[:, bass.ds(m - 1, 1), :]).then_inc(s["n_xst"], 1)
                if y_on:
                    until(dve, s["n_yst"], m + 1)
                    dve.tensor_copy(seen[:, 2:3], cst[:, 0:1])
                    dve.bn_aggr(nmv[:, 0, :], nst[:, 0, :]).then_inc(s["n_ymv"], 1)
                    until(dve, s["n_ymv"], m + 1)
                if x_on:
                    until(dve, s["n_xst"], m)
                    dve.tensor_copy(seen[:, 3:4], cst[:, 0:1])
                    dve.bn_aggr(nmv[:, 1, :], nst[:, 1, :]).then_inc(s["n_xmv"], 1)
                    until(dve, s["n_xmv"], m)
                lo, hi = 0 if y_on else 1, 2 if x_on else 1
                dve.tensor_scalar_add(nve[:, lo:hi], nmv[:, lo:hi, 1], EPS).then_inc(s["n_ve"], 1)

            def normalise(n, b):
                m = n - 2
                until(dve, s["n_rs"], m + 1)
                if not isinstance(n, int) or 0 <= m < NT:
                    until(dve, s["n_x"], m)
                    dve.tensor_scalar(nt[:, 0, :], y_all[:, bass.ds(m, 1), :].rearrange("p o d -> p (o d)"),
                                      nmv[:, 0, 0:1], nrs[:, 0:1], ALU.subtract, ALU.mult).then_inc(s["n_yt"], 1)
                if not isinstance(n, int) or 0 <= m - 1 < NT:
                    until(dve, s["n_h"], m - 1)
                    dve.tensor_scalar(nt[:, 1, :], x_all[:, bass.ds(m - 1, 1), :].rearrange("p o d -> p (o d)"),
                                      nmv[:, 1, 0:1], nrs[:, 1:2], ALU.subtract, ALU.mult).then_inc(s["n_xt"], 1)

            dve.memset(pad[:, 0:D + 1], 0.0).then_inc(s["init"], 1)
            dve.tensor_copy(pad[:, D + 1:].bitcast(I32), cst[:, C_PAD:C_PAD + 1]).then_inc(s["init"], 1)
            dve.memset(pad_i[:, :], E * REGION).then_inc(s["init"], 1)
            dve.memset(count[:, :], 0.0).then_inc(s["init"], 1)
            dve.tensor_copy(ids[:, :, :].rearrange("p b c -> p (b c)"), cst[:, C_ROW:C_ROW + 2 * B]).then_inc(s["init"], 1)
            dve.tensor_copy(tri[:, :], cst[:, C_TRI:C_TRI + P]).then_inc(s["init"], 1)
            dve.tensor_copy(one[:, :], cst[:, C_ONE:C_ONE + P]).then_inc(s["init"], 1)
            dve.wait_ge(s["init"], 7)
            dve.wait_ge(s["g1"], 2)
            front1(0, 0)
            front2(0, 0)
            queries(0, 0)
            front3(0, 0)
            for b in range(B):
                step(0, b, first=b == 0)
            with dve.Fori(1, NC - 1) as c:
                for b in range(B):
                    step(c, b)
            for b in range(B):
                step(NC - 1, b, last=b == 3)
            back(NT - 1, 3)

            for n in range(NT, NT + 3):
                statistics(n, n % B)
                normalise(n, n % B)

            def route(c, q, turn):
                until(dve, s["c_lg"], c + 1)
                dve.tensor_copy(lg[:, :, :].rearrange("p b e -> p (b e)"), S[q][:, 0:B * E]).then_inc(s["c_l"], 1)
                until(dve, s["c_l"], c + 1)
                dve.tensor_copy(seen[:, 0:1], lg[:, 0, 0:1])
                for b in range(B):
                    dve.max(m8[:, b, :], lg[:, b, :]).then_inc(s["c_m8"], 1)
                until(dve, s["c_m8"], c * 4 + 4)
                dve.tensor_tensor(gap[:, :], m8[:, :, 1], m8[:, :, 0], ALU.subtract).then_inc(s["c_gap"], 1)
                for b in range(B):
                    dve.max_index(i8[:, b, :], m8[:, b, :], lg[:, b, :]).then_inc(s["c_i8"], 1)
                until(dve, s["c_i8"], c * 4 + 4)
                dve.tensor_copy(i8f[:, :, :], i8[:, :, 0:2]).then_inc(s["c_if"], 1)
                until(dve, s["c_if"], c + 1)
                iota = cst[:, C_IOTA:C_IOTA + E].unsqueeze(1).to_broadcast([P, B, E])
                for choice in range(2):
                    dve.tensor_tensor(pick[:, choice, :, :], iota, bcast(i8f[:, :, choice], E),
                                      ALU.is_equal).then_inc(s["c_pk"], 1)
                until(dve, s["c_pk"], 2 * c + 2)
                dve.tensor_tensor(used[:, :].rearrange("p (b e) -> p b e", e=E), pick[:, 0, :, :], pick[:, 1, :, :],
                                  ALU.add).then_inc(s["c_us"], 1)
                until(dve, s["c_e2"], c + 1)
                dve.tensor_scalar_add(e3[:, :], e2[:, :], 1.0).then_inc(s["c_w"], 1)
                until(dve, s["c_w"], 3 * c + 1)
                until(dve, s[f"c_sc{q}"], 16 * 2 * B * turn)
                dve.reciprocal(rows[:, q, :, 0, D], e3[:, :]).then_inc(s["c_w"], 1)
                until(dve, s["c_w"], 3 * c + 2)
                dve.tensor_tensor(rows[:, q, :, 1, D], rows[:, q, :, 0, D], e2[:, :], ALU.mult).then_inc(s["c_w"], 1)
                dve.tensor_copy(rows[:, q, :, :, D + 1].bitcast(I32), ids[:, :, :]).then_inc(s["c_id"], 1)
                until(dve, s["c_id"], c + 1)
                dve.tensor_scalar_add(ids[:, :, :], ids[:, :, :], float(B * P)).then_inc(s["c_idn"], 1)
                until(dve, s["c_ps"], c + 1)
                places = (TD, O)[q]
                dve.tensor_tensor(posb[:, :, :], places[:, 0:B * E].rearrange("p (b e) -> p b e", e=E),
                                  count[:, :].unsqueeze(1).to_broadcast([P, B, E]), ALU.add).then_inc(s["c_pl"], 1)
                until(dve, s["c_pl"], 5 * c + 1)
                dve.tensor_tensor(count[:, :], count[:, :], places[:, B * E:(B + 1) * E], ALU.add).then_inc(s["c_cnt"], 1)
                dve.tensor_tensor(posr[:, :, :], posb[:, :, :],
                                  cst[:, C_REG:C_REG + E].unsqueeze(1).to_broadcast([P, B, E]), ALU.add).then_inc(s["c_pl"], 1)
                until(dve, s["c_pl"], 5 * c + 2)
                for choice in range(2):
                    dve.tensor_tensor(prod[:, choice, :, :], pick[:, choice, :, :], posr[:, :, :],
                                      ALU.mult).then_inc(s["c_pl"], 1)
                until(dve, s["c_pl"], 5 * c + 4)
                dve.tensor_reduce(dest[:, :, :], prod[:, :, :, :], AX.X, ALU.add).then_inc(s["c_pl"], 1)
                until(dve, s["c_pl"], 5 * c + 5)
                until(dve, s["c_w"], 3 * c + 3)
                until(dve, s["c_seen"], c)
                until(dve, s["c_r"], c + 1)
                dve.tensor_copy(desti[:, q, :, :], dest[:, :, :]).then_inc(s["c_di"], 1)

            for q in range(2):
                route(q, q, 0)
            with dve.Fori(1, NC // 2) as k:
                for q in range(2):
                    route(2 * k + q, q, k)

            dve.wait_ge(s["c_cnt"], NC)
            dve.tensor_scalar_add(cnt1[:, :], count[:, :], float(P - 1)).then_inc(s["tile"], 1)
            dve.tensor_tensor(pad_f[:, :], count[0:1, :], cst[0:1, C_REG:C_REG + E], ALU.add).then_inc(s["tile"], 1)
            dve.wait_ge(s["tile"], 2)
            dve.tensor_copy(pad_i[:, 0:E], pad_f[:, :]).then_inc(s["meta"], 1)
            dve.tensor_copy(cnti[:, :], cnt1[:, :]).then_inc(s["tile"], 1)
            dve.wait_ge(s["tile"], 3)
            dve.tensor_single_scalar(cnti[:, :], cnti[:, :], 7, op=ALU.logical_shift_right).then_inc(s["tile"], 1)
            dve.wait_ge(s["tile"], 4)
            dve.tensor_copy(nts[:, :], cnti[:, :]).then_inc(s["tile"], 1)
            dve.wait_ge(s["tile"], 5)
            src = nts[:, :]
            for i, d in enumerate((1, 2, 4)):
                dve.tensor_copy(cum[:, i, 0:d], src[:, 0:d]).then_inc(s["tile"], 1)
                dve.tensor_tensor(cum[:, i, d:], src[:, d:], src[:, 0:E - d], ALU.add).then_inc(s["tile"], 1)
                dve.wait_ge(s["tile"], 2 * i + 7)
                src = cum[:, i, :]
            tau = cst[0:1, C_TAU:C_TAU + FT]
            dve.tensor_tensor(ge[:, :, :], bcast(tau, E), cum[0:1, 2, :].unsqueeze(1).to_broadcast([1, FT, E]),
                              ALU.is_ge).then_inc(s["tile"], 1)
            dve.wait_ge(s["tile"], 12)
            dve.tensor_tensor(gn[:, :, :], ge[:, :, :], nts[0:1, :].unsqueeze(1).to_broadcast([1, FT, E]),
                              ALU.mult).then_inc(s["tile"], 1)
            dve.tensor_reduce(meta[:, 0, :], ge[:, :, :], AX.X, ALU.add).then_inc(s["tile"], 1)
            dve.wait_ge(s["tile"], 14)
            dve.tensor_reduce(meta[:, 1, :], gn[:, :, :], AX.X, ALU.add).then_inc(s["tile"], 1)
            dve.tensor_scalar(meta[:, 2, :], meta[:, 0, :], float(E), None, ALU.is_lt).then_inc(s["tile"], 1)
            dve.wait_ge(s["tile"], 16)
            dve.tensor_tensor(meta[:, 3, :], tau, meta[:, 1, :], ALU.subtract).then_inc(s["tile"], 1)
            dve.wait_ge(s["tile"], 17)
            dve.tensor_tensor(meta[:, 4, :], meta[:, 3, :], meta[:, 2, :], ALU.mult).then_inc(s["tile"], 1)
            dve.tensor_scalar(meta[:, 1, :], meta[:, 0, :], float(REGION), None, ALU.mult).then_inc(s["tile"], 1)
            dve.wait_ge(s["tile"], 19)
            dve.scalar_tensor_tensor(meta[:, 3, :], meta[:, 4, :], float(P), meta[:, 1, :], ALU.mult,
                                     ALU.add).then_inc(s["tile"], 1)
            dve.tensor_scalar_min(meta_i[:, 1, :], meta[:, 0, :], float(E - 1)).then_inc(s["tile"], 1)
            dve.wait_ge(s["tile"], 21)
            dve.tensor_copy(meta_i[:, 0, :], meta[:, 3, :]).then_inc(s["meta"], 1)
            dve.wait_ge(s["meta"], 2)

            def stage(t, u):
                e = expert_of(dve, t)
                until(dve, s["f_m1"], t - 3)
                dve.tensor_copy(w1s[:, u % 4, :], w1T[:, bass.ds(e * HID, HID)]).then_inc(s["f_ws"], 1)
                until(dve, s["f_xp"], t + 1)
                dve.tensor_copy(xT[:, u % 4, :], (TA, TD)[u % 2][:, 0:P]).then_inc(s["f_xT"], 1)

            def gated(t, u, turn):
                until(dve, s["f_m2"], t + 1)
                until(dve, s["f_seen"], t - RING + 1)
                until(dve, s[f"f_sc{u}"], 16 * turn)
                dve.tensor_scalar_mul(ys[:, u, :], (O, M)[u % 2][:, 0:D], xt[:, u, D:D + 1]).then_inc(s["f_y"], 1)

            def expert(t, u, turn, ahead):
                if ahead > 3:
                    stage(t + 3, u + 3)
                gated(t, u, turn)

            stage(0, 0)
            stage(1, 1)
            stage(2, 2)
            for u in range(RING):
                expert(u, u, 0, RING)
            with dve.Fori(1, FT // RING - 1) as k:
                for u in range(RING):
                    expert(k * RING + u, u, k, RING)
            for u in range(RING):
                expert(FT - RING + u, u, FT // RING - 1, RING - u)

            for c in range(NC):
                dve.wait_ge(s[f"o_ld{c % 4}"], 32 * (c // 4 + 1))
                y0 = 8 * (c % 4)
                dve.tensor_tensor(ya[:, :, :], y_all[:, y0:y0 + 4, :], y_all[:, y0 + 4:y0 + 8, :], ALU.add).then_inc(s["o_s"], 1)
                dve.wait_ge(s["o_s"], c + 1)
                dve.tensor_tensor(yb[:, :, :], ya[:, :, :], mod[:, :, 5 * D:], ALU.mult).then_inc(s["o_g"], 1)
                dve.wait_ge(s["o_g"], c + 1)
                xc = x_all[:, 4 * c:4 * c + 4, :]
                dve.tensor_tensor(xc, xc, yb[:, :, :], ALU.add).then_inc(s["o_x"], 1)

        @block.tensor
        def _(pe):
            pe.wait_ge(s["fold"], 7)
            pe.wait_ge(s["w"], 16 * NW)
            for bank, lo, hi, i, at in ((PA, 0, DE, 0, 0), (PA, DE, 2 * DE, 1, DE), (PV, 2 * DE, 4 * DE, 2, 0)):
                dst = bank[:, at:at + hi - lo]
                pe.matmul(dst, bcol[:, i, :], wraw[:, lo:hi], start=True, stop=False)
                ins = pe.matmul(dst, bcol[:, 3, :], wcat[:, lo:hi], start=False, stop=True)
            ins.then_inc(s["bp"], 1)
            pe.wait_ge(s["cb"], 1)
            for b in range(B):
                until(pe, s["mc"], b)
                pe.matmul(S0[:, :], cB[:, b, :], wmod_sb[:, 0:512], start=True, stop=True)
                pe.matmul(S1[:, 0:256], cB[:, b, :], wmod_sb[:, 512:], start=True, stop=True).then_inc(s["mp"], 1)
            with pe.Fori(0, NC) as c:
                pe.wait_ge(s["a_z"], c * 4 + 4)
                until(pe, s["a_za"], c)
                for b in range(B):
                    last_ = pe.transpose(TA[:, b * P:(b + 1) * P], zt[:, b, :], ident)
                last_.then_inc(s["a_zT"], 1)

            def front_qk(n, b):
                until(pe, s["d"], n)
                pe.matmul(PA[:, :], zs[:, b * P:(b + 1) * P], wcat[:, 0:512], start=True, stop=True).then_inc(s["pqk"], 1)

            def front_vp(n, b):
                until(pe, s["vp"], 2 * n)
                pe.matmul(PV[:, :], zs[:, b * P:(b + 1) * P], wcat[:, 512:], start=True, stop=True).then_inc(s["pvp"], 1)

            def queries(n):
                until(pe, s["e"], n + 1)
                until(pe, s["qT"], n)
                for i in range(2):
                    ins = pe.transpose(TD[:, i * P:(i + 1) * P], ex[:, i * P:(i + 1) * P], ident)
                ins.then_inc(s["tq"], 1)

            def scores(n, b, j):
                until(pe, s["pm"], n * 4 + j - 1)
                r = 32 * j
                for half_ in range(2):
                    ins = pe.matmul(S[j % 2][:, half_ * 256:(half_ + 1) * 256], kT[r:r + 32, half_, :],
                                    qeo[r:r + 32, b % 2, half_, :, :], start=True, stop=True)
                ins.then_inc(s["sc"], 1)

            def values(n, b, j):
                until(pe, s["pm"], n * 4 + 2 * (j % 2) + 2)
                if j == 0:
                    until(pe, s["qw"], n + 1)
                    until(pe, s["oc"], n)
                    if isinstance(n, int):
                        until(pe, s["we"], 2 * n if n <= 4 else 8 + 2 * max(n - NT + 4, 0))
                    until(pe, s["st"], 2 * (n - 3))
                    until(pe, s["vv"], n + 1)
                half_ = j // 2
                lhsT = state[:, b, 4 * j:4 * j + 4, :].rearrange("p h w -> p (h w)")
                oj = O[:, j * P:(j + 1) * P]
                pe.matmul(oj, lhsT, qw[:, b % 2, half_, :], start=True, stop=False, skip_group_check=True)
                for i in range(4):
                    h = 4 * j + i
                    ins = pe.matmul(oj[32 * i:32 * i + VW, :], vs[:, b % 2, h, :], Pm[:, slot(h), :],
                                    start=False, stop=True, tile_position=(0, 32 * i), skip_group_check=True)
                if j == 3:
                    ins.then_inc(s["o"], 1)

            def g_back(n):
                until(pe, s["oc"], n + 1)
                until(pe, s["s1"], n + 1)
                until(pe, s["av"], n)
                for j in range(4):
                    ins = pe.transpose(M[:, j * P:(j + 1) * P], oT[:, j, :], ident)
                ins.then_inc(s["g"], 1)

            def t_gate(n):
                until(pe, s["gg"], n + 1)
                until(pe, s["kt"], n + 2)
                until(pe, s["yc"], n)
                for i in range(2):
                    ins = pe.transpose(TA[:, i * P:(i + 1) * P], gg[:, i * P:(i + 1) * P], ident)
                ins.then_inc(s["tg"], 1)

            def out_proj(n):
                until(pe, s["gt"], n + 1)
                for i in range(2):
                    ins = pe.matmul(TA[:, 256:256 + D], gT[:, i, :], wo_sb[:, i, :], start=i == 0, stop=i == 1)
                ins.then_inc(s["y"], 1)

            def step(c, b, first=False, last=False):
                n = c * 4 + b
                nxt = (b + 1) % B
                until(pe, s["kf"], n + 1)
                until(pe, s["yc"], n - 1)
                for i in range(2):
                    ins = pe.transpose(TA[:, i * P:(i + 1) * P], kf[:, i * P:(i + 1) * P], ident)
                ins.then_inc(s["tk"], 1)
                if not last:
                    if b == 3:
                        until(pe, s["zs"], c + 2)
                    front_qk(n + 1, nxt)
                if not first:
                    g_back(n - 1)
                if not last:
                    front_vp(n + 1, nxt)
                until(pe, s["qt"], n * 4 + 4)
                until(pe, s["kt"], n + 1)
                scores(n, b, 0)
                scores(n, b, 1)
                scores(n, b, 2)
                if not first:
                    t_gate(n - 1)
                values(n, b, 0)
                scores(n, b, 3)
                values(n, b, 2)
                if not last:
                    queries(n + 1)
                values(n, b, 1)
                if not first:
                    out_proj(n - 1)
                values(n, b, 3)
                until(pe, s["kw"], n + 1)
                until(pe, s["av"], n)
                for i in range(2):
                    ins = pe.matmul(M[:, i * HV:(i + 1) * HV], kw[:, i * P:(i + 1) * P],
                                    vs[:, b % 2, 8 * i:8 * i + 8, :], start=True, stop=True)
                ins.then_inc(s["u"], 1)
                if isinstance(c, int):
                    e = b if c == 0 else 4 + b
                    pe.wait_ge(s["ww"], 16 * 2 * E)
                    pe.wait_ge(s["oc"], n + 1)
                    for i in range(2):
                        until(pe, s["we"], 2 * e + i)
                        for k in range(4):
                            src = w1n[:, e, k, :] if i == 0 else w2n[:, e, k * P:(k + 1) * P]
                            ins = pe.transpose(O[:, k * P:(k + 1) * P], src, ident)
                        ins.then_inc(s["wt"], 1)

            pe.wait_ge(s["bc1"], 3)
            pe.wait_ge(s["zs"], 1)
            front_qk(0, 0)
            front_vp(0, 0)
            queries(0)
            for b in range(B):
                step(0, b, first=b == 0)
            with pe.Fori(1, NC - 1) as c:
                for b in range(B):
                    step(c, b)
            for b in range(B):
                step(NC - 1, b, last=b == 3)
            g_back(NT - 1)
            pe.wait_ge(s["gg"], NT)
            pe.wait_ge(s["yc"], NT - 1)
            for i in range(2):
                ins = pe.transpose(TA[:, i * P:(i + 1) * P], gg[:, i * P:(i + 1) * P], ident)
            ins.then_inc(s["tg"], 1)
            out_proj(NT - 1)

            pe.wait_ge(s["wg"], 32)
            pe.wait_ge(s["qT"], NT)
            pe.transpose(TD[:, 0:E], wgn[:, :], ident[0:E, 0:E])
            pe.transpose(TD[:, E:E + 4 * E], b1n[:, :], ident[0:4 * E, 0:4 * E]).then_inc(s["wgt"], 1)
            pe.wait_ge(s["wgt"], 3)
            pe.wait_ge(s["yc"], NT)
            pe.wait_ge(s["init"], 7)
            def h_transposes(c, q):
                until(pe, s["c_z"], c + 1)
                until(pe, s["c_hs"], c - 1)
                for b in range(B):
                    ins = pe.transpose((TA, PA)[q][:, b * P:(b + 1) * P], hs[:, b * P:(b + 1) * P], ident)
                ins.then_inc(s["c_hT"], 1)

            def route(c, q, last=False):
                until(pe, s["c_hs"], c + 1)
                until(pe, s["c_l"], c - 1)
                for b in range(B):
                    ins = pe.matmul(S[q][:, b * E:(b + 1) * E], hTs[:, q, b * P:(b + 1) * P], wgT[:, :], start=True, stop=True)
                ins.then_inc(s["c_lg"], 1)
                if not last:
                    h_transposes(c + 1, 1 - q)
                until(pe, s["c_us"], c + 1)
                until(pe, s["c_cnt"], c - 1)
                for b in range(B + 1):
                    for a in range(min(b + 1, B)):
                        ins = pe.matmul((TD, O)[q][:, b * E:(b + 1) * E], (tri if a == b else one)[:, :],
                                        used[:, a * E:(a + 1) * E], start=a == 0, stop=a == min(b, B - 1))
                ins.then_inc(s["c_ps"], 1)

            h_transposes(0, 0)
            for q in range(2):
                route(q, q)
            with pe.Fori(1, NC // 2 - 1) as k:
                for q in range(2):
                    route(2 * k + q, q)
            for q in range(2):
                route(NC - 2 + q, q, last=q == 1)

            def x_transpose(t, u, turn):
                until(pe, s[f"f_xt{u}"], 16 * turn + 16)
                until(pe, s["f_xT"], t - 1)
                pe.transpose((TA, TD)[u % 2][:, 0:P], xt[:, u, 0:D], ident).then_inc(s["f_xp"], 1)

            def up(t, u):
                until(pe, s["f_xT"], t + 1)
                until(pe, s["f_ws"], t + 1)
                until(pe, s["f_h"], 4 * (t - 1))
                for k in range(4):
                    ins = pe.matmul(S[u % 2][:, k * P:(k + 1) * P], w1s[:, u % 4, k * P:(k + 1) * P], xT[:, u % 4, :],
                                    start=True, stop=True)
                ins.then_inc(s["f_m1"], 1)

            def down(t, u):
                e = expert_of(pe, t)
                until(pe, s["f_h"], 4 * (t + 1))
                until(pe, s["f_y"], t - 1)
                y = (O, M)[u % 2][:, 0:D]
                pe.matmul(y, cst[0:1, C_ONE:C_ONE + P], b2_row[0:1, bass.ds(e * D, D)], start=True, stop=False)
                for k in range(4):
                    ins = pe.matmul(y, hT[:, u % 2, k, :], w2T[:, bass.ds(e * HID + k * P, P)], start=False, stop=k == 3)
                ins.then_inc(s["f_m2"], 1)

            def expert(t, u, turn, ahead):
                if ahead > 3:
                    x_transpose(t + 3, (u + 3) % RING, turn + (u + 3 >= RING))
                if ahead > 1:
                    up(t + 1, u + 1)
                down(t, u)

            pe.wait_ge(s["meta"], 2)
            pe.wait_ge(s["wb"], 16)
            pe.wait_ge(s["we"], 2 * E)
            x_transpose(0, 0, 0)
            x_transpose(1, 1, 0)
            x_transpose(2, 2, 0)
            up(0, 0)
            for u in range(RING):
                expert(u, u, 0, RING)
            with pe.Fori(1, FT // RING - 1) as k:
                for u in range(RING):
                    expert(k * RING + u, u, k, RING)
            for u in range(RING):
                expert(FT - RING + u, u, FT // RING - 1, RING - u)


NW = 19
_INS = ["L0_attn_x", "L0_attn_in_ln_w", "L0_attn_in_ln_b", "L0_attn_q_ln_w", "L0_attn_q_ln_b", "L0_attn_k_ln_w",
        "L0_attn_k_ln_b", "L0_attn_out_ln_w", "L0_attn_out_ln_b", "L0_attn_W_in", "L0_attn_W_out", "L0_attn_Wq",
        "L0_attn_bq", "L0_attn_Wk", "L0_attn_bk", "L0_attn_smear_factor", "L0_attn_log_scale", "L0_ffn_Wg",
        "L0_ffn_W1", "L0_ffn_b1", "L0_ffn_W2", "L0_ffn_b2", "L0_c", "L0_wmod"]


def kernel(**inputs):
    import numpy as _np
    import concourse.bacc as _bacc
    from concourse import mybir as _mybir
    from concourse.bass_utils import run_bass_kernel_spmd as _run

    nc = _bacc.Bacc("TRN2", target_bir_lowering=False, num_devices=1)
    arrays, args = {}, []
    for name in _INS:
        a = _np.ascontiguousarray(inputs[name])
        arrays[f"in_{name}_dram"] = a
        args.append(nc.dram_tensor(f"in_{name}_dram", a.shape, _mybir.dt.from_np(a.dtype), kind="ExternalInput").ap())
    k = shape_constants()
    arrays["consts_dram"] = k
    args.append(nc.dram_tensor("consts_dram", k.shape, F32, kind="ExternalInput").ap())
    out = nc.dram_tensor("out_0_dram", (B, L, D), F32, kind="ExternalOutput").ap()
    build(nc, *args, out)
    r = _run(nc, [arrays], core_ids=[0])
    return r.results[0]["out_0_dram"]
```

```python
from contextlib import ExitStack

import numpy as np

import concourse.bass as bass
from concourse import mybir

F32 = mybir.dt.float32
BF16 = mybir.dt.bfloat16
I32 = mybir.dt.int32
U32 = mybir.dt.uint32
ALU = mybir.AluOpType
ACT = mybir.ActivationFunctionType
AX = mybir.AxisListType

B, L, D = 4, 1024, 128
P = 128
NC = L // P
NT = B * NC
DE = 256
H = 16
DH = DE // H
HD = H // 2
E, HID = 8, 512
VW = DH + 1
HV = 8 * VW
EPS = 1e-5
POOL_CHUNKS = (1, 4, 7)
DVE_CHUNKS = (0, 2, 3, 5, 6)
COMBINED = (0, 1, 2, 4, 3, 7, 5, 6)
BEHIND = 2
AHEAD = 2

REGION = B * L + P
XROWS = E * REGION + P
XW = D + 2
FT = (2 * B * L + E * (P - 1)) // P
RING = 8
TURNS, REST = divmod(FT, RING)

C_ID = 0
C_PM = C_ID + P
C_WQ = C_PM + 2
C_BM = C_WQ + 2 * P
C_LAM = C_BM + 2 * HV
C_WK = C_LAM + 2
C_TRI = C_WK + H
C_ONE = C_TRI + P
C_IOTA = C_ONE + P
C_REG = C_IOTA + E
C_TAU = C_REG + E
C_ROW = C_TAU + FT
C_PAD = C_ROW + 2 * B
C_MASK = C_PAD + 1
C_N = C_MASK + H * P


def slot(h):
    return 4 * (h % 8 // 2) + 2 * (h // 8) + h % 2


def shape_constants():
    slope = (2.0 ** np.linspace(0.0, -8.0, HD)).astype(np.float32).astype(np.float64)
    rate = np.concatenate([slope, np.zeros(H - HD)])
    t = np.arange(P)
    k = np.zeros((P, C_N), np.float64)
    k[:, C_ID:C_ID + P] = np.eye(P)
    ahead = t[None, :] - t[:, None]
    for h in range(H):
        s, at = rate[h], C_MASK + slot(h) * P
        k[:, at:at + P] = np.where(ahead >= 0, np.exp(-s * np.maximum(ahead, 0)), 0.0)
    for par in range(2):
        k[:, C_PM + par] = (t // DH) % 2 == par
    for half in range(2):
        r = rate[8 * half + t // DH]
        k[:, C_WQ + half * P:C_WQ + (half + 1) * P] = np.exp(-r[:, None] * (t[None, :] + 1))
        own = (t // DH)[:, None] == np.arange(8)[None, :].repeat(VW, 1)
        k[:, C_BM + half * HV:C_BM + (half + 1) * HV] = own
        k[:, C_LAM + half] = np.exp(-r * P)
    k[:, C_TRI:C_TRI + P] = t[:, None] < t[None, :]
    k[:, C_ONE:C_ONE + P] = 1.0
    k[:, C_IOTA:C_IOTA + E] = np.arange(E)
    k[:, C_REG:C_REG + E] = np.arange(E) * REGION
    k[:, C_TAU:C_TAU + FT] = np.arange(FT)
    for b in range(B):
        for choice in range(2):
            k[:, C_ROW + 2 * b + choice] = choice * B * L + b * P + t
    k[:, C_PAD] = 2 * B * L + t
    k[:, C_WK:C_WK + H] = np.exp(-rate[None, :] * (P - 1 - t)[:, None])
    return k.astype(np.float32)


def until(eng, sem, value):
    if isinstance(value, int) and value <= 0:
        return
    eng.wait_ge(sem, value)


def build(nc, x, in_w, in_b, q_w, q_b, k_w, k_b, out_w, out_b, W_in, W_out, Wq, bq, Wk, bk,
          smear, log_scale, Wg, W1, b1, W2, b2, cond, wmod, consts, out):
    ctx = ExitStack()
    with ctx:
        def sb(name, shape, dt=F32):
            return ctx.enter_context(nc.sbuf_tensor(name, shape, dt))

        def psum(name):
            return ctx.enter_context(nc.psum_tensor(name, [P, 512], F32))

        def sem(name):
            return ctx.enter_context(nc.semaphore(name))

        x_all = sb("x_all", [P, NT, D])
        zT_all = sb("zT_all", [P, NT * P])
        y_all = sb("y_all", [P, NT, D])
        cst = sb("cst", [P, C_N])
        ident = cst[:, C_ID:C_ID + P]
        mod = sb("mod", [P, B, 6 * D])
        gaw = sb("gaw", [P, B, D])
        gab = sb("gab", [P, B, D])
        wcat = sb("wcat", [P, 4 * DE])
        wraw = sb("wraw", [P, 4 * DE])
        wo_sb = sb("wo_sb", [P, 2, D])
        cols = sb("cols", [P, 6])
        bcol = sb("bcol", [P, 4, P])
        bqk = sb("bqk", [P, 2 * DE])
        ow_bc = sb("ow_bc", [P, 2, D])
        hv = sb("hv", [P, 2, H])
        sig = sb("sig", [P, 2, H])
        hexp = sb("hexp", [P, H])
        deps = sb("deps", [P, H])
        cT = sb("cT", [P, B])
        cE = sb("cE", [P, B])
        cR = sb("cR", [P, B])
        cS = sb("cS", [P, B])
        cB = sb("cB", [P, B, P])
        wmod_sb = sb("wmod_sb", [P, 6 * D])
        half = sb("half", [P, B])

        st = sb("st", [P, B, 6])
        mv = sb("mv", [P, AHEAD, B, 2])
        seen = sb("seen", [P, 3])
        seen_a = sb("seen_a", [P, 3])
        seen_p = sb("seen_p", [P, 1 + RING])
        ve = sb("ve", [P, AHEAD, B])
        rstd = sb("rstd", [P, AHEAD, B])

        work = sb("work", [P, 4, B, D])
        ya, yb, sq, zt = (work[:, i, :, :] for i in range(4))

        zs = sb("zs", [P, B * P])
        qk = sb("qk", [P, 2 * DE])
        mx = sb("mx", [P, 2 * H])
        ex = sb("ex", [P, 2 * DE])
        sm = sb("sm", [P, 2, 2 * H])
        rs = sb("rs", [P, H])
        rk = sb("rk", [P, 2, H])
        k1 = sb("k1", [P, DE])
        k2 = sb("k2", [P, DE])
        kf = sb("kf", [P, DE])
        kp = sb("kp", [P, B, DE])
        kw = sb("kw", [P, DE])
        vs = sb("vs", [P, 2, H, VW])
        ps_ = sb("ps_", [P, B, DE])
        ep = sb("ep", [P, B, DE])
        qeo = sb("qeo", [P, 2, 2, 2, P])
        qT = sb("qT", [P, 2 * P])
        qw = sb("qw", [P, 2, 2, P])
        kT = sb("kT", [P, 2, P])
        Pm = sb("Pm", [P, H, P])
        state = sb("state", [P, B, H, 32])
        own_kv = sb("own_kv", [P, H, VW])
        oT = sb("oT", [P, 4, P])
        den = sb("den", [P, 2, H])
        epsq = sb("epsq", [P, 2, H])
        av = sb("av", [P, DE])
        gg = sb("gg", [P, DE])
        gT = sb("gT", [P, 2, P])

        nst = sb("nst", [P, 4, 6])
        nmv = sb("nmv", [P, 4, 2])
        nve = sb("nve", [P, 4])
        nmean = sb("nmean", [P, 4])
        nrs = sb("nrs", [P, 4])
        nshift = sb("nshift", [P, 4])
        nt = sb("nt", [P, 4, D])
        np_ = sb("np", [P, 4, D])
        modulated = sb("modulated", [P, D])
        h_all = zT_all

        w1n = sb("w1n", [P, E, 4, D])
        w2n = sb("w2n", [P, E, HID])
        w1T = w1n[:, :, :, :].rearrange("p e h d -> p (e h d)")
        w2T = w2n[:, :, :].rearrange("p e h -> p (e h)")
        b1n = sb("b1n", [4 * E, P])
        b1T = sb("b1T", [P, 4 * E])
        b2_bc = sb("b2_bc", [P, E * D])
        wgn = sb("wgn", [E, D])
        wgT = sb("wgT", [P, E])
        tri = sb("tri", [P, P], BF16)
        one = sb("one", [P, P], BF16)
        hs = work[:, 3, :, :].rearrange("p b d -> p (b d)")
        hTs = wraw[:, 0:B * P]
        lg = sb("lg", [P, B, E])
        m8 = sb("m8", [P, B, 8])
        i8 = sb("i8", [P, B, 8], U32)
        i8f = sb("i8f", [P, B, 2])
        pick = sb("pick", [P, 2, B, E])
        used = sb("used", [P, B * E], BF16)
        gap = sb("gap", [P, B])
        e2 = sb("e2", [P, B])
        e3 = sb("e3", [P, B])
        count = sb("count", [P, E])
        posb = sb("posb", [P, B, E])
        posr = sb("posr", [P, B, E])
        prod = sb("prod", [P, 2, B, E])
        dest = sb("dest", [P, 2, B])
        desti = sb("desti", [P, 2, 2, B], I32)
        ids = sb("ids", [P, B, 2])
        rows_at = tuple(room_[:, 0:2 * B * XW].rearrange("p (b c w) -> p b c w", b=B, c=2) for room_ in (
            work[:, :, :, :].rearrange("p i b d -> p (i b d)"), y_all[:, :, :].rearrange("p n d -> p (n d)")))
        pad = sb("pad", [P, XW])
        cnt1 = sb("cnt1", [P, E])
        cnti = sb("cnti", [P, E], I32)
        nts = sb("nts", [P, E])
        cum = sb("cum", [P, 3, E])
        room = Pm[:, :, :].rearrange("p h i -> p (h i)")
        ge = room[0:1, 0:FT * E].rearrange("p (t e) -> p t e", e=E)
        gn = room[0:1, FT * E:2 * FT * E].rearrange("p (t e) -> p t e", e=E)
        hT = room[:, 0:2 * HID].rearrange("p (u h t) -> p u h t", u=2, h=4)
        w1s = zT_all[:, 0:4 * HID].rearrange("p (u h) -> p u h", u=4)
        xT = zT_all[:, 4 * HID:4 * HID + 4 * P].rearrange("p (u t) -> p u t", u=4)
        b2s = zT_all[:, 4 * HID + 4 * P:4 * HID + 4 * P + 4 * D].rearrange("p (u d) -> p u d", u=4)
        meta = sb("meta", [1, 5, FT])
        meta_i = sb("meta_i", [1, 2, FT], I32)
        pad_f = sb("pad_f", [1, E])
        pad_i = sb("pad_i", [1, E + 1], I32)
        xt = state[:, :, :, :].rearrange("p b h w -> p (b h w)")[:, 0:RING * XW].rearrange("p (u w) -> p u w", u=RING)
        ys = kp[:, :, :].rearrange("p b (u d) -> p (b u) d", d=D)
        X = nc.dram_tensor("expert_in", (XROWS, XW), F32).ap()
        Y = nc.dram_tensor("expert_out", (2 * NT * P, D), F32).ap()

        PA, PV, TD, TA, S0, S1, O, M = (psum(n) for n in ("PA", "PV", "TD", "TA", "S0", "S1", "O", "M"))
        S = (S0, S1)
        MA, MB = (S0, O), (S1, M)

        names = ("w w_c w_mod w_mask w_out x_in0 x_in1 x_in2 sigE sigR ce cr cb mp mc mcb mg fold bp bc1 half_ok g1 "
                 "a_st a_mv a_ve a_rs a_y a_m a_st2 a_mv2 a_ve2 a_rs2 a_z a_zT a_za "
                 "zs pqk pvp mx vv vp d e ep1 sp sum r rk eq k2 ka kb k1 kf kw tq tk qT qt qw kt sc pm o u s1 st "
                 "oc g dn av gg tg gt y yc "
                 "b_out n_st n_mv n_ve n_rs n_yt n_xt n_x n_xp n_h n_hp n_at n_zt n_m n_mp n_zT n_za "
                 "ww wb wt we wg wgt init c_z c_r c_hT c_hs c_lg c_l c_m8 c_i8 c_if c_pk "
                 "c_us c_gap c_e2 c_w c_ps c_pl c_cnt c_di c_id c_sc "
                 "tile meta padd "
                 "f_seen f_xp f_xT f_ws f_m1 f_h f_m2 f_yb f_y o_v o_x o_pv o_px "
                 + " ".join(f"f_xt{u} f_sc{u}" for u in range(RING)) + " " + " ".join(f"o_ld{i}" for i in range(NC // 2)))
        s = {n: sem("s_" + n) for n in names.split()}

        block = ctx.enter_context(nc.Block())

        def bcast(ap, n):
            return ap.unsqueeze(2).to_broadcast([ap.shape[0], ap.shape[1], n])

        def expert_of(eng, t):
            at = meta_i[0:1, 1, t:t + 1] if isinstance(t, int) else meta_i[0:1, 1, bass.ds(t, 1)]
            return eng.value_load(at, min_val=0, max_val=E - 1)

        def tiles(n):
            every = ((0, n - 3, 0, "x"), (1, n - 2, 0, "y"), (2, n + 7, 4 * AHEAD, "z"), (3, n + 8, 4 * AHEAD, "a"))
            return [(i, m, m - lo, k) for i, m, lo, k in every if not isinstance(n, int) or lo <= m < NT]

        def norms(n):
            first = sum(len(tiles(i)) for i in range(4))
            return sum(len(tiles(i)) for i in range(n + 1)) if isinstance(n, int) else first + 4 * (n - 3)

        def norm_input(i, m):
            if i == 2:
                return modulated[:, :]
            return (y_all if i == 1 else x_all)[:, bass.ds(m, 1), :].rearrange("p o d -> p (o d)")

        def routed(c):
            return not isinstance(c, int) or c >= BEHIND

        def last_chunk(g):
            return int(isinstance(g, int) and g == NC - 1)

        def z_there(n):
            return not isinstance(n, int) or 4 * AHEAD <= n + 6 < NT

        heads = lambda ap: ap.rearrange("p (h f) -> p h f", f=DH)

        def outputs(c, choice):
            if c < NC // 2:
                return y_all[:, 8 * c + 4 * choice:8 * c + 4 * choice + 4, :]
            at = (8 * (c - NC // 2) + 4 * choice) * D
            return w1T[:, at:at + B * D].rearrange("p (b d) -> p b d", b=B)

        @block.sync
        def _(sp):
            for c in range(NC):
                if c == 1:
                    sp.dma_start(wraw[:, 2 * DE:], W_in).then_inc(s["w"], 16)
                    sp.dma_start(wo_sb[:, :, :], W_out.rearrange("(h k) d -> k h d", h=2)).then_inc(s["w"], 16)
                if c == 2:
                    for i, v in enumerate((q_w, q_b, k_w, k_b, in_w, in_b)):
                        sp.dma_start(cols[:, i:i + 1], v.unsqueeze(1), allow_slow_non_contiguous=True).then_inc(s["w"], 16)
                    for i, v in enumerate((smear, log_scale)):
                        sp.dma_start(hv[:, i, :], v.partition_broadcast(P)).then_inc(s["w"], 16)
                    for i, v in enumerate((bq, bk)):
                        sp.dma_start(bqk[:, i * DE:(i + 1) * DE], v.partition_broadcast(P)).then_inc(s["w"], 16)
                    sp.dma_start(cst[:, 0:C_MASK], consts[:, 0:C_MASK]).then_inc(s["w"], 16)
                    sp.dma_start(cst[:, C_MASK:], consts[:, C_MASK:]).then_inc(s["w_mask"], 16)
                    for i, v in enumerate((out_w, out_b)):
                        sp.dma_start(ow_bc[:, i, :], v.partition_broadcast(P)).then_inc(s["w_out"], 16)
                sp.dma_start(x_all[:, 4 * c:4 * c + 4, :],
                             x[:, c * P:(c + 1) * P, :].rearrange("b p d -> p b d")).then_inc(s[f"x_in{min(c, AHEAD)}"], 16)
            sp.dma_start(wgn[:, :], Wg).then_inc(s["wg"], 16)
            sp.dma_start(b1n[:, :], b1.rearrange("e (k p) -> (e k) p", p=P)).then_inc(s["wg"], 16)
            sp.dma_start(b2_bc[:, :], b2.rearrange("e d -> (e d)").partition_broadcast(P)).then_inc(s["wb"], 16)
            for e in range(E):
                sp.dma_start(w1n[:, e, :, :], W1[e].rearrange("(h p) d -> p h d", p=P)).then_inc(s["ww"], 16)
                sp.dma_start(w2n[:, e, :], W2[e]).then_inc(s["ww"], 16)
            def shift(c, b):
                n = c * 4 + b
                done = n + 1
                until(sp, s["k2"], done)
                sp.dma_start(kp[1:113, b, :], k2[0:112, :]).then_inc(s["ka"], 16)
                sp.dma_start(kp[113:128, b, :], k2[112:127, :]).then_inc(s["ka"], 16)
                until(sp, s["kf"], done)
                sp.dma_start(kp[0:1, b, :], k2[127:128, :]).then_inc(s["kb"], 16)

            for b in range(B):
                shift(0, b)
            with sp.Fori(1, NC) as c:
                for b in range(B):
                    shift(c, b)
            sp.wait_ge(s["meta"], 1)
            sp.wait_ge(s["init"], 3)
            for e in range(E + 1):
                r = sp.value_load(pad_i[0:1, e:e + 1], min_val=0, max_val=XROWS - P)
                sp.dma_start(X[bass.ds(r, P), :], pad[:, :]).then_inc(s["padd"], 16)
            sp.wait_ge(s["meta"], 2)
            def row_of(t):
                return sp.value_load(meta_i[0:1, 0, t:t + 1] if isinstance(t, int) else meta_i[0:1, 0, bass.ds(t, 1)],
                                     min_val=0, max_val=XROWS - P)

            def fetch(t, u, turn, r=None):
                r = row_of(t) if r is None else r
                until(sp, s[f"f_sc{u}"], 16 * turn)
                sp.dma_start(xt[:, u, :], X[bass.ds(r, P), :]).then_inc(s[f"f_xt{u}"], 16)

            first_rows = [row_of(t) for t in range(4)]
            sp.wait_ge(s["padd"], 16 * (E + 1))
            sp.wait_ge(s["c_sc"], 16 * 2 * NT)
            for u in range(RING):
                fetch(u, u, 0, first_rows[u] if u < 4 else None)
            with sp.Fori(1, TURNS) as k:
                for u in range(RING):
                    fetch(k * RING + u, u, k)
            for u in range(REST):
                fetch(TURNS * RING + u, u, TURNS)

            for u in range(RING):
                sp.wait_ge(s[f"f_sc{u}"], 16 * (TURNS + (u < REST)))
            for i, c in enumerate(COMBINED):
                for choice in range(2):
                    r0 = choice * NT * P + c * B * P
                    sp.dma_start(outputs(c, choice),
                                 Y[r0:r0 + B * P, :].rearrange("(b p) d -> p b d", p=P)).then_inc(s[f"o_ld{i // 2}"], 16)
            sp.wait_ge(s["b_out"], 16 * NC)

        @block.scalar
        def _(act):
            act.dma_start(cT[:, :], cond.rearrange("b k -> k b"), allow_slow_non_contiguous=True).then_inc(s["w_c"], 16)
            act.dma_start(wmod_sb[:, :], wmod).then_inc(s["w_mod"], 16)
            act.wait_ge(s["half_ok"], 2)
            act.activation(seen_a[:, 2:3], half[:, 0:1], ACT.Exp)
            act.wait_ge(s["w_c"], 16)
            act.activation(cE[:, :], cT[:, :], ACT.Exp, scale=-1.0).then_inc(s["ce"], 1)
            act.dma_start(wraw[:, 0:DE], Wq).then_inc(s["w"], 16)
            act.dma_start(wraw[:, DE:2 * DE], Wk).then_inc(s["w"], 16)
            for b in range(B):
                act.wait_ge(s["mp"], b + 1)
                act.copy(mod[:, b, 512:], MB[b % 2][:, 0:256]).then_inc(s["mcb"], 1)
            act.wait_ge(s["w"], 16 * NW)
            act.activation(hexp[:, :], hv[:, 0, :], ACT.Exp, scale=-1.0).then_inc(s["sigE"], 1)
            act.activation(deps[:, :], hv[:, 1, :], ACT.Exp, scale=2.0).then_inc(s["sigE"], 1)
            def first_z(c):
                act.wait_ge(s["a_zT"], c + 1)
                act.activation(zT_all[:, c * 512:(c + 1) * 512], TA[:, :], ACT.Identity, bias=1.0).then_inc(s["a_za"], 1)

            def stage_z(c):
                until(act, s["pvp"], c * 4)
                act.copy(zs[:, :], zT_all[:, bass.ds(c * 512, 512)]).then_inc(s["zs"], 1)

            def front(n, b):
                until(act, s["pvp"], n + 1)
                until(act, s["u"], n - 1)
                act.copy(vs[:, b % 2, :, 0:DH], heads(PV[:, 0:DE])).then_inc(s["vv"], 1)
                until(act, s["sp"], n - 3)
                act.copy(ps_[:, b, :], PV[:, DE:]).then_inc(s["vp"], 1)
                act.activation(ep[:, b, :], PV[:, DE:], ACT.Tanh, scale=0.5).then_inc(s["vp"], 1)
                until(act, s["d"], n + 1)
                until(act, s["tq"], n)
                until(act, s["k2"], n)
                until(act, s["sum"], n)
                act.activation(ex[:, :], qk[:, :], ACT.Exp).then_inc(s["e"], 1)
                until(act, s["vp"], 2 * n + 2)
                act.activation(ep[:, b, :], ep[:, b, :], ACT.Identity, bias=1.0).then_inc(s["ep1"], 1)
            def queries(n, b):
                until(act, s["tq"], n + 1)
                until(act, s["qw"], n)
                act.copy(qT[:, :], TD[:, 0:2 * P]).then_inc(s["qT"], 1)
                until(act, s["qT"], n + 1)
                until(act, s["o"], n - 1)
                for half_ in range(2):
                    for par in range(2):
                        act.activation(qeo[:, b % 2, half_, par, :], qT[:, half_ * P:(half_ + 1) * P], ACT.Copy,
                                       scale=cst[:, C_PM + par:C_PM + par + 1]).then_inc(s["qt"], 1)

            def normalise(n):
                until(act, s["n_rs"], 2 * n + 2)
                for i, m, count, k in tiles(n):
                    if k != "x" or isinstance(n, int):
                        until(act, s[{"x": "n_h", "y": "n_x", "a": "n_m", "z": "n_zT"}[k]], count)
                act.copy(seen_a[:, 0:1], cst[:, 0:1])
                for i, m, count, k in tiles(n):
                    act.activation(nt[:, i, :], norm_input(i, m), ACT.Identity, bias=nshift[:, i:i + 1],
                                   scale=nrs[:, i:i + 1]).then_inc(s[f"n_{k}t"], 1)

            def stage_h(g):
                until(act, s["n_h"], 4 * g + 4)
                act.copy(seen_a[:, 1:2], cst[:, 0:1])
                act.copy(hs, h_all[:, bass.ds(g * 512, 512)]).then_inc(s["c_z"], 1)

            def take_h(g):
                until(act, s["c_hT"], g + 1)
                act.copy(hTs, PV[:, :]).then_inc(s["c_hs"], 1)

            def rows_of(g):
                if not last_chunk(g):
                    until(act, s["c_sc"], 128 * g)
                    act.copy(seen_a[:, 2:3], cst[:, 0:1])
                h = h_all[:, bass.ds(g * 512, 512)].rearrange("p (b d) -> p b d", b=B)
                act.copy(rows_at[last_chunk(g)][:, :, :, 0:D],
                         h.unsqueeze(2).to_broadcast([P, B, 2, D])).then_inc(s["c_r"], 1)

            def weigh(g):
                until(act, s["c_gap"], g + 1)
                act.activation(e2[:, :], gap[:, :], ACT.Exp).then_inc(s["c_e2"], 1)

            def step(c, b, first=False, last=False):
                n = c * 4 + b
                nxt = (b + 1) % B
                until(act, s["tk"], n + 1)
                until(act, s["o"], n)
                act.copy(kT[:, :, :], TA[:, 0:2 * P]).then_inc(s["kt"], 1)
                if not isinstance(n, int) or n > 0:
                    normalise(n - 1)
                if not last:
                    front(n + 1, nxt)
                if b == 0 and routed(c):
                    stage_h(c - BEHIND)
                if not first:
                    until(act, s["tg"], n)
                    until(act, s["y"], n - 1)
                    act.copy(gT[:, :, :], TA[:, 0:2 * P]).then_inc(s["gt"], 1)
                    if z_there(n):
                        act.activation(zT_all[:, bass.ds((n + 6) * P, P)], TA[:, 384:512], ACT.Identity,
                                       bias=1.0).then_inc(s["n_za"], 1)
                if not last:
                    queries(n + 1, nxt)
                if b == 0 and routed(c):
                    take_h(c - BEHIND)
                if b == 1 and routed(c):
                    rows_of(c - BEHIND)
                if not first:
                    until(act, s["y"], n)
                    act.copy(y_all[:, bass.ds(n - 1, 1), :], TA[:, 256:256 + D]).then_inc(s["yc"], 1)
                if b == 1 and routed(c):
                    weigh(c - BEHIND)
                if b == 2 and (not isinstance(c, int) or c < NC - AHEAD):
                    until(act, s["n_za"], 4 * c)
                until(act, s["o"], n + 1)
                until(act, s["g"], n)
                act.copy(oT[:, :, :], O[:, :]).then_inc(s["oc"], 1)
                if isinstance(c, int) and c in (0, NC - 1):
                    e = b if c == 0 else 4 + b
                    for i, dst in enumerate((w1T, w2T)):
                        act.wait_ge(s["wt"], 2 * e + i + 1)
                        act.copy(dst[:, e * HID:(e + 1) * HID], O[:, :]).then_inc(s["we"], 1)
                if b == 2 and not (isinstance(c, int) and c == NC - 1):
                    stage_z(c + 1)

            first_z(0)
            act.wait_ge(s["a_za"], 1)
            stage_z(0)
            act.wait_ge(s["wgt"], 1)
            act.copy(b1T[:, :], TD[:, E:E + 4 * E]).then_inc(s["wgt"], 1)
            act.copy(wgT[:, :], TD[:, 0:E]).then_inc(s["wgt"], 1)
            for c in range(1, AHEAD):
                first_z(c)
            front(0, 0)
            queries(0, 0)
            for c in range(BEHIND + 1):
                for b in range(B):
                    step(c, b, first=c == 0 and b == 0)
            with act.Fori(BEHIND + 1, NC - 2) as c:
                for b in range(B):
                    step(c, b)
            for c in (NC - 2, NC - 1):
                for b in range(B):
                    step(c, b, last=c == NC - 1 and b == 3)
            n = NT
            act.wait_ge(s["tg"], n)
            act.wait_ge(s["y"], n - 1)
            act.copy(gT[:, :, :], TA[:, 0:2 * P]).then_inc(s["gt"], 1)
            act.wait_ge(s["y"], n)
            act.copy(y_all[:, n - 1, :], TA[:, 256:256 + D]).then_inc(s["yc"], 1)
            stage_h(NC - 2)
            normalise(NT - 1)
            take_h(NC - 2)
            rows_of(NC - 2)
            weigh(NC - 2)
            for n in range(NT, NT + 3):
                normalise(n)
            stage_h(NC - 1)
            take_h(NC - 1)
            rows_of(NC - 1)
            weigh(NC - 1)
            act.activation(seen_a[:, 2:3], cst[:, 0:1], ACT.Gelu)

            def expert(t, u):
                e = expert_of(act, t)
                until(act, s["f_m1"], t + 1)
                until(act, s["f_m2"], t - 1)
                for k in range(4):
                    act.activation(hT[:, u % 2, k, :], S[u % 2][:, k * P:(k + 1) * P], ACT.Gelu,
                                   bias=b1T[:, bass.ds(e * 4 + k, 1)]).then_inc(s["f_h"], 1)

            act.wait_ge(s["meta"], 2)
            for u in range(RING):
                expert(u, u)
            with act.Fori(1, TURNS) as k:
                for u in range(RING):
                    expert(k * RING + u, u)
            for u in range(REST):
                expert(TURNS * RING + u, u)
            for c in COMBINED:
                if c in POOL_CHUNKS:
                    act.wait_ge(s["o_px"], POOL_CHUNKS.index(c) + 1)
                else:
                    act.wait_ge(s["o_x"], DVE_CHUNKS.index(c) + 1)
                act.dma_start(out[:, c * P:(c + 1) * P, :].rearrange("b p d -> p b d"),
                              x_all[:, 4 * c:4 * c + 4, :]).then_inc(s["b_out"], 16)

        @block.gpsimd
        def _(pool):
            pool.memset(half[:, :], -0.5).then_inc(s["half_ok"], 1)
            pool.memset(kp[0:1, :, :], 0.0).then_inc(s["half_ok"], 1)
            pool.memset(seen_p[:, :], 0.0)
            pool.wait_ge(s["half_ok"], 2)
            for v_ready, r_ready in (("a_ve", "a_rs"), ("a_ve2", "a_rs2")):
                for c in range(AHEAD):
                    pool.wait_ge(s[v_ready], c + 1)
                    pool.tensor_tensor(rstd[:, c, :], ve[:, c, :], half[:, :], ALU.pow).then_inc(s[r_ready], 1)

            def front(n, b):
                until(pool, s["rk"], n + 1)
                until(pool, s["kb"], n * 16)
                pool.tensor_tensor(heads(k2[:, :]), heads(ex[:, DE:]), bcast(rk[:, 1, :], DH),
                                   ALU.mult).then_inc(s["k2"], 1)
                until(pool, s["kf"], n)
                pool.tensor_tensor(heads(k1[:, :]), heads(ex[:, DE:]), bcast(rk[:, 0, :], DH),
                                   ALU.mult).then_inc(s["k1"], 1)
                until(pool, s["ep1"], n + 1)
                pool.tensor_tensor(ps_[:, b, :], ps_[:, b, :], ep[:, b, :], ALU.mult).then_inc(s["sp"], 1)

            def norm_power(n):
                lo, hi = tiles(n)[0][0], tiles(n)[-1][0] + 1
                until(pool, s["n_ve"], 2 * n + 2)
                pool.tensor_tensor(nrs[:, lo:hi], nve[:, lo:hi], half[:, lo:hi], ALU.pow).then_inc(s["n_rs"], 1)
                until(pool, s["n_rs"], 2 * n + 1)
                pool.tensor_tensor(nshift[:, lo:hi], nmean[:, lo:hi], nrs[:, lo:hi], ALU.mult).then_inc(s["n_rs"], 1)

            on = lambda k, lo=0: not isinstance(k, int) or lo <= k < NT

            def affine_products(n, b):
                m = n - 2
                if on(n + 8, 4 * AHEAD):
                    until(pool, s["n_at"], n + 1)
                    pool.tensor_tensor(np_[:, 3, :], nt[:, 3, :], mod[:, b, D:2 * D], ALU.mult).then_inc(s["n_mp"], 1)
                if on(m):
                    until(pool, s["n_yt"], m + 1)
                    pool.tensor_tensor(np_[:, 0, :], nt[:, 1, :], gaw[:, (b - 2) % B, :], ALU.mult).then_inc(s["n_xp"], 1)
                if on(m - 1):
                    until(pool, s["n_xt"], m)
                    pool.tensor_tensor(np_[:, 2, :], nt[:, 0, :], mod[:, (b - 3) % B, 4 * D:5 * D],
                                       ALU.mult).then_inc(s["n_hp"], 1)

            def affine_sums(n, b):
                m = n - 2
                if on(m):
                    until(pool, s["n_xp"], 2 * m + 1)
                    pool.tensor_tensor(np_[:, 1, :], np_[:, 0, :], gab[:, (b - 2) % B, :], ALU.add).then_inc(s["n_xp"], 1)
                if on(n + 8, 4 * AHEAD):
                    until(pool, s["n_mp"], n + 1)
                    until(pool, s["n_zt"], n)
                    pool.tensor_tensor(modulated[:, :], np_[:, 3, :], mod[:, b, 0:D], ALU.add).then_inc(s["n_m"], 1)
                if on(m):
                    xm = x_all[:, bass.ds(m, 1), :].rearrange("p o d -> p (o d)")
                    until(pool, s["n_xp"], 2 * m + 2)
                    pool.tensor_tensor(xm, xm, np_[:, 1, :], ALU.add).then_inc(s["n_x"], 1)
                if on(m - 1):
                    until(pool, s["n_hp"], m)
                    pool.tensor_tensor(h_all[:, bass.ds((m - 1) * D, D)], np_[:, 2, :], mod[:, (b - 3) % B, 3 * D:4 * D],
                                       ALU.add).then_inc(s["n_h"], 1)

            def send(g, i):
                at, choice, b = last_chunk(g), i // B, i % B
                if i == 0:
                    until(pool, s["c_di"], g + 1)
                    pool.tensor_tensor(seen_p[:, 0:1], half[:, 0:1], half[:, 0:1], ALU.mult)
                pool.indirect_dma_start(
                    X, bass.IndirectOffsetOnAxis(ap=desti[:, at, choice, b:b + 1], axis=0),
                    rows_at[at][:, b, choice, :], None).then_inc(s["c_sc"], 16)

            SENDS = {(3, 0): (0,), (3, 1): (1, 2, 3), (0, 0): (4,), (0, 1): (5, 6, 7)}

            def sends(c, b, place):
                turn = c - 1 if b == 0 else c
                if routed(turn):
                    for i in SENDS.get((b, place), ()):
                        send(turn - BEHIND, i)

            def gate(n, b):
                until(pool, s["av"], n + 1)
                until(pool, s["sp"], n + 1)
                until(pool, s["tg"], n)
                pool.tensor_tensor(gg[:, :], av[:, :], ps_[:, b, :], ALU.mult).then_inc(s["gg"], 1)

            def step(c, b, first=False, last=False):
                n = c * 4 + b
                until(pool, s["kf"], n + 1)
                until(pool, s["u"], n)
                pool.tensor_tensor(heads(kw[:, :]), heads(kf[:, :]), bcast(cst[:, C_WK:C_WK + H], DH),
                                   ALU.mult).then_inc(s["kw"], 1)
                sends(c, b, 0)
                if not first:
                    gate(n - 1, (b - 1) % B)
                    affine_products(n - 1, (b - 1) % B)
                if not last:
                    front(n + 1, (b + 1) % B)
                if not first:
                    affine_sums(n - 1, (b - 1) % B)
                sends(c, b, 1)
                norm_power(n)
                sends(c, b, 2)

            front(0, 0)
            for c in range(BEHIND + 1):
                for b in range(B):
                    step(c, b, first=c == 0 and b == 0)
            with pool.Fori(BEHIND + 1, NC - 2) as c:
                for b in range(B):
                    step(c, b)
            for c in (NC - 2, NC - 1):
                for b in range(B):
                    step(c, b, last=c == NC - 1 and b == 3)
            sends(NC, 0, 0)
            gate(NT - 1, 3)
            sends(NC, 0, 1)
            for n in range(NT, NT + 4):
                affine_products(n - 1, (n - 1) % B)
                affine_sums(n - 1, (n - 1) % B)
                if n > NT:
                    send(NC - 2, n - NT - 1)
                if n < NT + 3:
                    norm_power(n)
            for i in range(3, 2 * B):
                send(NC - 2, i)
            for i in range(2 * B):
                send(NC - 1, i)

            def scatter(t, u):
                until(pool, s["f_y"], t + 1)
                pool.tensor_tensor(seen_p[:, 1 + u:2 + u], half[:, 0:1], half[:, 0:1], ALU.mult).then_inc(s["f_seen"], 1)
                pool.indirect_dma_start(
                    Y, bass.IndirectOffsetOnAxis(ap=xt[:, u, D + 1:D + 2].bitcast(I32), axis=0),
                    ys[:, u, :], None, bounds_check=2 * NT * P - 1, oob_is_err=False).then_inc(s[f"f_sc{u}"], 16)

            for u in range(RING):
                scatter(u, u)
            with pool.Fori(1, TURNS) as k:
                for u in range(RING):
                    scatter(k * RING + u, u)
            for u in range(REST):
                scatter(TURNS * RING + u, u)

            for i, c in enumerate(POOL_CHUNKS):
                pool.wait_ge(s[f"o_ld{COMBINED.index(c) // 2}"], 64)
                pool.tensor_tensor(sq[:, :, :], outputs(c, 0), outputs(c, 1), ALU.add).then_inc(s["o_pv"], 1)
                pool.wait_ge(s["o_pv"], 2 * i + 1)
                pool.tensor_tensor(zt[:, :, :], sq[:, :, :], mod[:, :, 5 * D:], ALU.mult).then_inc(s["o_pv"], 1)
                pool.wait_ge(s["o_pv"], 2 * i + 2)
                xc = x_all[:, 4 * c:4 * c + 4, :]
                pool.tensor_tensor(xc, xc, zt[:, :, :], ALU.add).then_inc(s["o_px"], 1)

        @block.vector
        def _(dve):
            dve.memset(vs[:, :, :, :], 1.0).then_inc(s["g1"], 1)
            dve.memset(state[:, :, :, :], 0.0).then_inc(s["g1"], 1)
            def layernorm_sums(c, source, st_done, mv_done, ve_done):
                for b in range(B):
                    dve.bn_stats(st[:, b, :], source(b)).then_inc(s[st_done], 1)
                dve.wait_ge(s[st_done], c * 4 + 4)
                for b in range(B):
                    dve.bn_aggr(mv[:, c, b, :], st[:, b, :]).then_inc(s[mv_done], 1)
                dve.wait_ge(s[mv_done], c * 4 + 4)
                dve.tensor_scalar_add(ve[:, c, :], mv[:, c, :, 1], EPS).then_inc(s[ve_done], 1)

            def first_norm(c, dst):
                dve.wait_ge(s["a_rs"], c + 1)
                for b in range(B):
                    dve.tensor_scalar(dst[:, b, :], x_all[:, c * 4 + b, :], mv[:, c, b, 0:1], rstd[:, c, b:b + 1],
                                      ALU.subtract, ALU.mult).then_inc(s["a_y"], 1)

            def modulate_chunk(c, src):
                dve.wait_ge(s["a_y"], c * 4 + 4)
                dve.tensor_tensor(yb[:, :, :], src[:, :, :], mod[:, :, D:2 * D], ALU.mult).then_inc(s["a_m"], 1)
                dve.wait_ge(s["a_m"], 2 * c + 1)
                dve.tensor_tensor(src[:, :, :], yb[:, :, :], mod[:, :, 0:D], ALU.add).then_inc(s["a_m"], 1)
                dve.wait_ge(s["a_m"], 2 * c + 2)
                layernorm_sums(c, lambda b: src[:, b, :], "a_st2", "a_mv2", "a_ve2")

            def second_norm(c, src):
                dve.wait_ge(s["a_rs2"], c + 1)
                until(dve, s["a_zT"], c)
                for b in range(B):
                    dve.tensor_scalar(zt[:, b, :], src[:, b, :], mv[:, c, b, 0:1], rstd[:, c, b:b + 1],
                                      ALU.subtract, ALU.mult).then_inc(s["a_z"], 1)

            dve.wait_ge(s["x_in0"], 16)
            layernorm_sums(0, lambda b: x_all[:, b, :], "a_st", "a_mv", "a_ve")
            dve.wait_ge(s["w_c"], 16)
            dve.wait_ge(s["ce"], 1)
            dve.tensor_scalar_add(cR[:, :], cE[:, :], 1.0).then_inc(s["cr"], 1)
            dve.wait_ge(s["cr"], 1)
            dve.reciprocal(cE[:, :], cR[:, :]).then_inc(s["cr"], 1)
            dve.wait_ge(s["cr"], 2)
            dve.tensor_tensor(cS[:, :], cE[:, :], cT[:, :], ALU.mult).then_inc(s["cr"], 1)
            dve.wait_ge(s["cr"], 3)
            dve.tensor_copy(cB[:, :, :], bcast(cS[:, :], P)).then_inc(s["cb"], 1)
            first_norm(0, ya)
            dve.wait_ge(s["x_in1"], 16)
            layernorm_sums(1, lambda b: x_all[:, 4 + b, :], "a_st", "a_mv", "a_ve")
            first_norm(1, sq)
            def take_modulation(b):
                dve.wait_ge(s["mp"], b + 1)
                dve.tensor_copy(mod[:, b, 0:512], MA[b % 2][:, :]).then_inc(s["mc"], 1)

            for b in range(B - 1):
                take_modulation(b)
            dve.wait_ge(s["w"], 16 * NW)
            for i, (lo, hi) in enumerate(((0, DE), (DE, 2 * DE), (2 * DE, 4 * DE))):
                dve.tensor_scalar_mul(wcat[:, lo:hi], wraw[:, lo:hi], cols[:, 2 * i:2 * i + 1]).then_inc(s["fold"], 1)
                dve.tensor_copy(bcol[:, i, :], cols[:, 2 * i + 1:2 * i + 2].to_broadcast([P, P])).then_inc(s["fold"], 1)
            dve.memset(bcol[:, 3, :], -1.0).then_inc(s["fold"], 1)
            take_modulation(B - 1)
            dve.wait_ge(s["mc"], B)
            dve.tensor_scalar_add(mod[:, :, D:2 * D], mod[:, :, D:2 * D], 1.0).then_inc(s["mc"], 1)
            dve.wait_ge(s["mc"], B + 1)
            modulate_chunk(0, ya)
            second_norm(0, ya)
            dve.wait_ge(s["bp"], 1)
            dve.tensor_tensor(bqk[:, :], PA[:, :], bqk[:, :], ALU.add).then_inc(s["bc1"], 1)
            dve.wait_ge(s["bc1"], 1)
            for lo, src in ((0, bqk), (512, PV)):
                w = wcat[:, lo:lo + 512]
                dve.scalar_tensor_tensor(w, src[:, :], 1.0 / D, w, ALU.mult, ALU.add).then_inc(s["bc1"], 1)
            modulate_chunk(1, sq)
            dve.wait_ge(s["sigE"], 2)
            dve.tensor_scalar_add(sig[:, 0, :], hexp[:, :], 1.0).then_inc(s["sigR"], 1)
            dve.wait_ge(s["sigR"], 1)
            dve.reciprocal(sig[:, 1, :], sig[:, 0, :]).then_inc(s["sigR"], 1)
            dve.wait_ge(s["sigR"], 2)
            dve.tensor_scalar(sig[:, 0, :], sig[:, 1, :], -1.0, 1.0, ALU.mult, ALU.add).then_inc(s["sigR"], 1)
            dve.tensor_scalar_mul(deps[:, :], deps[:, :], EPS).then_inc(s["sigR"], 1)
            second_norm(1, sq)

            def front1(n, b):
                until(dve, s["pqk"], n + 1)
                dve.tensor_reduce(mx[:, :], heads(PA[:, :]), AX.X, ALU.max).then_inc(s["mx"], 1)
                until(dve, s["mx"], n + 1)
                until(dve, s["e"], n)
                dve.tensor_tensor(heads(qk[:, :]), heads(PA[:, :]), bcast(mx[:, :], DH), ALU.subtract).then_inc(s["d"], 1)

            def front2(n, b):
                until(dve, s["e"], n + 1)
                dve.tensor_reduce(sm[:, b % 2, :], heads(ex[:, :]), AX.X, ALU.add).then_inc(s["sum"], 1)
                until(dve, s["sum"], n + 1)
                dve.reciprocal(rs[:, :], sm[:, b % 2, H:]).then_inc(s["r"], 1)
                until(dve, s["r"], n + 1)
                until(dve, s["k1"], n)
                dve.tensor_tensor(rk[:, :, :], sig[:, :, :], rs[:, :].unsqueeze(1).to_broadcast([P, 2, H]),
                                  ALU.mult).then_inc(s["rk"], 1)
                until(dve, s["dn"], 2 * (n - 1))
                dve.tensor_tensor(epsq[:, b % 2, :], deps[:, :], sm[:, b % 2, 0:H], ALU.mult).then_inc(s["eq"], 1)

            def front3(n, b):
                until(dve, s["k1"], n + 1)
                until(dve, s["ka"], n * 32 + 32)
                until(dve, s["kb"], n * 16 - 48)
                if isinstance(n, int) and n == 0:
                    dve.wait_ge(s["half_ok"], 2)
                until(dve, s["kw"], n)
                until(dve, s["tk"], n)
                dve.tensor_tensor(kf[:, :], k1[:, :], kp[:, b, :], ALU.add).then_inc(s["kf"], 1)

            def back(n, b):
                until(dve, s["g"], n + 1)
                until(dve, s["eq"], n + 1)
                G = M[:, :].rearrange("p (h w) -> p h w", w=32)
                dve.tensor_tensor(den[:, 0, :], G[:, :, DH], epsq[:, b % 2, :], ALU.add).then_inc(s["dn"], 1)
                until(dve, s["dn"], 2 * n + 1)
                dve.reciprocal(den[:, 1, :], den[:, 0, :]).then_inc(s["dn"], 1)
                until(dve, s["dn"], 2 * n + 2)
                until(dve, s["gg"], n)
                dve.tensor_tensor(heads(av[:, :]), G[:, :, 0:DH], bcast(den[:, 1, :], DH), ALU.mult).then_inc(s["av"], 1)

            def queries(n, b):
                until(dve, s["qT"], n + 1)
                until(dve, s["o"], n - 1)
                dve.tensor_tensor(qw[:, b % 2, :, :].rearrange("p a i -> p (a i)"), qT[:, :], cst[:, C_WQ:C_WQ + 2 * P],
                                  ALU.mult).then_inc(s["qw"], 1)

            def masked(n, j):
                until(dve, s["sc"], n * 4 + j + 1)
                until(dve, s["o"], n)
                mask = cst[:, C_MASK + 4 * j * P:C_MASK + 4 * (j + 1) * P].rearrange("p (h i) -> p h i", i=P)
                dve.tensor_tensor(Pm[:, 4 * j:4 * j + 4, :], S[j % 2][:, :].rearrange("p (h i) -> p h i", i=P), mask,
                                  ALU.mult).then_inc(s["pm"], 1)

            def step(c, b, first=False, last=False):
                n = c * 4 + b
                nxt = (b + 1) % B
                if b == 2 and routed(c):
                    take_places(c - BEHIND)
                if not last:
                    front1(n + 1, nxt)
                if not first:
                    back(n - 1, (b - 1) % B)
                masked(n, 0)
                masked(n, 1)
                if not last:
                    front2(n + 1, nxt)
                masked(n, 2)
                masked(n, 3)
                if not last:
                    queries(n + 1, nxt)
                if b == 1 and routed(c):
                    choose(c - BEHIND)
                if b == 2 and routed(c):
                    settle(c - BEHIND)
                if not last:
                    front3(n + 1, nxt)
                statistics(n)
                until(dve, s["u"], n + 1)
                dve.tensor_tensor(own_kv[:, :, :], M[:, 0:2 * HV].rearrange("p (h w) -> p h w", w=VW),
                                  cst[:, C_BM:C_BM + 2 * HV].rearrange("p (h w) -> p h w", w=VW),
                                  ALU.mult).then_inc(s["s1"], 1)
                until(dve, s["s1"], n + 1)
                until(dve, s["o"], n + 1)
                for half_ in range(2):
                    own = state[:, b, 8 * half_:8 * half_ + 8, 0:VW]
                    dve.scalar_tensor_tensor(own, own, cst[:, C_LAM + half_:C_LAM + half_ + 1],
                                             own_kv[:, 8 * half_:8 * half_ + 8, :], ALU.mult, ALU.add).then_inc(s["st"], 1)
                if b == 0 and routed(c):
                    take_logits(c - BEHIND)

            def gates():
                dve.tensor_scalar_mul(wo_sb[:, :, :], wo_sb[:, :, :], 0.5).then_inc(s["mg"], 1)
                dve.wait_ge(s["mcb"], B)
                m = mod[:, :, 4 * D:5 * D]
                dve.tensor_scalar_add(m, m, 1.0).then_inc(s["mg"], 1)
                dve.wait_ge(s["a_zT"], AHEAD)
                for i, tmp in ((2, ya), (5, yb)):
                    m = mod[:, :, i * D:(i + 1) * D]
                    dve.tensor_scalar(tmp[:, :, :], m, 0.0, 2.0, ALU.is_ge, ALU.mult).then_inc(s["mg"], 1)
                for i, tmp in ((2, zt), (5, sq)):
                    m = mod[:, :, i * D:(i + 1) * D]
                    dve.scalar_tensor_tensor(tmp[:, :, :], m, -1.0, m, ALU.mult, ALU.max).then_inc(s["mg"], 1)
                dve.wait_ge(s["mg"], 6)
                for i, tmp in ((2, zt), (5, sq)):
                    dve.tensor_scalar_max(tmp[:, :, :], tmp[:, :, :], 0.25).then_inc(s["mg"], 1)
                dve.wait_ge(s["mg"], 8)
                for i, sign, size in ((2, ya, zt), (5, yb, sq)):
                    dve.scalar_tensor_tensor(mod[:, :, i * D:(i + 1) * D], sign[:, :, :], -1.0, size[:, :, :],
                                             ALU.add, ALU.mult).then_inc(s["mg"], 1)
                dve.wait_ge(s["mg"], 10)
                dve.wait_ge(s["w_out"], 32)
                for i, dst in enumerate((gaw, gab)):
                    dve.tensor_tensor(dst[:, :, :], mod[:, :, 2 * D:3 * D],
                                      ow_bc[:, i, :].unsqueeze(1).to_broadcast([P, B, D]), ALU.mult).then_inc(s["mg"], 1)

            def statistics(n):
                made = {"x": "n_x", "y": "yc", "z": "n_m"}
                for i, m, count, k in tiles(n):
                    if k != "a":
                        until(dve, s[made[k]], count + 1)
                    until(dve, s[f"n_{k}t"], count)
                dve.tensor_copy(seen[:, 0:1], cst[:, 0:1])
                for i, m, count, k in tiles(n):
                    dve.bn_stats(nst[:, i, :], norm_input(i, m)).then_inc(s["n_st"], 1)
                until(dve, s["n_st"], norms(n))
                dve.tensor_copy(seen[:, 1:2], cst[:, 0:1])
                for i, m, count, k in tiles(n):
                    dve.bn_aggr(nmv[:, i, :], nst[:, i, :]).then_inc(s["n_mv"], 1)
                until(dve, s["n_mv"], norms(n))
                lo, hi = tiles(n)[0][0], tiles(n)[-1][0] + 1
                dve.tensor_scalar_mul(nmean[:, lo:hi], nmv[:, lo:hi, 0], -1.0).then_inc(s["n_ve"], 1)
                dve.tensor_scalar_add(nve[:, lo:hi], nmv[:, lo:hi, 1], EPS).then_inc(s["n_ve"], 1)

            def take_logits(g):
                until(dve, s["c_lg"], g + 1)
                dve.tensor_copy(lg[:, :, :].rearrange("p b e -> p (b e)"), PV[:, 0:B * E]).then_inc(s["c_l"], 1)

            def choose(g):
                until(dve, s["c_l"], g + 1)
                dve.tensor_copy(seen[:, 2:3], lg[:, 0, 0:1])
                for b in range(B):
                    dve.max(m8[:, b, :], lg[:, b, :]).then_inc(s["c_m8"], 1)
                until(dve, s["c_m8"], g * 4 + 4)
                dve.tensor_tensor(gap[:, :], m8[:, :, 1], m8[:, :, 0], ALU.subtract).then_inc(s["c_gap"], 1)
                for b in range(B):
                    dve.max_index(i8[:, b, :], m8[:, b, :], lg[:, b, :]).then_inc(s["c_i8"], 1)
                until(dve, s["c_i8"], g * 4 + 4)
                dve.tensor_copy(i8f[:, :, :], i8[:, :, 0:2]).then_inc(s["c_if"], 1)
                until(dve, s["c_if"], g + 1)
                iota = cst[:, C_IOTA:C_IOTA + E].unsqueeze(1).to_broadcast([P, B, E])
                for choice in range(2):
                    dve.tensor_tensor(pick[:, choice, :, :], iota, bcast(i8f[:, :, choice], E),
                                      ALU.is_equal).then_inc(s["c_pk"], 1)
                until(dve, s["c_pk"], 2 * g + 2)
                dve.tensor_tensor(used[:, :].rearrange("p (b e) -> p b e", e=E), pick[:, 0, :, :], pick[:, 1, :, :],
                                  ALU.add).then_inc(s["c_us"], 1)

            def take_places(g):
                until(dve, s["c_ps"], g + 1)
                dve.tensor_tensor(posb[:, :, :], PV[:, 0:B * E].rearrange("p (b e) -> p b e", e=E),
                                  count[:, :].unsqueeze(1).to_broadcast([P, B, E]), ALU.add).then_inc(s["c_pl"], 1)
                until(dve, s["c_pl"], 5 * g + 1)
                dve.tensor_tensor(count[:, :], count[:, :], PV[:, B * E:(B + 1) * E], ALU.add).then_inc(s["c_cnt"], 1)

            def settle(g):
                rows = rows_at[last_chunk(g)]
                until(dve, s["c_e2"], g + 1)
                dve.tensor_scalar_add(e3[:, :], e2[:, :], 1.0).then_inc(s["c_w"], 1)
                dve.tensor_tensor(posr[:, :, :], posb[:, :, :],
                                  cst[:, C_REG:C_REG + E].unsqueeze(1).to_broadcast([P, B, E]), ALU.add).then_inc(s["c_pl"], 1)
                if not last_chunk(g):
                    until(dve, s["c_sc"], 128 * g)
                until(dve, s["c_w"], 3 * g + 1)
                dve.reciprocal(rows[:, :, 0, D], e3[:, :]).then_inc(s["c_w"], 1)
                dve.tensor_copy(rows[:, :, :, D + 1].bitcast(I32), ids[:, :, :]).then_inc(s["c_id"], 1)
                until(dve, s["c_pl"], 5 * g + 2)
                for choice in range(2):
                    dve.tensor_tensor(prod[:, choice, :, :], pick[:, choice, :, :], posr[:, :, :],
                                      ALU.mult).then_inc(s["c_pl"], 1)
                until(dve, s["c_w"], 3 * g + 2)
                dve.tensor_tensor(rows[:, :, 1, D], rows[:, :, 0, D], e2[:, :], ALU.mult).then_inc(s["c_w"], 1)
                until(dve, s["c_id"], g + 1)
                dve.tensor_scalar_add(ids[:, :, :], ids[:, :, :], float(B * P))
                until(dve, s["c_pl"], 5 * g + 4)
                dve.tensor_reduce(dest[:, :, :], prod[:, :, :, :], AX.X, ALU.add).then_inc(s["c_pl"], 1)
                until(dve, s["c_pl"], 5 * g + 5)
                until(dve, s["c_w"], 3 * g + 3)
                until(dve, s["c_r"], g + 1)
                dve.tensor_copy(desti[:, last_chunk(g), :, :], dest[:, :, :]).then_inc(s["c_di"], 1)

            dve.wait_ge(s["g1"], 2)
            front1(0, 0)
            front2(0, 0)
            queries(0, 0)
            dve.memset(pad[:, 0:D + 1], 0.0).then_inc(s["init"], 1)
            dve.tensor_copy(pad[:, D + 1:].bitcast(I32), cst[:, C_PAD:C_PAD + 1]).then_inc(s["init"], 1)
            dve.memset(pad_i[:, :], E * REGION).then_inc(s["init"], 1)
            dve.memset(count[:, :], 0.0).then_inc(s["init"], 1)
            dve.tensor_copy(ids[:, :, :].rearrange("p b c -> p (b c)"), cst[:, C_ROW:C_ROW + 2 * B]).then_inc(s["init"], 1)
            dve.tensor_copy(tri[:, :], cst[:, C_TRI:C_TRI + P]).then_inc(s["init"], 1)
            dve.tensor_copy(one[:, :], cst[:, C_ONE:C_ONE + P]).then_inc(s["init"], 1)
            gates()
            front3(0, 0)
            dve.wait_ge(s["x_in2"], 16 * (NC - AHEAD))
            dve.wait_ge(s["w_mask"], 16)
            dve.wait_ge(s["init"], 7)
            dve.wait_ge(s["mg"], 12)
            for c in range(BEHIND + 1):
                for b in range(B):
                    step(c, b, first=c == 0 and b == 0)
            with dve.Fori(BEHIND + 1, NC - 2) as c:
                for b in range(B):
                    step(c, b)
            for c in (NC - 2, NC - 1):
                for b in range(B):
                    step(c, b, last=c == NC - 1 and b == 3)
            back(NT - 1, 3)

            statistics(NT)
            take_logits(NC - 2)
            choose(NC - 2)
            take_places(NC - 2)
            settle(NC - 2)
            statistics(NT + 1)
            statistics(NT + 2)
            take_logits(NC - 1)
            choose(NC - 1)
            take_places(NC - 1)
            settle(NC - 1)

            dve.wait_ge(s["c_cnt"], NC)
            dve.tensor_scalar_add(cnt1[:, :], count[:, :], float(P - 1)).then_inc(s["tile"], 1)
            dve.tensor_tensor(pad_f[:, :], count[0:1, :], cst[0:1, C_REG:C_REG + E], ALU.add).then_inc(s["tile"], 1)
            dve.wait_ge(s["tile"], 2)
            dve.tensor_copy(pad_i[:, 0:E], pad_f[:, :]).then_inc(s["meta"], 1)
            dve.tensor_copy(cnti[:, :], cnt1[:, :]).then_inc(s["tile"], 1)
            dve.wait_ge(s["tile"], 3)
            dve.tensor_single_scalar(cnti[:, :], cnti[:, :], 7, op=ALU.logical_shift_right).then_inc(s["tile"], 1)
            dve.wait_ge(s["tile"], 4)
            dve.tensor_copy(nts[:, :], cnti[:, :]).then_inc(s["tile"], 1)
            dve.wait_ge(s["tile"], 5)
            src = nts[:, :]
            for i, d in enumerate((1, 2, 4)):
                dve.tensor_copy(cum[:, i, 0:d], src[:, 0:d]).then_inc(s["tile"], 1)
                dve.tensor_tensor(cum[:, i, d:], src[:, d:], src[:, 0:E - d], ALU.add).then_inc(s["tile"], 1)
                dve.wait_ge(s["tile"], 2 * i + 7)
                src = cum[:, i, :]
            tau = cst[0:1, C_TAU:C_TAU + FT]
            dve.tensor_tensor(ge[:, :, :], bcast(tau, E), cum[0:1, 2, :].unsqueeze(1).to_broadcast([1, FT, E]),
                              ALU.is_ge).then_inc(s["tile"], 1)
            dve.wait_ge(s["tile"], 12)
            dve.tensor_tensor(gn[:, :, :], ge[:, :, :], nts[0:1, :].unsqueeze(1).to_broadcast([1, FT, E]),
                              ALU.mult).then_inc(s["tile"], 1)
            dve.tensor_reduce(meta[:, 0, :], ge[:, :, :], AX.X, ALU.add).then_inc(s["tile"], 1)
            dve.wait_ge(s["tile"], 14)
            dve.tensor_reduce(meta[:, 1, :], gn[:, :, :], AX.X, ALU.add).then_inc(s["tile"], 1)
            dve.tensor_scalar(meta[:, 2, :], meta[:, 0, :], float(E), None, ALU.is_lt).then_inc(s["tile"], 1)
            dve.wait_ge(s["tile"], 16)
            dve.tensor_tensor(meta[:, 3, :], tau, meta[:, 1, :], ALU.subtract).then_inc(s["tile"], 1)
            dve.wait_ge(s["tile"], 17)
            dve.tensor_tensor(meta[:, 4, :], meta[:, 3, :], meta[:, 2, :], ALU.mult).then_inc(s["tile"], 1)
            dve.tensor_scalar(meta[:, 1, :], meta[:, 0, :], float(REGION), None, ALU.mult).then_inc(s["tile"], 1)
            dve.wait_ge(s["tile"], 19)
            dve.scalar_tensor_tensor(meta[:, 3, :], meta[:, 4, :], float(P), meta[:, 1, :], ALU.mult,
                                     ALU.add).then_inc(s["tile"], 1)
            dve.tensor_scalar_min(meta_i[:, 1, :], meta[:, 0, :], float(E - 1)).then_inc(s["tile"], 1)
            dve.wait_ge(s["tile"], 21)
            dve.tensor_copy(meta_i[:, 0, :], meta[:, 3, :]).then_inc(s["meta"], 1)
            dve.wait_ge(s["meta"], 2)

            def stage(t, u):
                e = expert_of(dve, t)
                until(dve, s["f_m1"], t - 3)
                dve.tensor_copy(w1s[:, u % 4, :], w1T[:, bass.ds(e * HID, HID)]).then_inc(s["f_ws"], 1)
                dve.tensor_copy(b2s[:, u % 4, :], b2_bc[:, bass.ds(e * D, D)]).then_inc(s["f_ws"], 1)
                until(dve, s["f_xp"], t + 1)
                dve.tensor_copy(xT[:, u % 4, :], (TA, TD)[u % 2][:, 0:P]).then_inc(s["f_xT"], 1)

            def gated(t, u, turn):
                until(dve, s["f_m2"], t + 1)
                until(dve, s["f_ws"], 2 * t + 2)
                until(dve, s["f_seen"], t - RING + 1)
                until(dve, s[f"f_sc{u}"], 16 * turn)
                dve.tensor_tensor(ys[:, u, :], (O, M)[u % 2][:, 0:D], b2s[:, u % 4, :], ALU.add).then_inc(s["f_yb"], 1)
                until(dve, s["f_yb"], t + 1)
                dve.tensor_scalar_mul(ys[:, u, :], ys[:, u, :], xt[:, u, D:D + 1]).then_inc(s["f_y"], 1)

            def expert(t, u, turn, ahead):
                if ahead > 3:
                    stage(t + 3, u + 3)
                gated(t, u, turn)

            dve.wait_ge(s["wb"], 16)
            stage(0, 0)
            stage(1, 1)
            stage(2, 2)
            for u in range(RING):
                expert(u, u, 0, RING)
            with dve.Fori(1, TURNS) as k:
                for u in range(RING):
                    expert(k * RING + u, u, k, RING)
            for u in range(REST):
                expert(TURNS * RING + u, u, TURNS, REST - u)

            for i, c in enumerate(DVE_CHUNKS):
                dve.wait_ge(s[f"o_ld{COMBINED.index(c) // 2}"], 64)
                dve.tensor_tensor(ya[:, :, :], outputs(c, 0), outputs(c, 1), ALU.add).then_inc(s["o_v"], 1)
                dve.wait_ge(s["o_v"], 2 * i + 1)
                dve.tensor_tensor(yb[:, :, :], ya[:, :, :], mod[:, :, 5 * D:], ALU.mult).then_inc(s["o_v"], 1)
                dve.wait_ge(s["o_v"], 2 * i + 2)
                xc = x_all[:, 4 * c:4 * c + 4, :]
                dve.tensor_tensor(xc, xc, yb[:, :, :], ALU.add).then_inc(s["o_x"], 1)

        @block.tensor
        def _(pe):
            pe.wait_ge(s["cb"], 1)
            pe.wait_ge(s["w_mod"], 16)
            for b in range(B):
                until(pe, s["mc"], b - 1)
                until(pe, s["mcb"], b - 1)
                pe.matmul(MA[b % 2][:, :], cB[:, b, :], wmod_sb[:, 0:512], start=True, stop=True)
                pe.matmul(MB[b % 2][:, 0:256], cB[:, b, :], wmod_sb[:, 512:], start=True, stop=True).then_inc(s["mp"], 1)
            pe.wait_ge(s["fold"], 7)
            pe.wait_ge(s["w"], 16 * NW)
            for bank, lo, hi, i, at in ((PA, 0, DE, 0, 0), (PA, DE, 2 * DE, 1, DE), (PV, 2 * DE, 4 * DE, 2, 0)):
                dst = bank[:, at:at + hi - lo]
                pe.matmul(dst, bcol[:, i, :], wraw[:, lo:hi], start=True, stop=False)
                ins = pe.matmul(dst, bcol[:, 3, :], wcat[:, lo:hi], start=False, stop=True)
            ins.then_inc(s["bp"], 1)
            def first_transposes(c):
                pe.wait_ge(s["a_z"], c * 4 + 4)
                until(pe, s["a_za"], c)
                for b in range(B):
                    ins = pe.transpose(TA[:, b * P:(b + 1) * P], zt[:, b, :], ident)
                ins.then_inc(s["a_zT"], 1)

            first_transposes(0)
            pe.wait_ge(s["wg"], 32)
            pe.transpose(TD[:, 0:E], wgn[:, :], ident[0:E, 0:E])
            pe.transpose(TD[:, E:E + 4 * E], b1n[:, :], ident[0:4 * E, 0:4 * E]).then_inc(s["wgt"], 1)

            def h_transposes(g):
                until(pe, s["c_z"], g + 1)
                for b in range(B):
                    ins = pe.transpose(PV[:, b * P:(b + 1) * P], hs[:, b * P:(b + 1) * P], ident)
                ins.then_inc(s["c_hT"], 1)

            def logits(g):
                until(pe, s["c_hs"], g + 1)
                for b in range(B):
                    ins = pe.matmul(PV[:, b * E:(b + 1) * E], hTs[:, b * P:(b + 1) * P], wgT[:, :], start=True, stop=True)
                ins.then_inc(s["c_lg"], 1)

            def places(g):
                until(pe, s["c_us"], g + 1)
                for b in range(B + 1):
                    for a in range(min(b + 1, B)):
                        ins = pe.matmul(PV[:, b * E:(b + 1) * E], (tri if a == b else one)[:, :],
                                        used[:, a * E:(a + 1) * E], start=a == 0, stop=a == min(b, B - 1))
                ins.then_inc(s["c_ps"], 1)

            def front_qk(n, b):
                until(pe, s["d"], n)
                pe.matmul(PA[:, :], zs[:, b * P:(b + 1) * P], wcat[:, 0:512], start=True, stop=True).then_inc(s["pqk"], 1)

            def front_vp(n, b):
                until(pe, s["vp"], 2 * n)
                pe.matmul(PV[:, :], zs[:, b * P:(b + 1) * P], wcat[:, 512:], start=True, stop=True).then_inc(s["pvp"], 1)

            def queries(n):
                until(pe, s["e"], n + 1)
                until(pe, s["qT"], n)
                for i in range(2):
                    ins = pe.transpose(TD[:, i * P:(i + 1) * P], ex[:, i * P:(i + 1) * P], ident)
                ins.then_inc(s["tq"], 1)

            def scores(n, b, j):
                until(pe, s["pm"], n * 4 + j - 1)
                r = 32 * j
                for half_ in range(2):
                    ins = pe.matmul(S[j % 2][:, half_ * 256:(half_ + 1) * 256], kT[r:r + 32, half_, :],
                                    qeo[r:r + 32, b % 2, half_, :, :], start=True, stop=True)
                ins.then_inc(s["sc"], 1)

            def values(n, b, j):
                until(pe, s["pm"], n * 4 + 2 * (j % 2) + 2)
                if j == 0:
                    until(pe, s["qw"], n + 1)
                    until(pe, s["oc"], n)
                    if isinstance(n, int):
                        until(pe, s["we"], 2 * n if n <= 4 else 8 + 2 * max(n - NT + 4, 0))
                    until(pe, s["st"], 2 * (n - 3))
                    until(pe, s["vv"], n + 1)
                half_ = j // 2
                lhsT = state[:, b, 4 * j:4 * j + 4, :].rearrange("p h w -> p (h w)")
                oj = O[:, j * P:(j + 1) * P]
                pe.matmul(oj, lhsT, qw[:, b % 2, half_, :], start=True, stop=False, skip_group_check=True)
                for i in range(4):
                    h = 4 * j + i
                    ins = pe.matmul(oj[32 * i:32 * i + VW, :], vs[:, b % 2, h, :], Pm[:, slot(h), :],
                                    start=False, stop=True, tile_position=(0, 32 * i), skip_group_check=True)
                if j == 3:
                    ins.then_inc(s["o"], 1)

            def g_back(n):
                until(pe, s["oc"], n + 1)
                until(pe, s["s1"], n + 1)
                until(pe, s["av"], n)
                for j in range(4):
                    ins = pe.transpose(M[:, j * P:(j + 1) * P], oT[:, j, :], ident)
                ins.then_inc(s["g"], 1)

            def t_gate(n):
                until(pe, s["gg"], n + 1)
                until(pe, s["kt"], n + 2)
                until(pe, s["yc"], n)
                if z_there(n + 1):
                    until(pe, s["n_zt"], n)
                    pe.transpose(TA[:, 384:512], nt[:, 2, :], ident).then_inc(s["n_zT"], 1)
                for i in range(2):
                    ins = pe.transpose(TA[:, i * P:(i + 1) * P], gg[:, i * P:(i + 1) * P], ident)
                ins.then_inc(s["tg"], 1)

            def out_proj(n):
                until(pe, s["gt"], n + 1)
                if z_there(n + 1):
                    until(pe, s["n_za"], n)
                for i in range(2):
                    ins = pe.matmul(TA[:, 256:256 + D], gT[:, i, :], wo_sb[:, i, :], start=i == 0, stop=i == 1)
                ins.then_inc(s["y"], 1)

            def step(c, b, first=False, last=False):
                n = c * 4 + b
                nxt = (b + 1) % B
                until(pe, s["kf"], n + 1)
                until(pe, s["yc"], n - 1)
                for i in range(2):
                    ins = pe.transpose(TA[:, i * P:(i + 1) * P], kf[:, i * P:(i + 1) * P], ident)
                ins.then_inc(s["tk"], 1)
                if b == 2 and routed(c):
                    until(pe, s["vp"], 2 * n + 2)
                    places(c - BEHIND)
                if not last:
                    if b == 3:
                        until(pe, s["zs"], c + 2)
                    front_qk(n + 1, nxt)
                if not first:
                    g_back(n - 1)
                if not last:
                    if routed(c) and b == 1:
                        until(pe, s["c_l"], c - BEHIND + 1)
                    if routed(c) and b == 2:
                        until(pe, s["c_cnt"], c - BEHIND + 1)
                    front_vp(n + 1, nxt)
                until(pe, s["qt"], n * 4 + 4)
                until(pe, s["kt"], n + 1)
                scores(n, b, 0)
                scores(n, b, 1)
                scores(n, b, 2)
                values(n, b, 0)
                scores(n, b, 3)
                if not first:
                    t_gate(n - 1)
                if not last:
                    queries(n + 1)
                values(n, b, 2)
                if b == 0 and routed(c):
                    until(pe, s["vp"], 2 * n + 4)
                    h_transposes(c - BEHIND)
                values(n, b, 1)
                if not first:
                    out_proj(n - 1)
                values(n, b, 3)
                if b == 0 and routed(c):
                    logits(c - BEHIND)
                until(pe, s["kw"], n + 1)
                until(pe, s["av"], n)
                for i in range(2):
                    ins = pe.matmul(M[:, i * HV:(i + 1) * HV], kw[:, i * P:(i + 1) * P],
                                    vs[:, b % 2, 8 * i:8 * i + 8, :], start=True, stop=True)
                ins.then_inc(s["u"], 1)
                if isinstance(c, int) and c in (0, NC - 1):
                    e = b if c == 0 else 4 + b
                    pe.wait_ge(s["ww"], 16 * 2 * E)
                    pe.wait_ge(s["oc"], n + 1)
                    for i in range(2):
                        until(pe, s["we"], 2 * e + i)
                        for k in range(4):
                            src = w1n[:, e, k, :] if i == 0 else w2n[:, e, k * P:(k + 1) * P]
                            ins = pe.transpose(O[:, k * P:(k + 1) * P], src, ident)
                        ins.then_inc(s["wt"], 1)

            pe.wait_ge(s["bc1"], 3)
            pe.wait_ge(s["zs"], 1)
            front_qk(0, 0)
            front_vp(0, 0)
            for c in range(1, AHEAD):
                first_transposes(c)
            pe.wait_ge(s["wgt"], 3)
            queries(0)
            for c in range(BEHIND + 1):
                for b in range(B):
                    step(c, b, first=c == 0 and b == 0)
            with pe.Fori(BEHIND + 1, NC - 2) as c:
                for b in range(B):
                    step(c, b)
            for c in (NC - 2, NC - 1):
                for b in range(B):
                    step(c, b, last=c == NC - 1 and b == 3)
            g_back(NT - 1)
            pe.wait_ge(s["gg"], NT)
            pe.wait_ge(s["yc"], NT - 1)
            for i in range(2):
                ins = pe.transpose(TA[:, i * P:(i + 1) * P], gg[:, i * P:(i + 1) * P], ident)
            ins.then_inc(s["tg"], 1)
            out_proj(NT - 1)

            for g in (NC - 2, NC - 1):
                pe.wait_ge(s["vp"], 2 * NT)
                until(pe, s["c_cnt"], g)
                h_transposes(g)
                logits(g)
                pe.wait_ge(s["c_l"], g + 1)
                places(g)

            def x_transpose(t, u, turn):
                until(pe, s[f"f_xt{u}"], 16 * turn + 16)
                until(pe, s["f_xT"], t - 1)
                pe.transpose((TA, TD)[u % 2][:, 0:P], xt[:, u, 0:D], ident).then_inc(s["f_xp"], 1)

            def up(t, u):
                until(pe, s["f_xT"], t + 1)
                until(pe, s["f_ws"], 2 * t + 2)
                until(pe, s["f_h"], 4 * (t - 1))
                for k in range(4):
                    ins = pe.matmul(S[u % 2][:, k * P:(k + 1) * P], w1s[:, u % 4, k * P:(k + 1) * P], xT[:, u % 4, :],
                                    start=True, stop=True)
                ins.then_inc(s["f_m1"], 1)

            def down(t, u):
                e = expert_of(pe, t)
                until(pe, s["f_h"], 4 * (t + 1))
                until(pe, s["f_yb"], t - 1)
                y = (O, M)[u % 2][:, 0:D]
                for k in range(4):
                    ins = pe.matmul(y, hT[:, u % 2, k, :], w2T[:, bass.ds(e * HID + k * P, P)], start=k == 0, stop=k == 3)
                ins.then_inc(s["f_m2"], 1)

            def expert(t, u, turn, ahead):
                if ahead > 3:
                    x_transpose(t + 3, (u + 3) % RING, turn + (u + 3 >= RING))
                if ahead > 1:
                    up(t + 1, u + 1)
                down(t, u)

            pe.wait_ge(s["meta"], 2)
            pe.wait_ge(s["we"], 2 * E)
            x_transpose(0, 0, 0)
            x_transpose(1, 1, 0)
            x_transpose(2, 2, 0)
            up(0, 0)
            for u in range(RING):
                expert(u, u, 0, RING)
            with pe.Fori(1, TURNS) as k:
                for u in range(RING):
                    expert(k * RING + u, u, k, RING)
            for u in range(REST):
                expert(TURNS * RING + u, u, TURNS, REST - u)


NW = 15
_INS = ["L0_attn_x", "L0_attn_in_ln_w", "L0_attn_in_ln_b", "L0_attn_q_ln_w", "L0_attn_q_ln_b", "L0_attn_k_ln_w",
        "L0_attn_k_ln_b", "L0_attn_out_ln_w", "L0_attn_out_ln_b", "L0_attn_W_in", "L0_attn_W_out", "L0_attn_Wq",
        "L0_attn_bq", "L0_attn_Wk", "L0_attn_bk", "L0_attn_smear_factor", "L0_attn_log_scale", "L0_ffn_Wg",
        "L0_ffn_W1", "L0_ffn_b1", "L0_ffn_W2", "L0_ffn_b2", "L0_c", "L0_wmod"]


def kernel(**inputs):
    import numpy as _np
    import concourse.bacc as _bacc
    from concourse import mybir as _mybir
    from concourse.bass_utils import run_bass_kernel_spmd as _run

    nc = _bacc.Bacc("TRN2", target_bir_lowering=False, num_devices=1)
    arrays, args = {}, []
    for name in _INS:
        a = _np.ascontiguousarray(inputs[name])
        arrays[f"in_{name}_dram"] = a
        args.append(nc.dram_tensor(f"in_{name}_dram", a.shape, _mybir.dt.from_np(a.dtype), kind="ExternalInput").ap())
    k = shape_constants()
    arrays["consts_dram"] = k
    args.append(nc.dram_tensor("consts_dram", k.shape, F32, kind="ExternalInput").ap())
    out = nc.dram_tensor("out_0_dram", (B, L, D), F32, kind="ExternalOutput").ap()
    build(nc, *args, out)
    r = _run(nc, [arrays], core_ids=[0])
    return r.results[0]["out_0_dram"]
```
